# Optimizing a Trainium2 kernel written in Bass

```python
import numpy as np
import jax
import jax.numpy as jnp

def _softmax(x, axis=-1):
    return jax.nn.softmax(x, axis=axis)

def _gelu(x):
    return jax.nn.gelu(x, approximate=True)

def _silu(x):
    return jax.nn.silu(x)

def _sigmoid(x):
    return jax.nn.sigmoid(x)

def _layernorm(x, axis=-1, eps=1e-05):
    m = jnp.mean(x, axis=axis, keepdims=True)
    v = jnp.var(x, axis=axis, keepdims=True)
    return (x - m) / jnp.sqrt(v + eps)

def _scatter_add(tgt, idx, src, axis=0):
    return tgt.at[idx].add(src)

def _segment_sum(src, seg, n):
    return jax.ops.segment_sum(src, seg, n)
kernel_name = 'mk_flamingo_gated_d2_seqx_r8_2c7ec3'

def setup_inputs(seed: int=0):
    np.random.seed(seed)
    _w = jnp.asarray

    def _rec_inputs():
        import jax
        import jax.numpy as jnp
        _rk = jax.random.key(seed)
        x = -0.0002928 + 1 * jax.random.normal(jax.random.fold_in(_rk, 1), (16, 128, 256), jnp.float32)
        _lenS = 128 - jax.random.randint(jax.random.fold_in(_rk, 7), (16,), 0, max(1, 128 // 4) + 1, jnp.int32)
        _lenS2 = 128 - jax.random.randint(jax.random.fold_in(_rk, 8), (16,), 0, max(1, 128 // 4) + 1, jnp.int32)
        _ctx_512P = jax.random.normal(jax.random.fold_in(_rk, 11), (16, 16, 64), jnp.float32)
        _ctx_512c = jax.random.dirichlet(jax.random.fold_in(_rk, 511), 0.3 * jnp.ones((16,), jnp.float32), (16, 128))
        _ctx_512t = jnp.einsum('bsk,bkd->bsd', _ctx_512c, _ctx_512P)
        _ctx_512t = _ctx_512t * jax.lax.rsqrt(jnp.mean(jnp.square(_ctx_512t)) + 1e-12) * 0.953939
        ctx_512 = 0.000227908 + 0.99994 * (_ctx_512t + 0.3 * jax.random.normal(jax.random.fold_in(_rk, 611), (16, 128, 64), jnp.float32))
        _g = jax.random.normal(jax.random.fold_in(_rk, 9001), (2, 2), jnp.float32)
        _g = jnp.sign(_g) * jnp.maximum(jnp.abs(_g), 1.0) + (_g == 0) * 1.0
        g_xattn = _g[0]
        g_ffn = _g[1]
        return (x, ctx_512, g_xattn, g_ffn)
    x, ctx_512, g_xattn, g_ffn = _rec_inputs()

    def _L0_xattn_setup():
        import jax, jax.numpy as jnp
        import numpy as np
        B, S, L = (2, 128, 128)
        DIM_Q, H, K, D_C, D_CQ, R = (256, 16, 128, 64, 192, 64)

        def _rope_tables(length, dim):
            inv = 1.0 / 10000.0 ** (jnp.arange(0, dim, 2, dtype=jnp.float32) / dim)
            f = jnp.arange(length, dtype=jnp.float32)[:, None] * inv[None, :]
            sin = jnp.repeat(jnp.sin(f), 2, axis=-1)
            cos = jnp.repeat(jnp.cos(f), 2, axis=-1)
            return (sin, cos)

        def _rotate_half(x):
            half = x.shape[-1] // 2
            return jnp.concatenate([-x[..., half:], x[..., :half]], axis=-1)

        def _apply_rope(x, sin, cos):
            return x * cos + _rotate_half(x) * sin
        key = jax.random.key(seed)
        ks = jax.random.split(key, 8)
        return {'hidden_q': jax.random.normal(ks[0], (B, S, DIM_Q), jnp.float32), 'kv_c': jax.random.normal(ks[1], (B, L, D_C), jnp.float32), 'Wq': jax.random.normal(ks[2], (H * K, DIM_Q), jnp.float32) / np.sqrt(DIM_Q).astype(np.float32), 'w_kc_q': jax.random.normal(ks[3], (H, K, D_CQ), jnp.float32) / np.sqrt(K).astype(np.float32), 'w_kc_kv': jax.random.normal(ks[4], (H, K, D_C), jnp.float32) / np.sqrt(K).astype(np.float32), 'W_qr': jax.random.normal(ks[5], (H, D_CQ, R), jnp.float32) / np.float32(np.sqrt(D_CQ) * np.sqrt(R)), 'W_kr': jax.random.normal(ks[6], (H, D_C, R), jnp.float32) / np.sqrt(D_C).astype(np.float32), 'Wo': jax.random.normal(ks[7], (DIM_Q, H * K), jnp.float32) / np.sqrt(H * K).astype(np.float32)}
    _L0_xattn_all = _L0_xattn_setup()
    _L0_xattn_in = {k: v for k, v in _L0_xattn_all.items() if k in ('Wq', 'w_kc_q', 'w_kc_kv', 'W_qr', 'W_kr', 'Wo')}
    del _L0_xattn_all

    def _L0_ffn_setup():
        import jax, jax.numpy as jnp
        import numpy as np
        import math
        D_MODEL = 256
        D_FF = 1024
        NUM_EXPERTS = 8
        TOP_K = 2
        CAPACITY_FACTOR = 1.25
        BATCH, SEQ = (4, 256)

        def _moe_forward(x, Wg, w1, w2):
            B, T, d = x.shape
            S = B * T
            E, K = (NUM_EXPERTS, TOP_K)
            C = math.ceil(CAPACITY_FACTOR * S * K / E)
            xr = x.reshape(S, d)
            probs = jax.nn.softmax(xr @ Wg, axis=-1)
            gate_vals, expert_idx = jax.lax.top_k(probs, K)
            flat_e = expert_idx.reshape(-1)
            oh = jax.nn.one_hot(flat_e, E, dtype=jnp.int32)
            pos = jnp.sum((jnp.cumsum(oh, axis=0) - 1) * oh, axis=1)
            kept = pos < C
            i = jnp.arange(S * K)
            slot = i % K * S + i // K
            sentinel = S * K
            pos_w = jnp.where(kept, pos, C)
            dispatch_mask = jnp.full((E, C), sentinel, dtype=jnp.int32)
            dispatch_mask = dispatch_mask.at[flat_e, pos_w].set(slot.astype(jnp.int32), mode='drop')
            combine_weights = (gate_vals * kept.reshape(S, K)).T
            dispatched = xr[dispatch_mask.reshape(-1) % S].reshape(E, C, d)
            h = jax.nn.relu(jnp.einsum('ecd,edf->ecf', dispatched, w1))
            expert_out = jnp.einsum('ecf,efd->ecd', h, w2)
            rerouted = jnp.zeros((S * K + 1, d), dtype=expert_out.dtype)
            rerouted = rerouted.at[dispatch_mask.reshape(-1)].set(expert_out.reshape(-1, d))
            rerouted = rerouted[:-1].reshape(K, S, d)
            out = jnp.einsum('ks,ksm->sm', combine_weights, rerouted)
            return out.reshape(B, T, d)
        key = jax.random.key(seed)
        k1, k2, k3, k4 = jax.random.split(key, 4)
        x = jax.random.normal(k1, (BATCH, SEQ, D_MODEL), dtype=jnp.float32)
        Wg = jax.random.normal(k2, (D_MODEL, NUM_EXPERTS), dtype=jnp.float32) * 0.02
        w1 = jax.random.normal(k3, (NUM_EXPERTS, D_MODEL, D_FF), dtype=jnp.float32) * 0.02
        w2 = jax.random.normal(k4, (NUM_EXPERTS, D_FF, D_MODEL), dtype=jnp.float32) * 0.02
        return {'x': x, 'Wg': Wg, 'w1': w1, 'w2': w2}
    _L0_ffn_all = _L0_ffn_setup()
    _L0_ffn_in = {k: v for k, v in _L0_ffn_all.items() if k in ('Wg', 'w1', 'w2')}
    del _L0_ffn_all

    def _L1_xattn_setup():
        import jax, jax.numpy as jnp
        import numpy as np
        B, S, L = (2, 128, 128)
        DIM_Q, H, K, D_C, D_CQ, R = (256, 16, 128, 64, 192, 64)

        def _rope_tables(seq_len, dim, dtype):
            inv_freq = 1.0 / 10000.0 ** (jnp.arange(0, dim, 2, dtype=dtype) / dim)
            t = jnp.arange(seq_len, dtype=dtype)
            freqs = t[:, None] * inv_freq[None, :]
            sin = jnp.repeat(jnp.sin(freqs), 2, axis=-1)
            cos = jnp.repeat(jnp.cos(freqs), 2, axis=-1)
            return (sin, cos)

        def _rotate_half(x):
            h = x.shape[-1] // 2
            return jnp.concatenate([-x[..., h:], x[..., :h]], axis=-1)
        key = jax.random.key(seed)
        ks = jax.random.split(key, 8)
        s_in = 1.0 / np.sqrt(DIM_Q)
        s_k = 1.0 / np.sqrt(K)
        s_cq = 1.0 / np.sqrt(D_CQ)
        s_c = 1.0 / np.sqrt(D_C)
        return {'hidden_q': jax.random.normal(ks[0], (B, S, DIM_Q), jnp.float32), 'kv_c': jax.random.normal(ks[1], (B, L, D_C), jnp.float32), 'Wq': jax.random.normal(ks[2], (H * K, DIM_Q), jnp.float32) * s_in, 'w_kc_q': jax.random.normal(ks[3], (H, K, D_CQ), jnp.float32) * s_k, 'w_kc_kv': jax.random.normal(ks[4], (H, K, D_C), jnp.float32) * s_k, 'W_qr': jax.random.normal(ks[5], (H, D_CQ, R), jnp.float32) * s_cq / np.sqrt(R), 'W_kr': jax.random.normal(ks[6], (H, D_C, R), jnp.float32) * s_c, 'Wo': jax.random.normal(ks[7], (DIM_Q, H * K), jnp.float32) * s_k}
    _L1_xattn_all = _L1_xattn_setup()
    _L1_xattn_in = {k: v for k, v in _L1_xattn_all.items() if k in ('Wq', 'w_kc_q', 'w_kc_kv', 'W_qr', 'W_kr', 'Wo')}
    del _L1_xattn_all

    def _L1_ffn_setup():
        import jax, jax.numpy as jnp
        import numpy as np
        DIM = 256
        N_EXPERTS = 8
        TOP_K = 2
        key = jax.random.key(seed)
        ks = jax.random.split(key, 5)
        x = jax.random.normal(ks[0], (4, 512, DIM), dtype=jnp.float32)
        W_up = jax.random.normal(ks[1], (DIM, DIM), dtype=jnp.float32) * (1.0 / np.sqrt(DIM))
        W_down = jax.random.normal(ks[2], (DIM, DIM), dtype=jnp.float32) * (1.0 / np.sqrt(DIM))
        W_gate = jax.random.normal(ks[3], (N_EXPERTS, DIM), dtype=jnp.float32) * (1.0 / np.sqrt(DIM))
        W_expert = jax.random.normal(ks[4], (DIM, DIM), dtype=jnp.float32) * (1.0 / np.sqrt(DIM))
        return {'x': x, 'W_up': W_up, 'W_down': W_down, 'W_gate': W_gate, 'W_expert': W_expert}
    _L1_ffn_all = _L1_ffn_setup()
    _L1_ffn_in = {k: v for k, v in _L1_ffn_all.items() if k in ('W_up', 'W_down', 'W_gate', 'W_expert')}
    del _L1_ffn_all
    return {'x': x, 'ctx_512': ctx_512, 'g_xattn': g_xattn, 'g_ffn': g_ffn, 'L0_xattn_Wq': _L0_xattn_in['Wq'], 'L0_xattn_w_kc_q': _L0_xattn_in['w_kc_q'], 'L0_xattn_w_kc_kv': _L0_xattn_in['w_kc_kv'], 'L0_xattn_W_qr': _L0_xattn_in['W_qr'], 'L0_xattn_W_kr': _L0_xattn_in['W_kr'], 'L0_xattn_Wo': _L0_xattn_in['Wo'], 'L0_ffn_Wg': _L0_ffn_in['Wg'], 'L0_ffn_w1': _L0_ffn_in['w1'], 'L0_ffn_w2': _L0_ffn_in['w2'], 'L1_xattn_Wq': _L1_xattn_in['Wq'], 'L1_xattn_w_kc_q': _L1_xattn_in['w_kc_q'], 'L1_xattn_w_kc_kv': _L1_xattn_in['w_kc_kv'], 'L1_xattn_W_qr': _L1_xattn_in['W_qr'], 'L1_xattn_W_kr': _L1_xattn_in['W_kr'], 'L1_xattn_Wo': _L1_xattn_in['Wo'], 'L1_ffn_W_up': _L1_ffn_in['W_up'], 'L1_ffn_W_down': _L1_ffn_in['W_down'], 'L1_ffn_W_gate': _L1_ffn_in['W_gate'], 'L1_ffn_W_expert': _L1_ffn_in['W_expert']}

def reference(x, ctx_512, g_xattn, g_ffn, L0_xattn_Wq, L0_xattn_w_kc_q, L0_xattn_w_kc_kv, L0_xattn_W_qr, L0_xattn_W_kr, L0_xattn_Wo, L0_ffn_Wg, L0_ffn_w1, L0_ffn_w2, L1_xattn_Wq, L1_xattn_w_kc_q, L1_xattn_w_kc_kv, L1_xattn_W_qr, L1_xattn_W_kr, L1_xattn_Wo, L1_ffn_W_up, L1_ffn_W_down, L1_ffn_W_gate, L1_ffn_W_expert):
    import jax
    import jax.numpy as jnp

    def _L0_xattn_ref(hidden_q, kv_c, Wq, w_kc_q, w_kc_kv, W_qr, W_kr, Wo):
        import jax, jax.numpy as jnp
        import numpy as np
        B, S, L = (2, 128, 128)
        DIM_Q, H, K, D_C, D_CQ, R = (256, 16, 128, 64, 192, 64)

        def _rope_tables(length, dim):
            inv = 1.0 / 10000.0 ** (jnp.arange(0, dim, 2, dtype=jnp.float32) / dim)
            f = jnp.arange(length, dtype=jnp.float32)[:, None] * inv[None, :]
            sin = jnp.repeat(jnp.sin(f), 2, axis=-1)
            cos = jnp.repeat(jnp.cos(f), 2, axis=-1)
            return (sin, cos)

        def _rotate_half(x):
            half = x.shape[-1] // 2
            return jnp.concatenate([-x[..., half:], x[..., :half]], axis=-1)

        def _apply_rope(x, sin, cos):
            return x * cos + _rotate_half(x) * sin
        Bv, Sv, _ = hidden_q.shape
        _, Lv, _ = kv_c.shape
        q_hk = (hidden_q @ Wq.T).reshape(Bv, Sv, H, K)
        q_big = jnp.einsum('bshk,hkq->bshq', q_hk, w_kc_q)
        sin_q, cos_q = _rope_tables(Sv, D_CQ)
        q_big = _apply_rope(q_big, sin_q[None, :, None, :], cos_q[None, :, None, :])
        sin_k, cos_k = _rope_tables(Lv, D_C)
        kv_r = _apply_rope(kv_c, sin_k[None], cos_k[None])
        q_r = jnp.einsum('bshq,hqr->bhsr', q_big, W_qr)
        k_r = jnp.einsum('bld,hdr->bhlr', kv_r, W_kr)
        scores = jnp.einsum('bhsr,bhlr->bhsl', q_r, k_r)
        attn = jax.nn.softmax(scores, axis=-1)
        ctx_c = jnp.einsum('bhsl,bld->bhsd', attn, kv_r)
        ctx_lat = jnp.einsum('bhsd,hkd->bhsk', ctx_c, w_kc_kv)
        ctx = ctx_lat.transpose(0, 2, 1, 3).reshape(Bv, Sv, H * K)
        return ctx @ Wo.T

    def _L0_ffn_ref(x, Wg, w1, w2):
        import jax, jax.numpy as jnp
        import numpy as np
        import math
        D_MODEL = 256
        D_FF = 1024
        NUM_EXPERTS = 8
        TOP_K = 2
        CAPACITY_FACTOR = 1.25
        BATCH, SEQ = (4, 256)

        def _moe_forward(x, Wg, w1, w2):
            B, T, d = x.shape
            S = B * T
            E, K = (NUM_EXPERTS, TOP_K)
            C = math.ceil(CAPACITY_FACTOR * S * K / E)
            xr = x.reshape(S, d)
            probs = jax.nn.softmax(xr @ Wg, axis=-1)
            gate_vals, expert_idx = jax.lax.top_k(probs, K)
            flat_e = expert_idx.reshape(-1)
            oh = jax.nn.one_hot(flat_e, E, dtype=jnp.int32)
            pos = jnp.sum((jnp.cumsum(oh, axis=0) - 1) * oh, axis=1)
            kept = pos < C
            i = jnp.arange(S * K)
            slot = i % K * S + i // K
            sentinel = S * K
            pos_w = jnp.where(kept, pos, C)
            dispatch_mask = jnp.full((E, C), sentinel, dtype=jnp.int32)
            dispatch_mask = dispatch_mask.at[flat_e, pos_w].set(slot.astype(jnp.int32), mode='drop')
            combine_weights = (gate_vals * kept.reshape(S, K)).T
            dispatched = xr[dispatch_mask.reshape(-1) % S].reshape(E, C, d)
            h = jax.nn.relu(jnp.einsum('ecd,edf->ecf', dispatched, w1))
            expert_out = jnp.einsum('ecf,efd->ecd', h, w2)
            rerouted = jnp.zeros((S * K + 1, d), dtype=expert_out.dtype)
            rerouted = rerouted.at[dispatch_mask.reshape(-1)].set(expert_out.reshape(-1, d))
            rerouted = rerouted[:-1].reshape(K, S, d)
            out = jnp.einsum('ks,ksm->sm', combine_weights, rerouted)
            return out.reshape(B, T, d)
        return _moe_forward(x, Wg, w1, w2)

    def _L1_xattn_ref(hidden_q, kv_c, Wq, w_kc_q, w_kc_kv, W_qr, W_kr, Wo):
        import jax, jax.numpy as jnp
        import numpy as np
        B, S, L = (2, 128, 128)
        DIM_Q, H, K, D_C, D_CQ, R = (256, 16, 128, 64, 192, 64)

        def _rope_tables(seq_len, dim, dtype):
            inv_freq = 1.0 / 10000.0 ** (jnp.arange(0, dim, 2, dtype=dtype) / dim)
            t = jnp.arange(seq_len, dtype=dtype)
            freqs = t[:, None] * inv_freq[None, :]
            sin = jnp.repeat(jnp.sin(freqs), 2, axis=-1)
            cos = jnp.repeat(jnp.cos(freqs), 2, axis=-1)
            return (sin, cos)

        def _rotate_half(x):
            h = x.shape[-1] // 2
            return jnp.concatenate([-x[..., h:], x[..., :h]], axis=-1)
        b, s, _ = hidden_q.shape
        l = kv_c.shape[1]
        q_hk = (hidden_q @ Wq.T).reshape(b, s, H, K)
        q_big = jnp.einsum('bshk,hkq->bshq', q_hk, w_kc_q)
        sin, cos = _rope_tables(l, D_C, kv_c.dtype)
        kv_rope = kv_c * cos[None] + _rotate_half(kv_c) * sin[None]
        q_r = jnp.einsum('bshq,hqr->bhsr', q_big, W_qr)
        k_r = jnp.einsum('bld,hdr->bhlr', kv_rope, W_kr)
        scores = jnp.einsum('bhsr,bhlr->bhsl', q_r, k_r)
        attn = jax.nn.softmax(scores, axis=-1)
        ctx_c = jnp.einsum('bhsl,bld->bhsd', attn, kv_rope)
        ctx_lat = jnp.einsum('bhsd,hkd->bshk', ctx_c, w_kc_kv)
        out = ctx_lat.reshape(b, s, H * K) @ Wo.T
        return out

    def _L1_ffn_ref(x, W_up, W_down, W_gate, W_expert):
        import jax, jax.numpy as jnp
        import numpy as np
        DIM = 256
        N_EXPERTS = 8
        TOP_K = 2
        logits = jnp.einsum('bsd,ed->bse', x, W_gate)
        routing_weights, selected_experts = jax.lax.top_k(logits, TOP_K)
        shared_out = jnp.einsum('bsd,od->bso', jax.nn.relu(jnp.einsum('bsd,od->bso', x, W_up)), W_down)
        rw = jax.nn.softmax(routing_weights, axis=-1)
        expert_out = jnp.einsum('bsd,do->bso', x, W_expert)
        moe_out = jnp.sum(rw, axis=-1, keepdims=True) * expert_out
        return shared_out + moe_out
    x = x + jnp.tanh(g_xattn[0]) * _L0_xattn_ref(_layernorm(x, axis=-1), ctx_512, L0_xattn_Wq, L0_xattn_w_kc_q, L0_xattn_w_kc_kv, L0_xattn_W_qr, L0_xattn_W_kr, L0_xattn_Wo)
    x = x + jnp.tanh(g_ffn[0]) * _L0_ffn_ref(_layernorm(x, axis=-1), L0_ffn_Wg, L0_ffn_w1, L0_ffn_w2)
    x = x + jnp.tanh(g_xattn[1]) * _L1_xattn_ref(_layernorm(x, axis=-1), ctx_512, L1_xattn_Wq, L1_xattn_w_kc_q, L1_xattn_w_kc_kv, L1_xattn_W_qr, L1_xattn_W_kr, L1_xattn_Wo)
    x = x + jnp.tanh(g_ffn[1]) * _L1_ffn_ref(_layernorm(x, axis=-1), L1_ffn_W_up, L1_ffn_W_down, L1_ffn_W_gate, L1_ffn_W_expert)
    return x

_drawn_inputs = setup_inputs


def setup_inputs(seed=0):
    import zlib

    import numpy as np

    out = dict(_drawn_inputs(seed))
    spreads = {'g_ffn': (-1.0, 0.2)}
    factors = {'L0_ffn_Wg': 2.873, 'L0_ffn_w1': 3.002, 'L1_ffn_W_gate': 8.0}
    for name, (base, spread) in spreads.items():
        noise = np.random.default_rng([zlib.crc32(name.encode()), seed]).standard_normal(out[name].shape)
        drawn = base * np.exp(spread * noise) if base else spread * noise
        out[name] = jnp.asarray(drawn.astype(out[name].dtype))
    for name, factor in factors.items():
        out[name] = (out[name] * factor).astype(out[name].dtype)
    return out
```

```python
from contextlib import ExitStack

import numpy as np

import concourse.bass as bass
from concourse import mybir

F32 = mybir.dt.float32
F32R = mybir.dt.float32r
I32 = mybir.dt.int32
ALU = mybir.AluOpType
ACT = mybir.ActivationFunctionType
AX = mybir.AxisListType

P = 128
B, S, D = 16, 128, 256
H, KH, DC, DQ = 16, 128, 64, 192
LO = DQ // 2
NP = H // 2
DK = D // P
GB = 4
NG = B // GB
TG = GB * S
NU = GB * H // 4
E, FF = 8, 1024
CAP = int(np.ceil(1.25 * B * S * 2 / E))
CT = CAP // P
FT = FF // P
DROPPED = 1.0e5
EPS = 1e-5

LAYERS = (0, 1)


def build(nc, io):
    with ExitStack() as ctx:
        def sb(name, shape, dt=F32):
            return ctx.enter_context(nc.sbuf_tensor(name, shape, dt))

        def sem(name):
            return ctx.enter_context(nc.semaphore(name))

        class Sems:

            def __init__(self, stage, signals):
                self.stage = stage
                self.of = {s: sem(f"{stage}_{s}") for s in signals.split()}

            def __call__(self, s):
                return self.of[s]

        PS = ctx.enter_context(nc.psum_tensor("PS", [P, 8, 512], F32))
        disp = nc.dram_tensor("disp_rows", (E * CAP, D), F32, kind="Internal").ap()
        eout = nc.dram_tensor("expert_rows", (E * CAP, D), F32, kind="Internal").ap()

        x = sb("x_res", [P, B, D])
        kv_aug = sb("kv_aug", [P, B, P])
        kvT = sb("kvT", [P, B, P])
        U = sb("U_out", [P, NP, D])
        G = sb("G_score", [P, DK, NP, P])
        xn = sb("x_norm", [P, GB, D])
        xn2 = sb("x_norm_ffn", [P, GB, D])
        xT = sb("xT", [P, DK, TG])
        tTr = sb("tT_round", [P, NP, TG], F32R)
        kvg = sb("kv_group", [P, GB, 2, P])
        kvgr = sb("kv_group_round", [P, GB, 2, P], F32R)
        diag = sb("diag", [P, 2, 4, P], F32R)
        PT = sb("probT", [P, 2, 4, P])
        ctxn = sb("ctx_norm", [P, 2, 4, DC])
        cT = sb("ctxT", [P, 2, 2, P])
        ident = sb("ident", [P, P])
        before = sb("before", [P, P])
        ones = sb("ones", [P, P])
        ones_r = sb("ones_round", [P, P], F32R)
        epsv = sb("eps", [P, GB])
        scrap_p = sb("scrap_pool", [P, 1])
        scrap = sb("scrap", [P, 2])
        mhalf = sb("minus_half", [P, GB])
        cosq = sb("cosq", [P, 3, S])
        sinq = sb("sinq", [P, 3, S])
        kv_tab = sb("kv_tab", [P, 2, DC])
        gains = sb("gains", [P, 4])
        tg = sb("tanh_gains", [P, 4])
        wg0 = sb("wg0", [P, DK, E])
        wg1 = sb("wg1", [P, DK, E])
        w_up = sb("w_up", [P, DK, D])
        w_dn = sb("w_dn", [P, DK, D])
        w_dn_g = sb("w_dn_gain", [P, DK, D])
        w_ex = sb("w_ex", [P, DK, D])
        stats = sb("stats", [P, GB, 6])
        mv = sb("mean_var", [P, GB, 2])
        veps = sb("var_eps", [P, GB])
        rstd = sb("rstd", [P, GB])
        negm = sb("neg_max", [P, 2, 4])
        rinv = sb("row_inv", [P, 2, 4])
        tie = sb("tie_order", [P, E])
        base = sb("slot_base", [P, E])
        ebuf = sb("route_tmp", [P, 12, GB, E])
        oh = sb("chosen", [P, 2, GB, E])
        sbuf2 = sb("slot_val", [P, 2, GB, E])
        macc = sb("chosen_before", [P, GB + 1, E])
        rsm = sb("route_small", [P, 24, GB])
        keep = sb("keep", [P, 2, GB])
        slot = sb("slot", [P, 2, GB])
        gates = sb("gates", [P, 2, GB])
        sidx = sb("scatter_idx", [P, GB, 2], I32)
        gidx = sb("gather_idx", [P, B, 2], I32)
        gw = sb("gate_weight", [P, B, 2])
        top8 = sb("top8", [P, GB, E])

        arena = sb("arena", [P, 88 * 256])

        def area(kib, n):
            return arena[:, kib * 256:kib * 256 + n]

        A = area(0, DK * NP * 3 * P).rearrange("p (k n t m) -> p k n t m", k=DK, n=NP, t=3)
        MK = area(24, NP * 3 * P).rearrange("p (n t m) -> p n t m", n=NP, t=3)
        qc = area(36, 2 * 3 * TG).rearrange("p (z t n) -> p z t n", z=2, t=3)
        qs = area(48, 2 * 3 * TG).rearrange("p (z t n) -> p z t n", z=2, t=3)
        qr = area(60, 2 * 3 * TG).rearrange("p (z t n) -> p z t n", z=2, t=3)
        tT = area(72, NP * TG).rearrange("p (n t) -> p n t", n=NP)
        zero = area(64, 8 * D)
        st_wq = area(36, 2 * 2 * D).rearrange("p (z h d) -> p z h d", z=2, h=2)
        st_cq = area(40, 2 * 2 * DQ).rearrange("p (z h q) -> p z h q", z=2, h=2)
        st_qr = area(43, 2 * 3 * P).rearrange("p (z t m) -> p z t m", z=2, t=3)
        st_kr = area(46, 2 * P).rearrange("p (z m) -> p z m", z=2)
        st_kv = area(47, 2 * 2 * DC).rearrange("p (z h m) -> p z h m", z=2, h=2)
        st_wo = area(48, 2 * 2 * D).rearrange("p (z h d) -> p z h d", z=2, h=2)
        mkst = area(52, 2 * 3 * P).rearrange("p (z t m) -> p z t m", z=2, t=3)
        at = area(55, 2 * 3 * D).rearrange("p (z t d) -> p z t d", z=2, t=3)
        kv_dup = area(0, B * P).rearrange("p (b m) -> p b m", b=B)
        kv_raw = area(72, B * DC).rearrange("p (b c) -> p b c", b=B)
        kv_sin = area(76, B * DC).rearrange("p (b c) -> p b c", b=B)
        kv_cos = area(80, B * DC).rearrange("p (b c) -> p b c", b=B)
        w1 = area(0, 2 * DK * FF).rearrange("p (z k f) -> p z k f", z=2, k=DK)
        w2 = area(16, 2 * FT * D).rearrange("p (z f d) -> p z f d", z=2, f=FT)
        hT = area(36, FT * CAP).rearrange("p (f c) -> p f c", f=FT)
        dx = area(56, 2 * CT * D).rearrange("p (z t d) -> p z t d", z=2, t=CT)
        dT = area(66, 2 * DK * CAP).rearrange("p (z k c) -> p z k c", z=2, k=DK)
        eo = area(76, 2 * CT * D).rearrange("p (z t d) -> p z t d", z=2, t=CT)
        grow = area(0, GB * 2 * D).rearrange("p (j k d) -> p j k d", j=GB, k=2)
        uT = area(8, DK * TG).rearrange("p (k t) -> p k t", k=DK)

        ld = Sems("load", "x kv const gain zero")
        cs = Sems("const", "ident ones misc tanh wdn zeros staged")
        kvs = Sems("kv", "cos sin rope ones turned copied group")
        fold = [Sems(f"fold{n}", "staged0 staged1 product0 product1 product1b a_out mu_out g_out") for n in LAYERS]
        NORM = "stats mean rstd normed turned xT veps"
        nrm = [Sems(f"norm_{n}", NORM) for n in ("att0", "ffn0", "att1", "ffn1")]
        qsem = Sems("query0", "q cos add t tT")
        q1sem = Sems("query1", "t tT")
        att = [Sems(f"att{n}", "scores negmax diag scoresT probs pv rinv ctx turned ctxT unit proj resid kvg") for n in LAYERS]
        rt = Sems("route", "logits shifted exp step pos scattered sent carry")
        MASK_STEP, ROUTE_STEPS = 21, 34
        moe = Sems("moe", "weights0 weights1 rows0 rows1 turned dT h relu y y_out stored0 stored1 eo_free")
        cb = Sems("combine", "gathered first added")
        ff = Sems("ffn1", "logits step exp rw up relu y added stored")

        block = ctx.enter_context(nc.Block())

        def stage_loads(sp, layer):
            f, w = fold[layer], io[layer]
            with sp.Fori(0, NP // 2) as i:
                for z in range(2):
                    h = (2 * i + z) * 2
                    sp.wait_ge(f("product1"), 2 * i + z + 1)
                    for dst, src in (
                        (st_wq[:, z], w["wq"][:, bass.ds(h, 2), :]),
                        (st_cq[:, z], w["w_kc_q"][:, bass.ds(h, 2), :]),
                        (st_kv[:, z], w["w_kc_kv"][:, bass.ds(h, 2), :]),
                        (st_wo[:, z], w["woT"][:, bass.ds(h, 2), :]),
                    ):
                        sp.dma_start(dst, src).then_inc(f(f"staged{z}"), 16)
                    qr0 = w["wqrT"][:, bass.ds(h, 1), :].rearrange("r h (a q) -> r (h a) q", a=2)
                    qr1 = w["wqrT"][:, bass.ds(h + 1, 1), :].rearrange("r h (a q) -> r (h a) q", a=2)
                    sp.dma_start(st_qr[0:64, z, 0:2, 0:LO], qr0).then_inc(f(f"staged{z}"), 16)
                    sp.dma_start(st_qr[64:P, z, 0:2, LO:P], qr1[:, :, 0:P - LO]).then_inc(f(f"staged{z}"), 16)
                    sp.dma_start(st_qr[64:P, z, 2, :].rearrange("p (a m) -> p a m", a=2),
                                 qr1[:, :, P - LO:LO]).then_inc(f(f"staged{z}"), 16)
                    sp.dma_start(st_kr[0:64, z, 0:64], w["wkrT"][:, bass.ds(h, 1), :].rearrange("r h d -> r (h d)")).then_inc(f(f"staged{z}"), 16)
                    sp.dma_start(st_kr[64:P, z, 64:P], w["wkrT"][:, bass.ds(h + 1, 1), :].rearrange("r h d -> r (h d)")).then_inc(f(f"staged{z}"), 16)
        STAGED = 9 * 16

        @block.sync
        def _(sp):
            sp.dma_start(gains[:, 0:2], io["g_xattn"]).then_inc(ld("gain"), 16)
            sp.dma_start(gains[:, 2:4], io["g_ffn"]).then_inc(ld("gain"), 16)
            sp.dma_start(kv_raw, io["ctx"]).then_inc(ld("kv"), 16)
            sp.dma_start(kv_tab[:], io["kv_tab"]).then_inc(ld("kv"), 16)
            sp.wait_ge(cs("staged"), 1)
            stage_loads(sp, 0)
            sp.dma_start(x[:], io["x"]).then_inc(ld("x"), 16)
            for dst, src in ((cosq[:], io["cosq"]), (sinq[:], io["sinq"]), (wg0[:], io["wg0"]), (wg1[:], io["wg1"]),
                             (w_up[:], io["w_up"]), (w_dn[:], io["w_dn"]), (w_ex[:], io["w_ex"])):
                sp.dma_start(dst, src).then_inc(ld("const"), 16)
            sp.wait_ge(cs("zeros"), 1)
            for n in range(E * CAP // (8 * P)):
                sp.dma_start(disp[n * 8 * P:(n + 1) * 8 * P, :].rearrange("(p j) d -> p (j d)", p=P),
                             zero).then_inc(ld("zero"), 16)
            sp.wait_ge(qsem("t"), NG * NP)
            sp.wait_ge(cs("staged"), 2)
            stage_loads(sp, 1)
            sp.wait_ge(rt("step"), ROUTE_STEPS * NG)
            with sp.Fori(0, E // 2) as i:
                for z in range(2):
                    e = 2 * i + z
                    sp.wait_ge(moe("y"), 2 * CT * i + CT * (z + 1))
                    sp.dma_start(w1[:, z], io["w1"][bass.ds(e, 1), :, :].rearrange("e (k p) f -> p (e k) f", p=P)).then_inc(moe(f"weights{z}"), 16)
                    sp.dma_start(w2[:, z], io["w2"][bass.ds(e, 1), :, :].rearrange("e (k p) f -> p (e k) f", p=P)).then_inc(moe(f"weights{z}"), 16)
                    if z == 0:
                        sp.wait_ge(rt("scattered"), 16 * 2 * B)
                        sp.wait_ge(fold[1]("product1b"), NP)
                    sp.dma_start(dx[:, z], disp.rearrange("(e t p) d -> e p t d", e=E, p=P)[bass.ds(e, 1)].rearrange("e p t d -> p (e t) d")).then_inc(moe(f"rows{z}"), 16)
            with sp.Fori(0, NG) as i:
                sp.wait_ge(ff("added"), GB * 2 * i + GB * 2)
                sp.dma_start(io["out"][:, bass.ds(GB * i, GB), :], x[:, bass.ds(GB * i, GB), :]).then_inc(ff("stored"), 16)
            sp.wait_ge(ff("stored"), 16 * NG)

        def gate_dve():
            nc.vector.memset(scrap[:, 0:1], 0.0)

        def gate_pool():
            nc.gpsimd.tensor_tensor(scrap_p[:], mhalf[:, 0:1], mhalf[:, 0:1], ALU.add)

        def rstd_pool(pool, n, i):
            s = nrm[n]
            pool.wait_ge(s("mean"), GB * i + GB)
            nc.gpsimd.tensor_tensor(veps[:], mv[:, :, 1], epsv[:], ALU.add).then_inc(s("veps"), 1)
            pool.wait_ge(s("veps"), i + 1)
            nc.gpsimd.tensor_tensor(rstd[:], veps[:], mhalf[:], ALU.pow).then_inc(s("rstd"), 1)

        @block.gpsimd
        def _(pool):
            nc.gpsimd.memset(arena[:, 43 * 256:47 * 256], 0.0).then_inc(cs("staged"), 1)
            nc.gpsimd.memset(ident[:], 0.0).then_inc(cs("ident"), 1)
            nc.gpsimd.memset(before[:], 1.0).then_inc(cs("ident"), 1)
            nc.gpsimd.memset(ones[:], 1.0).then_inc(cs("ones"), 1)
            nc.gpsimd.memset(mhalf[:], -0.5).then_inc(cs("misc"), 1)
            pool.wait_ge(cs("ident"), 2)
            nc.gpsimd.affine_select(out=ident[:], in_=ident[:], compare_op=ALU.not_equal, fill=1.0, base=0,
                                    pattern=[[-1, P]], channel_multiplier=1).then_inc(cs("ident"), 1)
            nc.gpsimd.affine_select(out=before[:], in_=before[:], compare_op=ALU.is_gt, fill=0.0, base=0,
                                    pattern=[[1, P]], channel_multiplier=-1).then_inc(cs("ident"), 1)
            nc.gpsimd.iota(ebuf[:, 0, 0, :].bitcast(I32), pattern=[[-1, E]], base=E, channel_multiplier=0).then_inc(cs("misc"), 1)
            nc.gpsimd.iota(ebuf[:, 1, 0, :].bitcast(I32), pattern=[[CAP, E]], base=0, channel_multiplier=0).then_inc(cs("misc"), 1)
            nc.gpsimd.memset(epsv[:], EPS).then_inc(cs("misc"), 1)
            pool.wait_ge(cs("misc"), 5)
            nc.gpsimd.tensor_copy(tie[:], ebuf[:, 0, 0, :].bitcast(I32)).then_inc(cs("misc"), 1)
            nc.gpsimd.tensor_copy(base[:], ebuf[:, 1, 0, :].bitcast(I32)).then_inc(cs("misc"), 1)
            nc.gpsimd.memset(zero, 0.0).then_inc(cs("zeros"), 1)
            pool.sem_inc(rt("sent"), 1)
            pool.sem_inc(moe("eo_free"), 2)
            pool.wait_ge(ld("zero"), 16 * (E * CAP // (8 * P)))
            with pool.Fori(0, NG) as i:
                rstd_pool(pool, 0, i)
                for p in range(NP):
                    pool.wait_ge(qsem("cos"), 4 * NP * i + 4 * p + 4)
                    if p >= 2:
                        pool.wait_ge(qsem("t"), NP * i + p - 1)
                    z = p % 2
                    for t in range(3):
                        nc.gpsimd.tensor_tensor(qr[:, z, t, :], qc[:, z, t, :], qs[:, z, (1, 0, 2)[t], :],
                                                ALU.add).then_inc(qsem("add"), 1)
                rstd_pool(pool, 1, i)
                pool.wait_ge(rt("step"), ROUTE_STEPS * i + ROUTE_STEPS)
                gate_pool()
                for j in range(GB):
                    for k in range(2):
                        nc.gpsimd.indirect_dma_start(
                            out=disp, out_offset=bass.IndirectOffsetOnAxis(ap=sidx[:, j, k:k + 1], axis=0),
                            in_=xn2[:, j, :], in_offset=None, bounds_check=E * CAP - 1,
                            oob_is_err=False).then_inc(rt("scattered"), 16)
                pool.wait_ge(rt("scattered"), 16 * 2 * GB * (i + 1))
                pool.sem_inc(rt("sent"), 1)
            pool.wait_ge(qsem("t"), NG * NP)
            nc.gpsimd.memset(arena[:, 43 * 256:47 * 256], 0.0).then_inc(cs("staged"), 1)
            with pool.Fori(0, E // 2) as i:
                for z in range(2):
                    e = 2 * i + z
                    pool.wait_ge(moe("y_out"), 2 * CT * i + CT * (z + 1) + 2)
                    nc.gpsimd.dma_start(eout.rearrange("(e t p) d -> e p t d", e=E, p=P)[bass.ds(e, 1)].rearrange("e p t d -> p (e t) d"),
                                        eo[:, z]).then_inc(moe(f"stored{z}"), 16)
                    pool.wait_ge(moe(f"stored{z}"), 16 * i + 16)
                    pool.sem_inc(moe("eo_free"), 1)
            for z in range(2):
                pool.wait_ge(moe(f"stored{z}"), 16 * E // 2)
            with pool.Fori(0, NG) as i:
                for j in range(GB):
                    for k in range(2):
                        if j == 0 and k == 0:
                            pool.wait_ge(cb("added"), 2 * GB * i + 1)
                        nc.gpsimd.tensor_copy(sidx[:, j, k:k + 1], gidx[:, bass.ds(GB * i + j, 1), k]).then_inc(cb("first"), 1)
                pool.wait_ge(cb("first"), 2 * GB * i + 2 * GB)
                gate_pool()
                for j in range(GB):
                    for k in range(2):
                        nc.gpsimd.indirect_dma_start(
                            out=grow[:, j, k, :], out_offset=None, in_=eout,
                            in_offset=bass.IndirectOffsetOnAxis(ap=sidx[:, j, k:k + 1], axis=0),
                            bounds_check=E * CAP - 1, oob_is_err=False).then_inc(cb("gathered"), 16)
                rstd_pool(pool, 2, i)
                rstd_pool(pool, 3, i)

        def turned_act(act, n, i):
            s = nrm[n]
            for j in range(GB):
                act.wait_ge(s("turned"), GB * i + j + 1)
                nc.scalar.activation(xT[:, :, j * S:(j + 1) * S],
                                     PS[:, 6 + j % 2, 0:D].rearrange("p (k m) -> p k m", k=DK), ACT.Copy).then_inc(s("xT"), 1)

        def group_kv(act, layer, i):
            s = att[layer]
            for half in range(2):
                h = slice(64 * half, 64 * half + 64)
                src = kvT[h, bass.ds(GB * i, GB), :]
                nc.scalar.activation(kvg[h, :, half, :], src, ACT.Copy).then_inc(s("kvg"), 1)
                nc.scalar.activation(kvgr[h, :, half, :], src, ACT.Copy).then_inc(s("kvg"), 1)

        def attend_act(act, layer, i):
            s = att[layer]
            for k in range(NU + 3):
                n = k
                if n < NU:
                    act.wait_ge(s("scoresT"), NU * i + n + 1)
                    if n >= 2:
                        act.wait_ge(s("pv"), NU * i + n - 1)
                    nc.scalar.activation(PT[:, n % 2], PS[:, 2 + n % 2, :].rearrange("p (h m) -> p h m", h=4),
                                         ACT.Exp).then_inc(s("probs"), 1)
                n = k - 2
                if 0 <= n < NU:
                    act.wait_ge(s("turned"), NU * i + n + 1)
                    if n >= 2:
                        act.wait_ge(s("unit"), NU * i + n - 1)
                    nc.scalar.activation(cT[:, n % 2], PS[:, 5, 0:2 * P].rearrange("p (h m) -> p h m", h=2),
                                         ACT.Copy).then_inc(s("ctxT"), 1)

        def t_act(act, s, i, p, bank):
            act.wait_ge(s("t"), NP * i + p + 1)
            nc.scalar.activation(tT[:, p, :], PS[:, bank, :], ACT.Copy).then_inc(s("tT"), 1)
            nc.scalar.activation(tTr[:, p, :], PS[:, bank, :], ACT.Copy).then_inc(s("tT"), 1)

        @block.scalar
        def _(act):
            act.sem_inc(fold[0]("a_out"), 2)
            act.sem_inc(fold[1]("a_out"), 2)
            act.wait_ge(ld("gain"), 32)
            nc.scalar.activation(tg[:], gains[:], ACT.Tanh).then_inc(cs("tanh"), 1)
            for b in range(B):
                act.wait_ge(kvs("turned"), b + 1)
                nc.scalar.activation(kvT[:, b, :], PS[:, b % 4, 0:P], ACT.Copy).then_inc(kvs("copied"), 1)
            act.wait_ge(kvs("ones"), 3)
            act.wait_ge(kvs("copied"), B)
            with act.Fori(0, NP // 2) as i:
                for z in range(2):
                    p = 2 * i + z
                    act.wait_ge(fold[0]("product0"), 2 * i + z + 1)
                    for k in range(DK):
                        src = PS[:, 4 * z + k, :]
                        h0 = src[:, 0:DQ].rearrange("p (a q) -> p a q", a=2)
                        h1 = src[:, DQ:2 * DQ].rearrange("p (a q) -> p a q", a=2)
                        dst = A[:, k, bass.ds(p, 1)].rearrange("p n t m -> p (n t) m")
                        nc.scalar.activation(dst[:, 0:2, 0:LO], h0, ACT.Copy)
                        nc.scalar.activation(dst[:, 0:2, LO:P], h1[:, :, 0:P - LO], ACT.Copy)
                        last = nc.scalar.activation(dst[:, 2, :].rearrange("p (a m) -> p a m", a=2), h1[:, :, P - LO:LO], ACT.Copy)
                    last.then_inc(fold[0]("a_out"), 1)
            with act.Fori(0, NG) as i:
                group_kv(act, 0, i)
                turned_act(act, 0, i)
                for p in range(NP):
                    t_act(act, qsem, i, p, 6 + p % 2)
                attend_act(act, 0, i)
                turned_act(act, 1, i)
                act.wait_ge(rt("shifted"), i + 1)
                nc.scalar.activation(ebuf[:, 1], ebuf[:, 0], ACT.Exp).then_inc(rt("exp"), 1)
            with act.Fori(0, NP // 2) as i:
                for z in range(2):
                    act.wait_ge(fold[1]("product0"), 2 * i + z + 1)
                    nc.scalar.activation(at[:, z, 0:2, :].rearrange("p t d -> p (t d)"), PS[:, 4 * z, :], ACT.Copy)
                    nc.scalar.activation(at[:, z, 2, :], PS[:, 4 * z + 1, 0:D], ACT.Copy).then_inc(fold[1]("a_out"), 1)
            with act.Fori(0, E // 2) as i:
                for z in range(2):
                    e = 2 * i + z
                    for t in range(CT):
                        act.wait_ge(moe("turned"), CT * e + t + 1)
                        nc.scalar.activation(dT[:, z, :, t * P:(t + 1) * P], PS[:, t % 2, 0:D].rearrange("p (k m) -> p k m", k=DK),
                                             ACT.Copy).then_inc(moe("dT"), 1)
                    for f in range(FT):
                        act.wait_ge(moe("h"), FT * e + f + 1)
                        nc.scalar.activation(hT[:, f, :].rearrange("p (a c) -> p a c", a=2),
                                             PS[:, 2 + 2 * (f % 2):4 + 2 * (f % 2), 0:CAP // 2], ACT.Relu).then_inc(moe("relu"), 1)
            with act.Fori(0, NG) as i:
                group_kv(act, 1, i)
                turned_act(act, 2, i)
                for p in range(NP):
                    t_act(act, q1sem, i, p, 6 + p % 2)
                attend_act(act, 1, i)
                turned_act(act, 3, i)
                act.wait_ge(ff("step"), 3 * i + 1)
                nc.scalar.activation(rsm[:, 21, :], rsm[:, 20, :], ACT.Exp).then_inc(ff("exp"), 1)
                for f in range(DK):
                    act.wait_ge(ff("up"), DK * i + f + 1)
                    nc.scalar.activation(uT[:, f, :], PS[:, f, :], ACT.Relu).then_inc(ff("relu"), 1)

        def turn_pe(pe, n, i, src):
            s = nrm[n]
            for j in range(GB):
                pe.wait_ge(s("normed"), GB * i + j + 1)
                if j >= 2:
                    pe.wait_ge(s("xT"), GB * i + j - 1)
                for k in range(DK):
                    mm = nc.tensor.transpose(PS[:, 6 + j % 2, k * P:(k + 1) * P], src[:, j, k * P:(k + 1) * P], ident[:])
                mm.then_inc(s("turned"), 1)

        def attend_pe(pe, layer, i):
            s = att[layer]
            pe.wait_ge(s("kvg"), 4 * i + 4)
            for k in range(NU + 4):
                n = k
                if n < NU:
                    j, q = n // 4, n % 4
                    tok = slice(j * S, (j + 1) * S)
                    if n >= 2:
                        pe.wait_ge(s("negmax"), NU * i + n - 1)
                    for pp in range(2):
                        mm = nc.tensor.matmul(PS[:, n % 2, pp * 2 * P:(pp + 1) * 2 * P], tTr[:, 2 * q + pp, tok],
                                              kvgr[:, j].rearrange("p a m -> p (a m)"), start=True, stop=True)
                    mm.then_inc(s("scores"), 1)
                    if n >= 2:
                        pe.wait_ge(s("probs"), NU * i + n - 1)
                    bank = PS[:, 2 + n % 2, :].rearrange("p (g a m) -> p g a m", g=2, a=2)
                    for a in range(2):
                        nc.tensor.matmul(bank[:, :, a, :], kvg[:, j, a, :], tT[:, 2 * q:2 * q + 2, tok],
                                         start=(a == 0), stop=False, skip_group_check=True)
                n = k - 1
                if 0 <= n < NU:
                    pe.wait_ge(s("diag"), NU * i + n + 1)
                    nc.tensor.matmul(PS[:, 2 + n % 2, :], ones_r[:], diag[:, n % 2].rearrange("p h m -> p (h m)"),
                                     start=False, stop=True, skip_group_check=True).then_inc(s("scoresT"), 1)
                n = k - 2
                if 0 <= n < NU:
                    pe.wait_ge(s("probs"), NU * i + n + 1)
                    if n >= 1:
                        pe.wait_ge(s("ctx"), NU * i + n)
                    for hh in range(4):
                        mm = nc.tensor.matmul(PS[:, 4, hh * P:(hh + 1) * P], PT[:, n % 2, hh, :],
                                              kv_aug[:, bass.ds(GB * i + n // 4, 1), :].rearrange("p b m -> p (b m)"),
                                              start=True, stop=True)
                    mm.then_inc(s("pv"), 1)
                n = k - 3
                if 0 <= n < NU:
                    pe.wait_ge(s("ctx"), NU * i + n + 1)
                    if n >= 1:
                        pe.wait_ge(s("ctxT"), NU * i + n)
                    for g in range(2):
                        mm = nc.tensor.transpose(PS[:, 5, g * P:(g + 1) * P],
                                                 ctxn[:, n % 2, 2 * g:2 * g + 2, :].rearrange("p h c -> p (h c)"), ident[:])
                    mm.then_inc(s("turned"), 1)
                n = k - 4
                if 0 <= n < NU:
                    j, q = n // 4, n % 4
                    pe.wait_ge(s("ctxT"), NU * i + n + 1)
                    if q == 0 and j >= 2:
                        pe.wait_ge(s("resid"), GB * i + j - 1)
                    for g in range(2):
                        mm = nc.tensor.matmul(PS[:, 6 + j % 2, 0:D], cT[:, n % 2, g, :], U[:, 2 * q + g, :],
                                              start=(q == 0 and g == 0), stop=(q == 3 and g == 1))
                    mm.then_inc(s("unit"), 1)

        def fold_u(z):
            for h in range(2):
                mm = nc.tensor.matmul(PS[64 * h:64 * h + 64, 4 * z + 3, 0:D], st_kv[:, z, h, :], st_wo[:, z, h, :],
                                      start=True, stop=True)
            return mm

        def fold_mk(z):
            for t in range(3):
                nc.tensor.matmul(PS[:, 4 * z + 2, t * P:(t + 1) * P], st_qr[:, z, t, :], st_kr[:, z, :],
                                 start=True, stop=True)

        @block.tensor
        def _(pe):
            pe.sem_inc(fold[0]("product1"), 2)
            pe.sem_inc(fold[1]("product1"), 2)
            pe.sem_inc(moe("y"), 2 * CT)
            pe.wait_ge(cs("ident"), 4)
            pe.wait_ge(kvs("rope"), 2)
            for b in range(B):
                if b >= 4:
                    pe.wait_ge(kvs("copied"), b - 3)
                nc.tensor.transpose(PS[:, b % 4, 0:P], kv_dup[:, b, :], ident[:]).then_inc(kvs("turned"), 1)
            pe.wait_ge(kvs("copied"), B)
            f = fold[0]
            with pe.Fori(0, NP // 2) as i:
                for z in range(2):
                    pe.wait_ge(f(f"staged{z}"), STAGED * i + STAGED)
                    pe.wait_ge(f("a_out"), 2 * i + z + 1)
                    pe.wait_ge(f("mu_out"), 2 * i + z + 1)
                    for k in range(DK):
                        for h in range(2):
                            mm = nc.tensor.matmul(PS[:, 4 * z + k, h * DQ:(h + 1) * DQ], st_wq[:, z, h, k * P:(k + 1) * P],
                                                  st_cq[:, z, h, :], start=True, stop=True)
                    mm.then_inc(f("product0"), 1)
                    fold_mk(z)
                    fold_u(z).then_inc(f("product1"), 1)
            pe.wait_ge(f("a_out"), NP + 2)
            pe.wait_ge(f("mu_out"), NP + 2)
            pe.wait_ge(cs("ones"), 2)
            with pe.Fori(0, NG) as i:
                turn_pe(pe, 0, i, xn)
                pe.wait_ge(nrm[0]("xT"), GB * i + GB)
                for p in range(NP + 1):
                    if p < NP:
                        if p >= 2:
                            pe.wait_ge(qsem("cos"), 4 * NP * i + 4 * (p - 1))
                        for t in range(3):
                            for k in range(DK):
                                mm = nc.tensor.matmul(PS[:, 3 * (p % 2) + t, :], A[:, k, p, t, :], xT[:, k, :],
                                                      start=(k == 0), stop=(k == DK - 1))
                        mm.then_inc(qsem("q"), 1)
                    if p >= 1:
                        o = p - 1
                        pe.wait_ge(qsem("add"), 3 * NP * i + 3 * o + 3)
                        if o >= 2:
                            pe.wait_ge(qsem("tT"), 2 * NP * i + 2 * (o - 1))
                        for t in range(3):
                            mm = nc.tensor.matmul(PS[:, 6 + o % 2, :], MK[:, o, t, :], qr[:, o % 2, t, :],
                                                  start=(t == 0), stop=(t == 2))
                        mm.then_inc(qsem("t"), 1)
                pe.wait_ge(qsem("tT"), 2 * NP * i + 2 * NP)
                attend_pe(pe, 0, i)
                turn_pe(pe, 1, i, xn2)
                pe.wait_ge(nrm[1]("xT"), GB * i + GB)
                for j in range(GB):
                    for k in range(DK):
                        mm = nc.tensor.matmul(PS[:, 0, j * E:(j + 1) * E], xT[:, k, j * S:(j + 1) * S], wg0[:, k, :],
                                              start=(k == 0), stop=(k == DK - 1))
                mm.then_inc(rt("logits"), 1)
                pe.wait_ge(rt("step"), ROUTE_STEPS * i + MASK_STEP)
                nc.tensor.matmul(PS[:, 1, 0:GB * E], before[:], ebuf[:, 7].rearrange("p j e -> p (j e)"), start=True, stop=False)
                nc.tensor.matmul(PS[:, 1, 0:GB * E], ones[:], macc[:, 0:GB, :].rearrange("p j e -> p (j e)"),
                                 start=False, stop=True).then_inc(rt("pos"), 1)
            f = fold[1]
            with pe.Fori(0, NP // 2) as i:
                for z in range(2):
                    pe.wait_ge(f(f"staged{z}"), STAGED * i + STAGED)
                    pe.wait_ge(f("mu_out"), 2 * i + z + 1)
                    c0, c1 = st_cq[:, z, 0, :], st_cq[:, z, 1, :]
                    for t in range(2):
                        bank = PS[:, 4 * z, t * D:(t + 1) * D]
                        nc.tensor.matmul(bank[0:LO, :], c0[:, t * LO:(t + 1) * LO], st_wq[:, z, 0, :], start=True, stop=True)
                        nc.tensor.matmul(bank[LO:P, :], c1[:, t * LO:t * LO + P - LO], st_wq[:, z, 1, :], start=True, stop=True)
                    bank = PS[:, 4 * z + 1, 0:D]
                    for t in range(2):
                        mm = nc.tensor.matmul(bank[64 * t:64 * t + 64, :], c1[:, t * LO + P - LO:(t + 1) * LO], st_wq[:, z, 1, :],
                                              start=True, stop=True)
                    mm.then_inc(f("product0"), 1)
                    fold_mk(z)
                    fold_u(z).then_inc(f("product1"), 1)
                    pe.wait_ge(f("a_out"), 2 * i + z + 3)
                    pe.wait_ge(f("g_out"), 4 * i + 2 * z + 1)
                    for k in range(DK):
                        for t in range(3):
                            mm = nc.tensor.matmul(PS[:, 4 * z + 1, D + k * P:D + (k + 1) * P], at[:, z, t, k * P:(k + 1) * P],
                                                  mkst[:, z, t, :], start=(t == 0), stop=(t == 2))
                    mm.then_inc(f("product1b"), 1)
            pe.wait_ge(f("mu_out"), NP + 2)
            with pe.Fori(0, E // 2) as i:
                for z in range(2):
                    e = 2 * i + z
                    pe.wait_ge(moe(f"rows{z}"), 16 * i + 16)
                    for t in range(CT):
                        if t >= 2:
                            pe.wait_ge(moe("dT"), CT * e + t - 1)
                        for k in range(DK):
                            mm = nc.tensor.transpose(PS[:, t % 2, k * P:(k + 1) * P], dx[:, z, t, k * P:(k + 1) * P], ident[:])
                        mm.then_inc(moe("turned"), 1)
                    pe.wait_ge(moe("dT"), CT * e + CT)
                    pe.wait_ge(moe(f"weights{z}"), 32 * i + 32)
                    for f_ in range(FT):
                        if f_ >= 2:
                            pe.wait_ge(moe("relu"), FT * e + f_ - 1)
                        for c in range(2):
                            for k in range(DK):
                                mm = nc.tensor.matmul(PS[:, 2 + 2 * (f_ % 2) + c, 0:CAP // 2], w1[:, z, k, f_ * P:(f_ + 1) * P],
                                                      dT[:, z, k, c * (CAP // 2):(c + 1) * (CAP // 2)],
                                                      start=(k == 0), stop=(k == DK - 1))
                        mm.then_inc(moe("h"), 1)
                    pe.wait_ge(moe("relu"), FT * e + FT)
                    for t in range(CT):
                        pe.wait_ge(moe("y_out"), CT * e + t + 1)
                        for f_ in range(FT):
                            mm = nc.tensor.matmul(PS[:, 6 + (z * CT + t) % 2, 0:D], hT[:, f_, t * P:(t + 1) * P], w2[:, z, f_, :],
                                                  start=(f_ == 0), stop=(f_ == FT - 1))
                        mm.then_inc(moe("y"), 1)
            with pe.Fori(0, NG) as i:
                turn_pe(pe, 2, i, xn)
                pe.wait_ge(nrm[2]("xT"), GB * i + GB)
                for p in range(NP):
                    if p >= 2:
                        pe.wait_ge(q1sem("tT"), 2 * NP * i + 2 * (p - 1))
                    for k in range(DK):
                        mm = nc.tensor.matmul(PS[:, 6 + p % 2, :], G[:, k, p, :], xT[:, k, :], start=(k == 0), stop=(k == DK - 1))
                    mm.then_inc(q1sem("t"), 1)
                pe.wait_ge(q1sem("tT"), 2 * NP * i + 2 * NP)
                attend_pe(pe, 1, i)
                turn_pe(pe, 3, i, xn)
                pe.wait_ge(nrm[3]("xT"), GB * i + GB)
                for j in range(GB):
                    for k in range(DK):
                        mm = nc.tensor.matmul(PS[:, 2, j * E:(j + 1) * E], xT[:, k, j * S:(j + 1) * S], wg1[:, k, :],
                                              start=(k == 0), stop=(k == DK - 1))
                mm.then_inc(ff("logits"), 1)
                for f_ in range(DK):
                    for k in range(DK):
                        mm = nc.tensor.matmul(PS[:, f_, :], w_up[:, k, f_ * P:(f_ + 1) * P], xT[:, k, :],
                                              start=(k == 0), stop=(k == DK - 1))
                    mm.then_inc(ff("up"), 1)
                pe.wait_ge(ff("relu"), DK * i + DK)
                for j in range(GB):
                    bank = 3 + j
                    for k in range(DK):
                        nc.tensor.matmul(PS[:, bank, 0:D], uT[:, k, j * S:(j + 1) * S], w_dn_g[:, k, :],
                                         start=(k == 0), stop=(k == DK - 1))
                    for k in range(DK):
                        mm = nc.tensor.matmul(PS[:, bank, D:2 * D], xT[:, k, j * S:(j + 1) * S], w_ex[:, k, :],
                                              start=(k == 0), stop=(k == DK - 1))
                    mm.then_inc(ff("y"), 1)

        def norm_dve(dve, n, i, dst):
            s = nrm[n]
            gate_dve()
            for j in range(GB):
                nc.vector.bn_stats(stats[:, j, :], x[:, bass.ds(GB * i + j, 1), :].rearrange("p b d -> p (b d)")).then_inc(s("stats"), 1)
            dve.wait_ge(s("stats"), GB * i + GB)
            gate_dve()
            for j in range(GB):
                nc.vector.bn_aggr(mv[:, j, :], stats[:, j, :]).then_inc(s("mean"), 1)
            dve.wait_ge(s("rstd"), i + 1)
            for j in range(GB):
                nc.vector.tensor_scalar(dst[:, j, :], x[:, bass.ds(GB * i + j, 1), :].rearrange("p b d -> p (b d)"),
                                        mv[:, j, 0:1], rstd[:, j:j + 1], ALU.subtract, ALU.mult).then_inc(s("normed"), 1)

        def attend_dve(dve, layer, i):
            s = att[layer]
            for k in range(NU + 4):
                n = k
                if n < NU:
                    dve.wait_ge(s("scores"), NU * i + n + 1)
                    nc.vector.tensor_reduce(negm[:, n % 2, :], PS[:, n % 2, :].rearrange("p (h m) -> p h m", h=4),
                                            AX.X, ALU.max, negate=True).then_inc(s("negmax"), 1)
                    dve.wait_ge(s("negmax"), NU * i + n + 1)
                    if n >= 2:
                        dve.wait_ge(s("scoresT"), NU * i + n - 1)
                    nc.vector.tensor_tensor(diag[:, n % 2], ident[:].unsqueeze(1).to_broadcast([P, 4, P]),
                                            negm[:, n % 2, :].unsqueeze(2).to_broadcast([P, 4, P]),
                                            ALU.mult).then_inc(s("diag"), 1)
                n = k - 2
                if 0 <= n < NU:
                    ctx4 = PS[:, 4, :].rearrange("p (h m) -> p h m", h=4)
                    dve.wait_ge(s("pv"), NU * i + n + 1)
                    nc.vector.reciprocal(rinv[:, n % 2, :], ctx4[:, :, DC]).then_inc(s("rinv"), 1)
                    dve.wait_ge(s("rinv"), NU * i + n + 1)
                    if n >= 2:
                        dve.wait_ge(s("turned"), NU * i + n - 1)
                    nc.vector.tensor_tensor(ctxn[:, n % 2], ctx4[:, :, 0:DC],
                                            rinv[:, n % 2, :].unsqueeze(2).to_broadcast([P, 4, DC]), ALU.mult).then_inc(s("ctx"), 1)
                n = k - 4
                if 0 <= n < NU and n % 4 == 3:
                    j = n // 4
                    dve.wait_ge(s("unit"), NU * i + n + 1)
                    xb = x[:, bass.ds(GB * i + j, 1), :].rearrange("p b d -> p (b d)")
                    nc.vector.tensor_tensor(xb, PS[:, 6 + j % 2, 0:D], xb, ALU.add).then_inc(s("resid"), 1)
            dve.wait_ge(s("resid"), GB * i + GB)

        

        def route_dve(dve, i):
            count = [0]

            def step(ins):
                count[0] += 1
                ins.then_inc(rt("step"), 1)
                dve.wait_ge(rt("step"), ROUTE_STEPS * i + count[0])

            def wide(a):
                return a.unsqueeze(2).to_broadcast([P, GB, E])

            V = nc.vector
            logits = PS[:, 0, 0:GB * E].rearrange("p (j e) -> p j e", j=GB)
            tie_b = tie[:].unsqueeze(1).to_broadcast([P, GB, E])
            dve.wait_ge(rt("logits"), i + 1)
            step(V.tensor_reduce(rsm[:, 0, :], logits, AX.X, ALU.max))
            V.tensor_tensor(ebuf[:, 0], logits, wide(rsm[:, 0, :]), ALU.subtract).then_inc(rt("shifted"), 1)
            dve.wait_ge(rt("exp"), i + 1)
            step(V.tensor_reduce(rsm[:, 1, :], ebuf[:, 1], AX.X, ALU.add))
            step(V.reciprocal(rsm[:, 2, :], rsm[:, 1, :]))
            step(V.tensor_tensor(ebuf[:, 2], ebuf[:, 1], wide(rsm[:, 2, :]), ALU.mult))
            probs = ebuf[:, 2]
            for k in range(2):
                step(V.tensor_reduce(gates[:, k, :], probs, AX.X, ALU.max))
                step(V.tensor_tensor(ebuf[:, 3], probs, wide(gates[:, k, :]), ALU.is_equal))
                step(V.tensor_tensor(ebuf[:, 4], ebuf[:, 3], tie_b, ALU.mult))
                step(V.tensor_reduce(rsm[:, 3, :], ebuf[:, 4], AX.X, ALU.max))
                step(V.tensor_tensor(oh[:, k], ebuf[:, 4], wide(rsm[:, 3, :]), ALU.is_equal))
                if k == 0:
                    step(V.scalar_tensor_tensor(out=ebuf[:, 5].rearrange("p j e -> p (j e)"), in0=oh[:, 0].rearrange("p j e -> p (j e)"),
                                                scalar=-2.0, in1=ebuf[:, 2].rearrange("p j e -> p (j e)"), op0=ALU.mult, op1=ALU.add))
                    probs = ebuf[:, 5]
            step(V.tensor_tensor(ebuf[:, 7], oh[:, 0], oh[:, 1], ALU.add))
            step(V.tensor_copy(macc[:, 0, :], macc[:, GB, :]))
            for j in range(GB):
                step(V.tensor_tensor(macc[:, j + 1, :], macc[:, j, :], ebuf[:, 7, j, :], ALU.add))
            assert count[0] == MASK_STEP, count
            dve.wait_ge(rt("pos"), i + 1)
            pos = PS[:, 1, 0:GB * E].rearrange("p (j e) -> p j e", j=GB)
            step(V.tensor_scalar(ebuf[:, 8], pos, float(CAP), None, ALU.is_lt))
            step(V.tensor_tensor(ebuf[:, 9], pos, base[:].unsqueeze(1).to_broadcast([P, GB, E]), ALU.add))
            for k in range(2):
                step(V.tensor_tensor(sbuf2[:, k], oh[:, k], ebuf[:, 8], ALU.mult))
            step(V.tensor_reduce(keep[:], sbuf2[:], AX.X, ALU.add))
            for k in range(2):
                step(V.tensor_tensor(sbuf2[:, k], oh[:, k], ebuf[:, 9], ALU.mult))
            step(V.tensor_reduce(slot[:], sbuf2[:], AX.X, ALU.add))
            kf, sf = keep[:], slot[:]
            r = rsm[:, 4:6, :]
            step(V.tensor_scalar(r, kf, -DROPPED, DROPPED, ALU.mult, ALU.add))
            step(V.tensor_tensor(sidx[:].rearrange("p j k -> p k j"), r, sf, ALU.add))
            step(V.tensor_tensor(gidx[:, bass.ds(GB * i, GB), :].rearrange("p j k -> p k j"), sf, kf, ALU.mult))
            step(V.tensor_tensor(rsm[:, 6:8, :], gates[:], kf, ALU.mult))
            step(V.tensor_scalar(gw[:, bass.ds(GB * i, GB), :].rearrange("p j k -> p k j"), rsm[:, 6:8, :], tg[:, 2:3], None, ALU.mult))
            assert count[0] == ROUTE_STEPS, count

        @block.vector
        def _(dve):
            V = nc.vector
            V.memset(kvg[:], 0.0).then_inc(kvs("ones"), 1)
            V.memset(kvgr[:].bitcast(F32), 0.0).then_inc(kvs("ones"), 1)
            V.memset(kv_aug[:, :, DC:P], 1.0).then_inc(kvs("ones"), 1)
            V.memset(macc[:], 0.0).then_inc(rt("carry"), 1)
            dve.sem_inc(fold[0]("mu_out"), 2)
            dve.sem_inc(fold[1]("mu_out"), 2)
            dve.sem_inc(moe("y_out"), 2)
            dve.sem_inc(cb("added"), 1)
            V.memset(scrap[:], 0.0).then_inc(cs("misc"), 1)
            dve.wait_ge(ld("kv"), 32)
            V.tensor_tensor(kv_cos, kv_raw, kv_tab[:, 0, :].unsqueeze(1).to_broadcast([P, B, DC]), ALU.mult).then_inc(kvs("cos"), 1)
            for a in range(2):
                o, s_ = slice(32 * a, 32 * a + 32), slice(32 - 32 * a, 64 - 32 * a)
                V.tensor_tensor(kv_sin[:, :, o], kv_raw[:, :, s_], kv_tab[:, 1, o].unsqueeze(1).to_broadcast([P, B, 32]),
                                ALU.mult).then_inc(kvs("sin"), 1)
            dve.wait_ge(kvs("cos"), 1)
            dve.wait_ge(kvs("sin"), 2)
            V.tensor_tensor(kv_aug[:, :, 0:DC], kv_cos, kv_sin, ALU.add).then_inc(kvs("rope"), 1)
            V.tensor_tensor(kv_dup.rearrange("p b (a c) -> p b a c", a=2), kv_cos.unsqueeze(2).to_broadcast([P, B, 2, DC]),
                            kv_sin.unsqueeze(2).to_broadcast([P, B, 2, DC]), ALU.add).then_inc(kvs("rope"), 1)
            dve.wait_ge(cs("ones"), 1)
            V.tensor_copy(ones_r[:], ones[:]).then_inc(cs("ones"), 1)
            dve.wait_ge(cs("tanh"), 1)
            with dve.Fori(0, NP // 2) as i:
                for z in range(2):
                    p = 2 * i + z
                    dve.wait_ge(fold[0]("product1"), 2 * i + z + 3)
                    V.tensor_copy(MK[:, bass.ds(p, 1)].rearrange("p n t m -> p (n t m)"), PS[:, 4 * z + 2, 0:3 * P])
                    V.tensor_scalar(U[:, bass.ds(p, 1), :].rearrange("p n d -> p (n d)"), PS[:, 4 * z + 3, 0:D], tg[:, 0:1], None,
                                    ALU.mult).then_inc(fold[0]("mu_out"), 1)
            dve.wait_ge(ld("const"), 16 * 7)
            V.tensor_scalar(w_dn_g[:], w_dn[:], tg[:, 3:4], None, ALU.mult).then_inc(cs("wdn"), 1)
            dve.wait_ge(ld("x"), 16)
            dve.wait_ge(cs("misc"), 7)
            with dve.Fori(0, NG) as i:
                norm_dve(dve, 0, i, xn)
                for p in range(NP):
                    z = p % 2
                    dve.wait_ge(qsem("q"), NP * i + p + 1)
                    if p >= 2:
                        dve.wait_ge(qsem("add"), 3 * NP * i + 3 * (p - 1))
                    q = PS[:, 3 * z:3 * z + 3, :].rearrange("p t (j s) -> p t j s", j=GB)
                    c_ = qc[:, z].rearrange("p t (j s) -> p t j s", j=GB)
                    s_ = qs[:, z].rearrange("p t (j s) -> p t j s", j=GB)

                    def tab(t, rows, lo, hi):
                        return t[rows, lo:hi, :].unsqueeze(2).to_broadcast([rows.stop - rows.start, hi - lo, GB, S])

                    every = slice(0, P)
                    V.tensor_tensor(c_, q, tab(cosq, every, 0, 3), ALU.mult).then_inc(qsem("cos"), 1)
                    V.tensor_tensor(s_[:, 0:2], q[:, 0:2], tab(sinq, every, 0, 2), ALU.mult).then_inc(qsem("cos"), 1)
                    for a in range(2):
                        src, dst = slice(64 * a, 64 * a + 64), slice(64 - 64 * a, P - 64 * a)
                        V.tensor_tensor(s_[dst, 2], q[src, 2], sinq[src, 2, :].unsqueeze(1).to_broadcast([64, GB, S]), ALU.mult).then_inc(qsem("cos"), 1)
                attend_dve(dve, 0, i)
                dve.wait_ge(rt("sent"), i + 1)
                norm_dve(dve, 1, i, xn2)
                route_dve(dve, i)
            with dve.Fori(0, NP // 2) as i:
                for z in range(2):
                    p = 2 * i + z
                    dve.wait_ge(fold[1]("product1"), 2 * i + z + 3)
                    V.tensor_copy(mkst[:, z].rearrange("p t m -> p (t m)"), PS[:, 4 * z + 2, 0:3 * P]).then_inc(fold[1]("g_out"), 1)
                    V.tensor_scalar(U[:, bass.ds(p, 1), :].rearrange("p n d -> p (n d)"), PS[:, 4 * z + 3, 0:D], tg[:, 1:2], None,
                                    ALU.mult).then_inc(fold[1]("g_out"), 1)
                    dve.wait_ge(fold[1]("product1b"), 2 * i + z + 1)
                    V.tensor_copy(G[:, :, bass.ds(p, 1), :].rearrange("p k n m -> p k (n m)"),
                                  PS[:, 4 * z + 1, D:2 * D].rearrange("p (k m) -> p k m", k=DK)).then_inc(fold[1]("mu_out"), 1)
            with dve.Fori(0, E // 2) as i:
                for z in range(2):
                    e = 2 * i + z
                    dve.wait_ge(moe("eo_free"), e + 1)
                    for t in range(CT):
                        dve.wait_ge(moe("y"), CT * e + 2 * CT + t + 1)
                        V.tensor_copy(eo[:, z, t, :], PS[:, 6 + (z * CT + t) % 2, 0:D]).then_inc(moe("y_out"), 1)
            with dve.Fori(0, NG) as i:
                for j in range(GB):
                    for k in range(2):
                        b = GB * i + j
                        xb = x[:, bass.ds(b, 1), :].rearrange("p b d -> p (b d)")
                        if j == 0 and k == 0:
                            dve.wait_ge(cb("gathered"), 32 * GB * i + 32 * GB)
                        if k == 1:
                            dve.wait_ge(cb("added"), 2 * b + 2)
                        V.scalar_tensor_tensor(out=xb, in0=grow[:, j, k, :], scalar=gw[:, bass.ds(b, 1), k], in1=xb,
                                               op0=ALU.mult, op1=ALU.add).then_inc(cb("added"), 1)
                dve.wait_ge(cb("added"), 2 * GB * i + 2 * GB + 1)
                norm_dve(dve, 2, i, xn)
                attend_dve(dve, 1, i)
                norm_dve(dve, 3, i, xn)
                dve.wait_ge(ff("logits"), i + 1)
                gate_dve()
                for j in range(GB):
                    V.max(top8[:, j, :], PS[:, 2, j * E:(j + 1) * E]).then_inc(ff("rw"), 1)
                dve.wait_ge(ff("rw"), 8 * i + 4)
                V.tensor_tensor(rsm[:, 20, :], top8[:, :, 1], top8[:, :, 0], ALU.subtract).then_inc(ff("step"), 1)
                dve.wait_ge(ff("exp"), i + 1)
                V.tensor_scalar(rsm[:, 22, :], rsm[:, 21, :], 1.0, None, ALU.add).then_inc(ff("step"), 1)
                dve.wait_ge(ff("step"), 3 * i + 2)
                V.reciprocal(rsm[:, 23, :], rsm[:, 22, :]).then_inc(ff("step"), 1)
                dve.wait_ge(ff("step"), 3 * i + 3)
                V.tensor_tensor(rsm[:, 8, :], rsm[:, 21, :], rsm[:, 23, :], ALU.mult).then_inc(ff("rw"), 1)
                dve.wait_ge(ff("rw"), 8 * i + 5)
                V.tensor_tensor(rsm[:, 9, :], rsm[:, 8, :], rsm[:, 23, :], ALU.add).then_inc(ff("rw"), 1)
                dve.wait_ge(ff("rw"), 8 * i + 6)
                V.tensor_scalar(rsm[:, 10, :], rsm[:, 9, :], tg[:, 3:4], None, ALU.mult).then_inc(ff("rw"), 2)
                dve.wait_ge(ff("rw"), 8 * i + 8)
                for j in range(GB):
                    b = GB * i + j
                    xb = x[:, bass.ds(b, 1), :].rearrange("p b d -> p (b d)")
                    dve.wait_ge(ff("y"), b + 1)
                    V.tensor_tensor(xb, PS[:, 3 + j, 0:D], xb, ALU.add).then_inc(ff("added"), 1)
                    dve.wait_ge(ff("added"), 2 * b + 1)
                    V.scalar_tensor_tensor(out=xb, in0=PS[:, 3 + j, D:2 * D], scalar=rsm[:, 10, j:j + 1], in1=xb,
                                           op0=ALU.mult, op1=ALU.add).then_inc(ff("added"), 1)


def rope_tables(length, dim):
    inv = (np.float32(1.0) / np.float32(10000.0) ** (np.arange(0, dim, 2, dtype=np.float32) / np.float32(dim))).astype(np.float32)
    f = np.arange(length, dtype=np.float32)[:, None] * inv[None, :]
    return np.repeat(np.sin(f), 2, axis=-1), np.repeat(np.cos(f), 2, axis=-1)


def query_tables():
    sin, cos = rope_tables(S, DQ)
    r = np.arange(P)
    q = np.stack([np.where(r < LO, r, r - LO), np.where(r < LO, r, r - LO) + LO,
                  np.where(r < 64, P - LO + r, P + r - 64)], axis=1)
    partner = np.where(q >= LO, q - LO, q + LO)
    sign = np.where(q >= LO, -1.0, 1.0).astype(np.float32)
    return (np.ascontiguousarray(cos.T[q], np.float32),
            np.ascontiguousarray(sin.T[partner] * sign[:, :, None], np.float32))


def context_table():
    sin, cos = rope_tables(S, DC)
    sign = np.where(np.arange(DC) < DC // 2, -1.0, 1.0).astype(np.float32)
    return np.ascontiguousarray(np.stack([cos, sin * sign], axis=1), np.float32)


def kernel(**inputs):
    import concourse.bacc as bacc
    from concourse.bass_utils import run_bass_kernel_spmd

    nc = bacc.Bacc("TRN2", target_bir_lowering=False, num_devices=1)
    arrays = {}

    def give(name, a):
        a = np.ascontiguousarray(a)
        arrays["in_" + name] = a
        return nc.dram_tensor("in_" + name, a.shape, mybir.dt.from_np(a.dtype), kind="ExternalInput").ap()

    def raw(name):
        return np.asarray(inputs[name])

    cosq, sinq = query_tables()
    io = {
        "x": give("x", raw("x")).rearrange("b s d -> s b d"),
        "ctx": give("ctx", raw("ctx_512")).rearrange("b l c -> l b c"),
        "g_xattn": give("g_xattn", raw("g_xattn").reshape(1, 2)).to_broadcast([P, 2]),
        "g_ffn": give("g_ffn", raw("g_ffn").reshape(1, 2)).to_broadcast([P, 2]),
        "cosq": give("cosq", cosq),
        "sinq": give("sinq", sinq),
        "kv_tab": give("kv_tab", context_table()),
        "wg0": give("wg0", raw("L0_ffn_Wg")).rearrange("(k p) e -> p k e", p=P),
        "w1": give("w1", raw("L0_ffn_w1")),
        "w2": give("w2", raw("L0_ffn_w2")),
        "wg1": give("wg1", raw("L1_ffn_W_gate").T).rearrange("(k p) e -> p k e", p=P),
        "w_up": give("w_up", raw("L1_ffn_W_up").T).rearrange("(k p) e -> p k e", p=P),
        "w_dn": give("w_dn", raw("L1_ffn_W_down").T).rearrange("(k p) e -> p k e", p=P),
        "w_ex": give("w_ex", raw("L1_ffn_W_expert")).rearrange("(k p) e -> p k e", p=P),
    }
    for n in LAYERS:
        io[n] = {
            "wq": give(f"wq{n}", raw(f"L{n}_xattn_Wq")).rearrange("(h k) d -> k h d", h=H),
            "w_kc_q": give(f"w_kc_q{n}", raw(f"L{n}_xattn_w_kc_q")).rearrange("h k q -> k h q"),
            "w_kc_kv": give(f"w_kc_kv{n}", raw(f"L{n}_xattn_w_kc_kv")).rearrange("h k c -> k h c"),
            "woT": give(f"woT{n}", raw(f"L{n}_xattn_Wo").T).rearrange("(h k) d -> k h d", h=H),
            "wqrT": give(f"wqrT{n}", raw(f"L{n}_xattn_W_qr").transpose(2, 0, 1)),
            "wkrT": give(f"wkrT{n}", raw(f"L{n}_xattn_W_kr").transpose(2, 0, 1)),
        }
    out = nc.dram_tensor("out", (B, S, D), F32, kind="ExternalOutput").ap()
    io["out"] = out.rearrange("b s d -> s b d")
    build(nc, io)
    done = run_bass_kernel_spmd(nc, [arrays], core_ids=[0])
    return done.results[0]["out"]
```

```python
from contextlib import ExitStack

import numpy as np

import concourse.bass as bass
from concourse import mybir

F32 = mybir.dt.float32
F32R = mybir.dt.float32r
I32 = mybir.dt.int32
ALU = mybir.AluOpType
ACT = mybir.ActivationFunctionType
AX = mybir.AxisListType

P = 128
B, S, D = 16, 128, 256
H, KH, DC, DQ = 16, 128, 64, 192
LO = DQ // 2
NP = H // 2
DK = D // P
GB = 4
NG = B // GB
TG = GB * S
NU = GB * H // 4
E, FF = 8, 1024
CAP = int(np.ceil(1.25 * B * S * 2 / E))
CT = CAP // P
FT = FF // P
DROPPED = 1.0e5
EPS = 1e-5

LAYERS = (0, 1)
PACK = (("wq", 2 * D), ("cq", 2 * DQ), ("kv", 2 * DC), ("wo", 2 * D), ("qr", 3 * P), ("kr", P))
PACKED = sum(n for _, n in PACK)


def build(nc, io):
    with ExitStack() as ctx:
        def sb(name, shape, dt=F32):
            return ctx.enter_context(nc.sbuf_tensor(name, shape, dt))

        def sem(name):
            return ctx.enter_context(nc.semaphore(name))

        class Sems:

            def __init__(self, stage, signals):
                self.of = {s: sem(f"{stage}_{s}") for s in signals.split()}

            def __call__(self, s):
                return self.of[s]

        PS = ctx.enter_context(nc.psum_tensor("PS", [P, 8, 512], F32))
        disp = nc.dram_tensor("disp_rows", (E * CAP, D), F32, kind="Internal").ap()
        eout = nc.dram_tensor("expert_rows", (E * CAP, D), F32, kind="Internal").ap()

        x = sb("x_res", [P, B, D])
        kv_r = sb("kv_roped", [P, B, DC])
        kvT = sb("kvT", [P, B, P])
        U = sb("U_out", [P, NP, D])
        G = sb("G_score", [P, DK, NP, P])
        wf = sb("w_ffn1", [P, 4, DK, D])
        xn = sb("x_norm", [P, GB, D])
        xn2 = sb("x_norm_ffn", [P, GB, D])
        xT = sb("xT", [P, DK, TG])
        xT2 = sb("xT_ffn", [P, DK, TG])
        tTr = sb("tT_round", [P, NP, TG], F32R)
        kvg = sb("kv_group", [P, GB, 2, P])
        kvgr = sb("kv_group_round", [P, GB, 2, P], F32R)
        kvag = sb("kv_group_ones", [P, GB, 3 * DC])
        diag = sb("diag", [P, 2, 4, P], F32R)
        PT = sb("probT", [P, 2, 4, P])
        cT = sb("ctxT", [P, 2, 2, P])
        sums = sb("exp_sums", [P, 2, 2, P])
        rinv = sb("sum_inv", [P, 2, 2, P])
        ident = sb("ident", [P, P])
        before = sb("before", [P, P])
        ones = sb("ones", [P, P])
        ones_r = sb("ones_round", [P, P], F32R)
        epsv = sb("eps", [P, GB])
        scrap_p = sb("scrap_pool", [P, 1])
        scrap = sb("scrap", [P, 1])
        mhalf = sb("minus_half", [P, GB])
        cosq = sb("cosq", [P, 3, S])
        sinq = sb("sinq", [P, 3, S])
        kv_tab = sb("kv_tab", [P, 2, DC])
        gains = sb("gains", [P, 4])
        tg = sb("tanh_gains", [P, 4])
        wg0 = sb("wg0", [P, DK, E])
        wg1 = sb("wg1", [P, DK, E])
        stats = sb("stats", [P, GB, 6])
        mv = sb("mean_var", [P, GB, 2])
        veps = sb("var_eps", [P, GB])
        rstd = sb("rstd", [P, GB])
        stats2 = sb("stats_ffn", [P, GB, 6])
        mv2 = sb("mean_var_ffn", [P, GB, 2])
        veps2 = sb("var_eps_ffn", [P, GB])
        rstd2 = sb("rstd_ffn", [P, GB])
        negm = sb("neg_max", [P, 2, 4])
        tie = sb("tie_order", [P, E])
        base = sb("slot_base", [P, E])
        ebuf = sb("route_tmp", [P, 10, GB, E])
        oh = sb("chosen", [P, 2, GB, E])
        sel = sb("chosen_value", [P, 2, GB, E])
        macc = sb("chosen_before", [P, GB + 1, E])
        rsm = sb("route_small", [P, 16, GB])
        keep = sb("keep", [P, 2, GB])
        slot = sb("slot", [P, 2, GB])
        gates = sb("gates", [P, 2, GB])
        sidx = sb("scatter_idx", [P, GB, 2], I32)
        gidx = sb("gather_idx", [P, B, 2], I32)
        gw = sb("gate_weight", [P, B, 2])
        top8 = sb("top8", [P, GB, E])

        arena = sb("arena", [P, 88 * 256])

        def area(kib, n):
            return arena[:, kib * 256:kib * 256 + n]

        A = area(0, DK * NP * 3 * P).rearrange("p (k n t m) -> p k n t m", k=DK, n=NP, t=3)
        MK = area(24, NP * 3 * P).rearrange("p (n t m) -> p n t m", n=NP, t=3)
        qc = area(36, 2 * 3 * TG).rearrange("p (z t n) -> p z t n", z=2, t=3)
        qs = area(48, 2 * 3 * TG).rearrange("p (z t n) -> p z t n", z=2, t=3)
        qr = area(60, 2 * 3 * TG).rearrange("p (z t n) -> p z t n", z=2, t=3)
        tT = area(72, NP * TG).rearrange("p (n t) -> p n t", n=NP)
        kv_dup = area(0, B * P).rearrange("p (b m) -> p b m", b=B)
        kv_raw = area(72, B * DC).rearrange("p (b c) -> p b c", b=B)
        kv_sin = area(76, B * DC).rearrange("p (b c) -> p b c", b=B)
        kv_cos = area(80, B * DC).rearrange("p (b c) -> p b c", b=B)
        mkst = area(52, 2 * 3 * P).rearrange("p (z t m) -> p z t m", z=2, t=3)
        at = area(55, 2 * 3 * D).rearrange("p (z t d) -> p z t d", z=2, t=3)
        w1 = area(0, 2 * DK * FF).rearrange("p (z k f) -> p z k f", z=2, k=DK)
        w2 = area(16, 2 * FT * D).rearrange("p (z f d) -> p z f d", z=2, f=FT)
        hT = area(36, FT * CAP).rearrange("p (f c) -> p f c", f=FT)
        dx = area(56, 2 * CT * D).rearrange("p (z t d) -> p z t d", z=2, t=CT)
        dT = area(66, 2 * DK * CAP).rearrange("p (z k c) -> p z k c", z=2, k=DK)
        eo = area(76, 2 * CT * D).rearrange("p (z t d) -> p z t d", z=2, t=CT)
        grow = area(0, GB * 2 * D).rearrange("p (j k d) -> p j k d", j=GB, k=2)
        uT = area(8, DK * TG).rearrange("p (k t) -> p k t", k=DK)

        staging = [[G[:].rearrange("p k n m -> p (k n m)"), wf[:].rearrange("p w k d -> p (w k d)")],
                   [area(36, PACKED), area(44, PACKED)]]

        def part(layer, z, name):
            at_ = 0
            for n, size in PACK:
                if n == name:
                    return staging[layer][z][:, at_:at_ + size]
                at_ += size

        def staged(layer, z):
            def heads(n):
                return part(layer, z, n).rearrange("p (h m) -> p h m", h=2)
            return (heads("wq"), heads("cq"), heads("kv"), heads("wo"),
                    part(layer, z, "qr").rearrange("p (t m) -> p t m", t=3), part(layer, z, "kr"))

        ld = Sems("load", "x0 x kv tab router gain zero ffn")
        cs = Sems("const", "ident ones misc tanh zeros")
        kvs = Sems("kv", "cos sin rope ones turned copied")
        fold = [Sems(f"fold{n}", "staged0 staged1 product score_w out g_out") for n in LAYERS]
        NORM = "stats mean rstd normed turned xT veps"
        nrm = [Sems(f"norm_{n}", NORM) for n in ("att0", "ffn0", "att1", "ffn1")]
        qsem = Sems("query0", "q cos add t tT")
        q1sem = Sems("query1", "t tT")
        att = [Sems(f"att{n}", "scores negmax diag scoresT probs pv sums ln guess near1 rinv ctx unit resid kvg") for n in LAYERS]
        rt = Sems("route", "logits shifted exp step pos scattered sent carry")
        MASK_STEP, ROUTE_STEPS = 21, 34
        moe = Sems("moe", "weights0 weights1 rows0 rows1 turned dT h relu y y_out stored0 stored1 eo_free")
        cb = Sems("combine", "index gathered0 gathered1 gathered2 gathered3 added")
        ff = Sems("ffn1", "logits step exp rw up relu y added stored w_down")
        NBUF = [(stats, mv, veps, rstd, xn, xT), (stats2, mv2, veps2, rstd2, xn2, xT2)] * 2

        block = ctx.enter_context(nc.Block())

        @block.sync
        def _(sp):
            def stage(layer, p):
                if p >= 2:
                    sp.wait_ge(fold[layer]("product"), p - 1)
                sp.dma_start(staging[layer][p % 2], io[layer][:, p, :]).then_inc(fold[layer](f"staged{p % 2}"), 16)

            sp.dma_start(kv_raw, io["ctx"]).then_inc(ld("kv"), 16)
            sp.dma_start(kv_tab[:], io["kv_tab"]).then_inc(ld("kv"), 16)
            stage(0, 0)
            sp.dma_start(x[:, 0:GB, :], io["x"][:, 0:GB, :]).then_inc(ld("x0"), 16)
            sp.dma_start(gains[:, 0:2], io["g_xattn"]).then_inc(ld("gain"), 16)
            sp.dma_start(gains[:, 2:4], io["g_ffn"]).then_inc(ld("gain"), 16)
            for dst, src in ((cosq[:], io["cosq"]), (sinq[:], io["sinq"])):
                sp.dma_start(dst, src).then_inc(ld("tab"), 16)
            for p in range(1, NP):
                stage(0, p)
            sp.dma_start(x[:, GB:B, :], io["x"][:, GB:B, :]).then_inc(ld("x"), 16)
            sp.dma_start(wg0[:], io["wg0"]).then_inc(ld("router"), 16)
            sp.dma_start(wg1[:], io["wg1"]).then_inc(ld("router"), 16)
            sp.wait_ge(cs("zeros"), 1)
            for n in range(E * CAP // (GB * P)):
                sp.dma_start(disp[n * GB * P:(n + 1) * GB * P, :].rearrange("(p j) d -> p j d", p=P),
                             xn2[:]).then_inc(ld("zero"), 16)
            sp.wait_ge(fold[0]("product"), NP)
            for n, name in enumerate(("w_up", "w_dn", "w_ex")):
                sp.dma_start(wf[:, n], io[name]).then_inc(ld("ffn"), 16)
            sp.wait_ge(qsem("t"), NG * NP)
            for p in range(NP):
                stage(1, p)
            sp.wait_ge(rt("step"), ROUTE_STEPS * NG)

            with sp.Fori(0, E // 2) as i:
                for z in range(2):
                    e = 2 * i + z
                    sp.wait_ge(moe("y"), 2 * CT * i + CT * (z + 1))
                    sp.dma_start(w1[:, z], io["w1"][bass.ds(e, 1), :, :].rearrange("e (k p) f -> p (e k) f", p=P)).then_inc(moe(f"weights{z}"), 16)
                    sp.dma_start(w2[:, z], io["w2"][bass.ds(e, 1), :, :].rearrange("e (k p) f -> p (e k) f", p=P)).then_inc(moe(f"weights{z}"), 16)
                    if z == 0:
                        sp.wait_ge(rt("scattered"), 16 * 2 * B)
                        sp.wait_ge(fold[1]("g_out"), NP)
                    sp.dma_start(dx[:, z], disp.rearrange("(e t p) d -> e p t d", e=E, p=P)[bass.ds(e, 1)].rearrange("e p t d -> p (e t) d")).then_inc(moe(f"rows{z}"), 16)
            for i in range(NG):
                sp.wait_ge(ff("added"), GB * 2 * i + GB * 2)
                sp.dma_start(io["out"][:, GB * i:GB * i + GB, :], x[:, GB * i:GB * i + GB, :]).then_inc(ff("stored"), 16)
            sp.wait_ge(ff("stored"), 16 * NG)

        def gate_dve():
            nc.vector.memset(scrap[:], 0.0)

        def gate_pool():
            nc.gpsimd.tensor_tensor(scrap_p[:], mhalf[:, 0:1], mhalf[:, 0:1], ALU.add)

        def rstd_pool(pool, n, i):
            s, (_, mv_, veps_, rstd_, _, _) = nrm[n], NBUF[n]
            pool.wait_ge(s("mean"), GB * i + GB)
            nc.gpsimd.tensor_tensor(veps_[:], mv_[:, :, 1], epsv[:], ALU.add).then_inc(s("veps"), 1)
            pool.wait_ge(s("veps"), i + 1)
            nc.gpsimd.tensor_tensor(rstd_[:], veps_[:], mhalf[:], ALU.pow).then_inc(s("rstd"), 1)

        def attend_pool(pool, layer, i, beside):
            s = att[layer]
            for n in range(NU):
                pool.wait_ge(s("guess"), NU * i + n + 1)
                nc.gpsimd.tensor_tensor(sums[:, n % 2], sums[:, n % 2], rinv[:, n % 2], ALU.mult).then_inc(s("near1"), 1)
                beside(n)

        def scatter_pool(pool, i, j, k):
            nc.gpsimd.indirect_dma_start(
                out=disp, out_offset=bass.IndirectOffsetOnAxis(ap=sidx[:, j, k:k + 1], axis=0),
                in_=xn2[:, j, :], in_offset=None, bounds_check=E * CAP - 1,
                oob_is_err=False).then_inc(rt("scattered"), 16)

        def scattered_pool(pool, i):
            pool.wait_ge(rt("scattered"), 16 * 2 * GB * i + 16 * 2 * GB)
            pool.sem_inc(rt("sent"), 1)

        def gathers_pool(pool, i):
            pool.wait_ge(cb("added"), 2 * GB * i + 1)
            for j in range(GB):
                for k in range(2):
                    nc.gpsimd.tensor_copy(sidx[:, j, k:k + 1], gidx[:, bass.ds(GB * i + j, 1), k]).then_inc(cb("index"), 1)
            pool.wait_ge(cb("index"), 2 * GB * i + 2 * GB)
            gate_pool()
            for j in range(GB):
                for k in range(2):
                    nc.gpsimd.indirect_dma_start(
                        out=grow[:, j, k, :], out_offset=None, in_=eout,
                        in_offset=bass.IndirectOffsetOnAxis(ap=sidx[:, j, k:k + 1], axis=0),
                        bounds_check=E * CAP - 1, oob_is_err=False).then_inc(cb(f"gathered{j}"), 16)

        def layer0_pool(pool, i, first, last):
            for p in range(NP):
                pool.wait_ge(qsem("cos"), 4 * NP * i + 4 * p + 4)
                if p >= 2:
                    pool.wait_ge(qsem("t"), NP * i + p - 1)
                z = p % 2
                for t in range(3):
                    nc.gpsimd.tensor_tensor(qr[:, z, t, :], qc[:, z, t, :], qs[:, z, (1, 0, 2)[t], :],
                                            ALU.add).then_inc(qsem("add"), 1)
                if p == 0 and not first:
                    rstd_pool(pool, 1, i - 1)

            def beside(k):
                if not last and k == 3:
                    rstd_pool(pool, 0, i + 1)
                if not first and k == 4:
                    pool.wait_ge(rt("step"), ROUTE_STEPS * (i - 1) + ROUTE_STEPS)
                    gate_pool()
                if not first and 4 <= k < 12:
                    scatter_pool(pool, i - 1, (k - 4) // 2, (k - 4) % 2)
                if not first and k == NU - 1:
                    scattered_pool(pool, i - 1)

            attend_pool(pool, 0, i, beside)

        def layer1_pool(pool, i, last):
            if not last:
                gathers_pool(pool, i + 1)

            def beside(k):
                if not last and k == 4:
                    rstd_pool(pool, 2, i + 1)

            attend_pool(pool, 1, i, beside)
            rstd_pool(pool, 3, i)

        @block.gpsimd
        def _(pool):
            nc.gpsimd.memset(ident[:], 0.0).then_inc(cs("ident"), 1)
            nc.gpsimd.memset(before[:], 1.0).then_inc(cs("ident"), 1)
            pool.wait_ge(cs("ident"), 2)
            nc.gpsimd.affine_select(out=ident[:], in_=ident[:], compare_op=ALU.not_equal, fill=1.0, base=0,
                                    pattern=[[-1, P]], channel_multiplier=1).then_inc(cs("ident"), 1)
            nc.gpsimd.affine_select(out=before[:], in_=before[:], compare_op=ALU.is_gt, fill=0.0, base=0,
                                    pattern=[[1, P]], channel_multiplier=-1).then_inc(cs("ident"), 1)
            nc.gpsimd.memset(ones[:], 1.0).then_inc(cs("ones"), 1)
            nc.gpsimd.memset(mhalf[:], -0.5).then_inc(cs("misc"), 1)
            nc.gpsimd.memset(epsv[:], EPS).then_inc(cs("misc"), 1)
            nc.gpsimd.memset(xn2[:], 0.0).then_inc(cs("zeros"), 1)
            nc.gpsimd.iota(ebuf[:, 0, 0, :].bitcast(I32), pattern=[[-1, E]], base=E, channel_multiplier=0).then_inc(cs("misc"), 1)
            nc.gpsimd.iota(ebuf[:, 1, 0, :].bitcast(I32), pattern=[[CAP, E]], base=0, channel_multiplier=0).then_inc(cs("misc"), 1)
            pool.wait_ge(cs("misc"), 4)
            nc.gpsimd.tensor_copy(tie[:], ebuf[:, 0, 0, :].bitcast(I32)).then_inc(cs("misc"), 1)
            nc.gpsimd.tensor_copy(base[:], ebuf[:, 1, 0, :].bitcast(I32)).then_inc(cs("misc"), 1)
            pool.sem_inc(rt("sent"), 1)
            pool.sem_inc(moe("eo_free"), 2)
            rstd_pool(pool, 0, 0)
            layer0_pool(pool, 0, True, False)
            with pool.Fori(1, NG - 1) as i:
                layer0_pool(pool, i, False, False)
            layer0_pool(pool, NG - 1, False, True)
            rstd_pool(pool, 1, NG - 1)
            pool.wait_ge(rt("step"), ROUTE_STEPS * NG)
            for j in range(GB):
                for k in range(2):
                    scatter_pool(pool, NG - 1, j, k)
            scattered_pool(pool, NG - 1)
            with pool.Fori(0, E // 2) as i:
                for z in range(2):
                    pool.wait_ge(moe("y_out"), 2 * CT * i + CT * (z + 1) + 2)
                    nc.gpsimd.dma_start(eout.rearrange("(e t p) d -> e p t d", e=E, p=P)[bass.ds(2 * i + z, 1)].rearrange("e p t d -> p (e t) d"),
                                        eo[:, z]).then_inc(moe(f"stored{z}"), 16)
                    pool.wait_ge(moe(f"stored{z}"), 16 * i + 16)
                    pool.sem_inc(moe("eo_free"), 1)
            gathers_pool(pool, 0)
            rstd_pool(pool, 2, 0)
            with pool.Fori(0, NG - 1) as i:
                layer1_pool(pool, i, False)
            layer1_pool(pool, NG - 1, True)

        def turned_act(act, n, i, j, bank):
            act.wait_ge(nrm[n]("turned"), GB * i + j + 1)
            nc.scalar.activation(NBUF[n][5][:, :, j * S:(j + 1) * S],
                                 PS[:, bank, 0:D].rearrange("p (k m) -> p k m", k=DK), ACT.Copy).then_inc(nrm[n]("xT"), 1)

        def group_kv(act, layer, i):
            s = att[layer]
            nc.scalar.activation(kvag[:, :, DC:2 * DC], kv_r[:, bass.ds(GB * i, GB), :], ACT.Copy).then_inc(s("kvg"), 1)
            for half in range(2):
                h = slice(64 * half, 64 * half + 64)
                src = kvT[h, bass.ds(GB * i, GB), :]
                nc.scalar.activation(kvg[h, :, half, :], src, ACT.Copy).then_inc(s("kvg"), 1)
                nc.scalar.activation(kvgr[h, :, half, :], src, ACT.Copy).then_inc(s("kvg"), 1)

        def t_act(act, s, i, p, bank):
            act.wait_ge(s("t"), NP * i + p + 1)
            nc.scalar.activation(tT[:, p, :], PS[:, bank, :], ACT.Copy).then_inc(s("tT"), 1)
            nc.scalar.activation(tTr[:, p, :], PS[:, bank, :], ACT.Copy).then_inc(s("tT"), 1)

        def attend_act(act, layer, i, beside):
            s = att[layer]
            for k in range(1, NU + 2):
                n = k - 1
                if n < NU:
                    act.wait_ge(s("scoresT"), NU * i + n + 1)
                    if n >= 2:
                        act.wait_ge(s("pv"), NU * i + n - 1)
                    nc.scalar.activation(PT[:, n % 2], PS[:, 2 + n % 2, :].rearrange("p (h m) -> p h m", h=4),
                                         ACT.Exp).then_inc(s("probs"), 1)
                n = k - 2
                if 0 <= n < NU:
                    act.wait_ge(s("pv"), NU * i + n + 1)
                    if n >= 2:
                        act.wait_ge(s("ctx"), 2 * NU * i + 2 * n - 2)
                    bank = PS[:, 4 + n % 2, :].rearrange("p (a g m) -> p a g m", a=2, g=2)
                    for a in range(2):
                        own, other = slice(64 * a, 64 * a + 64), slice(64 - 64 * a, P - 64 * a)
                        nc.scalar.activation(sums[own, n % 2], bank[other, a], ACT.Copy).then_inc(s("sums"), 1)
                    act.wait_ge(s("sums"), 2 * NU * i + 2 * n + 2)
                    nc.scalar.activation(rinv[:, n % 2], sums[:, n % 2], ACT.Ln).then_inc(s("ln"), 1)
                    act.wait_ge(s("ln"), NU * i + n + 1)
                    nc.scalar.activation(rinv[:, n % 2], rinv[:, n % 2], ACT.Exp, scale=-1.0).then_inc(s("guess"), 1)
                beside(k)

        def fold0_act(act, p):
            z = 3 * (p % 2)
            act.wait_ge(fold[0]("product"), p + 1)
            for k in range(DK):
                src = PS[:, z + k, :]
                h0 = src[:, 0:DQ].rearrange("p (a q) -> p a q", a=2)
                h1 = src[:, DQ:2 * DQ].rearrange("p (a q) -> p a q", a=2)
                dst = A[:, k, p]
                nc.scalar.activation(dst[:, 0:2, 0:LO], h0, ACT.Copy)
                nc.scalar.activation(dst[:, 0:2, LO:P], h1[:, :, 0:P - LO], ACT.Copy)
                nc.scalar.activation(dst[:, 2, :].rearrange("p (a m) -> p a m", a=2), h1[:, :, P - LO:LO], ACT.Copy)
            nc.scalar.activation(MK[:, p].rearrange("p t m -> p (t m)"), PS[:, z + 2, 0:3 * P], ACT.Copy)
            nc.scalar.activation(U[:, p, :], PS[:, 7, 0:D], ACT.Copy, scale=tg[:, 0:1]).then_inc(fold[0]("out"), 1)

        def fold1_act(act, p):
            z = p % 2
            act.wait_ge(fold[1]("product"), p + 1)
            nc.scalar.activation(at[:, z, 0:2, :].rearrange("p t d -> p (t d)"), PS[:, 3 * z, :], ACT.Copy)
            nc.scalar.activation(at[:, z, 2, :], PS[:, 3 * z + 1, 0:D], ACT.Copy)
            nc.scalar.activation(mkst[:, z].rearrange("p t m -> p (t m)"), PS[:, 3 * z + 2, 0:3 * P], ACT.Copy)
            nc.scalar.activation(U[:, p, :], PS[:, 3 * z + 1, D:2 * D], ACT.Copy, scale=tg[:, 1:2]).then_inc(fold[1]("out"), 1)

        def fold1g_act(act, p):
            act.wait_ge(fold[1]("score_w"), p + 1)
            nc.scalar.activation(G[:, :, p, :], PS[:, 3 * (p % 2), 0:2 * P].rearrange("p (k m) -> p k m", k=DK),
                                 ACT.Copy).then_inc(fold[1]("g_out"), 1)

        def layer0_act(act, i, first, last):
            for p in range(NP + 1):
                if first and p + 1 < NP:
                    fold0_act(act, p + 1)
                if p >= 1:
                    t_act(act, qsem, i, p - 1, 6)
                if p == 1:
                    group_kv(act, 0, i)
                if not first and 2 <= p < 6:
                    turned_act(act, 1, i - 1, p - 2, 7)
                if not first and p == 7:
                    route_exp_act(act, i - 1)

            def beside(k):
                if not last and 8 <= k < 12:
                    turned_act(act, 0, i + 1, k - 8, 7)

            attend_act(act, 0, i, beside)

        def route_exp_act(act, i):
            act.wait_ge(rt("shifted"), i + 1)
            nc.scalar.activation(ebuf[:, 1], ebuf[:, 0], ACT.Exp).then_inc(rt("exp"), 1)

        def expert_turned_act(act, e, z):
            for t in range(CT):
                act.wait_ge(moe("turned"), CT * e + t + 1)
                nc.scalar.activation(dT[:, z, :, t * P:(t + 1) * P], PS[:, t % 2, 0:D].rearrange("p (k m) -> p k m", k=DK),
                                     ACT.Copy).then_inc(moe("dT"), 1)

        def expert_act(act, e, z, last):
            for f in range(FT):
                act.wait_ge(moe("h"), FT * e + f + 1)
                nc.scalar.activation(hT[:, f, :].rearrange("p (a c) -> p a c", a=2),
                                     PS[:, 2 + 2 * (f % 2):4 + 2 * (f % 2), 0:CAP // 2], ACT.Relu).then_inc(moe("relu"), 1)
            if not last:
                expert_turned_act(act, e + 1, 1 - z)

        def query1_act(act, i):
            for p in range(NP):
                t_act(act, q1sem, i, p, 7 - p % 2)
                if p == 0:
                    group_kv(act, 1, i)

        def layer1_act(act, i, last):
            def beside(k):
                if not last and 10 <= k < 14:
                    turned_act(act, 2, i + 1, k - 10, 7)

            attend_act(act, 1, i, beside)
            if not last:
                query1_act(act, i + 1)
            for j in range(GB):
                turned_act(act, 3, i, j, 2 + j)
            for f in range(DK):
                act.wait_ge(ff("up"), DK * i + f + 1)
                nc.scalar.activation(uT[:, f, :], PS[:, f, :], ACT.Relu).then_inc(ff("relu"), 1)
            act.wait_ge(ff("step"), 3 * i + 1)
            nc.scalar.activation(rsm[:, 9, :], rsm[:, 8, :], ACT.Exp).then_inc(ff("exp"), 1)

        @block.scalar
        def _(act):
            for b in range(B):
                act.wait_ge(kvs("turned"), b + 1)
                nc.scalar.activation(kvT[:, b, :], PS[:, b % 4, 0:P], ACT.Copy).then_inc(kvs("copied"), 1)
            for j in range(GB):
                turned_act(act, 0, 0, j, 4 + j)
            act.wait_ge(ld("gain"), 32)
            nc.scalar.activation(tg[:], gains[:], ACT.Tanh).then_inc(cs("tanh"), 1)
            act.wait_ge(cs("tanh"), 1)
            nc.scalar.preload_act_table_set("natural_log_exp_and_others")
            act.wait_ge(kvs("ones"), 3)
            act.wait_ge(kvs("copied"), B)
            fold0_act(act, 0)
            layer0_act(act, 0, True, False)
            with act.Fori(1, NG - 1) as i:
                layer0_act(act, i, False, False)
            layer0_act(act, NG - 1, False, True)
            for p in range(NP):
                fold1_act(act, p)
                if p == 1:
                    for j in range(GB):
                        turned_act(act, 1, NG - 1, j, 6 + j % 2)
                if p == 2:
                    route_exp_act(act, NG - 1)
                fold1g_act(act, p)
            expert_turned_act(act, 0, 0)
            with act.Fori(0, E // 2 - 1) as i:
                for z in range(2):
                    expert_act(act, 2 * i + z, z, False)
            for z in range(2):
                expert_act(act, E - 2 + z, z, z == 1)
            for j in range(GB):
                turned_act(act, 2, 0, j, 2 + j)
            query1_act(act, 0)
            with act.Fori(0, NG - 1) as i:
                layer1_act(act, i, False)
            layer1_act(act, NG - 1, True)

        def turn_pe(pe, n, i, j, bank, reused):
            s, src = nrm[n], NBUF[n][4]
            pe.wait_ge(s("normed"), GB * i + j + 1)
            if j >= reused:
                pe.wait_ge(s("xT"), GB * i + j + 1 - reused)
            for k in range(DK):
                mm = nc.tensor.transpose(PS[:, bank, k * P:(k + 1) * P], src[:, j, k * P:(k + 1) * P], ident[:])
            mm.then_inc(s("turned"), 1)

        def attend_pe(pe, layer, i, beside):
            s = att[layer]
            pe.wait_ge(s("kvg"), 5 * i + 5)
            for k in range(NU + 4):
                n = k
                if n < NU:
                    j, q = n // 4, n % 4
                    tok = slice(j * S, (j + 1) * S)
                    if n >= 2:
                        pe.wait_ge(s("negmax"), NU * i + n - 1)
                    for pp in range(2):
                        mm = nc.tensor.matmul(PS[:, n % 2, pp * 2 * P:(pp + 1) * 2 * P], tTr[:, 2 * q + pp, tok],
                                              kvgr[:, j].rearrange("p a m -> p (a m)"), start=True, stop=True)
                    mm.then_inc(s("scores"), 1)
                    if n >= 2:
                        pe.wait_ge(s("probs"), NU * i + n - 1)
                    bank = PS[:, 2 + n % 2, :].rearrange("p (g a m) -> p g a m", g=2, a=2)
                    for a in range(2):
                        nc.tensor.matmul(bank[:, :, a, :], kvg[:, j, a, :], tT[:, 2 * q:2 * q + 2, tok],
                                         start=(a == 0), stop=False, skip_group_check=True)
                n = k - 1
                if 0 <= n < NU:
                    pe.wait_ge(s("diag"), NU * i + n + 1)
                    nc.tensor.matmul(PS[:, 2 + n % 2, :], ones_r[:], diag[:, n % 2].rearrange("p h m -> p (h m)"),
                                     start=False, stop=True, skip_group_check=True).then_inc(s("scoresT"), 1)
                n = k - 2
                if 0 <= n < NU:
                    pe.wait_ge(s("probs"), NU * i + n + 1)
                    if n >= 2:
                        pe.wait_ge(s("ctx"), 2 * NU * i + 2 * n - 2)
                    probs = PT[:, n % 2].rearrange("p (g a) m -> p g a m", a=2)
                    for a in range(2):
                        mm = nc.tensor.matmul(PS[:, 4 + n % 2, a * 2 * P:(a + 1) * 2 * P], kvag[:, n // 4, DC - DC * a:3 * DC - DC * a],
                                              probs[:, :, a, :], start=True, stop=True)
                    mm.then_inc(s("pv"), 1)
                n = k - 4
                if 0 <= n < NU:
                    j, q = n // 4, n % 4
                    pe.wait_ge(s("ctx"), 2 * NU * i + 2 * n + 2)
                    if q == 0 and j >= 1:
                        pe.wait_ge(s("resid"), GB * i + j)
                    for g in range(2):
                        mm = nc.tensor.matmul(PS[:, 6, 0:D], cT[:, n % 2, g, :], U[:, 2 * q + g, :],
                                              start=(q == 0 and g == 0), stop=(q == 3 and g == 1))
                    mm.then_inc(s("unit"), 1)
                beside(k)

        def fold_mk_u(layer, p, mk_bank, u_out):
            _, _, wkv, wo, wqr, wkr = staged(layer, p % 2)
            for t in range(3):
                nc.tensor.matmul(PS[:, mk_bank, t * P:(t + 1) * P], wqr[:, t, :], wkr, start=True, stop=True)
            for h in range(2):
                mm = nc.tensor.matmul(u_out[64 * h:64 * h + 64, :], wkv[:, h, :], wo[:, h, :], start=True, stop=True)
            mm.then_inc(fold[layer]("product"), 1)

        def fold0_pe(pe, p):
            wq, cq = staged(0, p % 2)[0:2]
            pe.wait_ge(fold[0](f"staged{p % 2}"), 16 * (p // 2 + 1))
            if p >= 1:
                pe.wait_ge(fold[0]("out"), p)
            for k in range(DK):
                for h in range(2):
                    nc.tensor.matmul(PS[:, 3 * (p % 2) + k, h * DQ:(h + 1) * DQ], wq[:, h, k * P:(k + 1) * P], cq[:, h, :],
                                     start=True, stop=True)
            fold_mk_u(0, p, 3 * (p % 2) + 2, PS[:, 7, 0:D])

        def fold1_pe(pe, p):
            z = p % 2
            wq, cq = staged(1, z)[0:2]
            pe.wait_ge(fold[1](f"staged{z}"), 16 * (p // 2 + 1))
            if p >= 2:
                pe.wait_ge(fold[1]("g_out"), p - 1)
            c0, c1 = cq[:, 0, :], cq[:, 1, :]
            for t in range(2):
                bank = PS[:, 3 * z, t * D:(t + 1) * D]
                nc.tensor.matmul(bank[0:LO, :], c0[:, t * LO:(t + 1) * LO], wq[:, 0, :], start=True, stop=True)
                nc.tensor.matmul(bank[LO:P, :], c1[:, t * LO:t * LO + P - LO], wq[:, 1, :], start=True, stop=True)
            for t in range(2):
                nc.tensor.matmul(PS[64 * t:64 * t + 64, 3 * z + 1, 0:D], c1[:, t * LO + P - LO:(t + 1) * LO], wq[:, 1, :],
                                 start=True, stop=True)
            fold_mk_u(1, p, 3 * z + 2, PS[:, 3 * z + 1, D:2 * D])

        def fold1g_pe(pe, p):
            z = p % 2
            pe.wait_ge(fold[1]("out"), p + 1)
            for k in range(DK):
                for t in range(3):
                    mm = nc.tensor.matmul(PS[:, 3 * z, k * P:(k + 1) * P], at[:, z, t, k * P:(k + 1) * P], mkst[:, z, t, :],
                                          start=(t == 0), stop=(t == 2))
            mm.then_inc(fold[1]("score_w"), 1)

        def logits_pe(pe, n, i, w, done):
            pe.wait_ge(nrm[n]("xT"), GB * i + GB)
            src = NBUF[n][5]
            for j in range(GB):
                for k in range(DK):
                    mm = nc.tensor.matmul(PS[:, 7, j * E:(j + 1) * E], src[:, k, j * S:(j + 1) * S], w[:, k, :],
                                          start=(k == 0), stop=(k == DK - 1))
            mm.then_inc(done, 1)

        def place_pe(pe, i):
            pe.wait_ge(rt("step"), ROUTE_STEPS * i + MASK_STEP)
            nc.tensor.matmul(PS[:, 7, 0:GB * E], before[:], ebuf[:, 7].rearrange("p j e -> p (j e)"), start=True, stop=False)
            nc.tensor.matmul(PS[:, 7, 0:GB * E], ones[:], macc[:, 0:GB, :].rearrange("p j e -> p (j e)"),
                             start=False, stop=True).then_inc(rt("pos"), 1)

        def layer0_pe(pe, i, first, last):
            pe.wait_ge(nrm[0]("xT"), GB * i + GB)
            for p in range(NP + 1):
                if p < NP:
                    if p >= 2:
                        pe.wait_ge(qsem("cos"), 4 * NP * i + 4 * (p - 1))
                    if first:
                        pe.wait_ge(fold[0]("out"), p + 1)
                    for t in range(3):
                        for k in range(DK):
                            mm = nc.tensor.matmul(PS[:, 3 * (p % 2) + t, :], A[:, k, p, t, :], xT[:, k, :],
                                                  start=(k == 0), stop=(k == DK - 1))
                    mm.then_inc(qsem("q"), 1)
                if first and p + 1 < NP:
                    if p >= 1:
                        pe.wait_ge(qsem("cos"), 4 * p)
                    fold0_pe(pe, p + 1)
                if not first and 2 <= p < 6:
                    turn_pe(pe, 1, i - 1, p - 2, 7, 1)
                if not first and p == 6:
                    logits_pe(pe, 1, i - 1, wg0, rt("logits"))
                if p >= 1:
                    o = p - 1
                    pe.wait_ge(qsem("add"), 3 * NP * i + 3 * o + 3)
                    if o >= 1:
                        pe.wait_ge(qsem("tT"), 2 * NP * i + 2 * o)
                    for t in range(3):
                        mm = nc.tensor.matmul(PS[:, 6, :], MK[:, o, t, :], qr[:, o % 2, t, :],
                                              start=(t == 0), stop=(t == 2))
                    mm.then_inc(qsem("t"), 1)
            pe.wait_ge(qsem("tT"), 2 * NP * i + 2 * NP)

            def beside(k):
                if not first and k == 1:
                    place_pe(pe, i - 1)
                if not last and 8 <= k < 12:
                    turn_pe(pe, 0, i + 1, k - 8, 7, 1)

            attend_pe(pe, 0, i, beside)

        def expert_turn_pe(pe, e, z, rows):
            pe.wait_ge(moe(f"rows{z}"), rows)
            for t in range(CT):
                if t >= 2:
                    pe.wait_ge(moe("dT"), CT * e + t - 1)
                for k in range(DK):
                    mm = nc.tensor.transpose(PS[:, t % 2, k * P:(k + 1) * P], dx[:, z, t, k * P:(k + 1) * P], ident[:])
                mm.then_inc(moe("turned"), 1)

        def expert_pe(pe, i, z, last):
            e = 2 * i + z
            pe.wait_ge(moe("dT"), CT * e + CT)
            pe.wait_ge(moe(f"weights{z}"), 32 * i + 32)
            for f in range(FT):
                if f >= 2:
                    pe.wait_ge(moe("relu"), FT * e + f - 1)
                for c in range(2):
                    for k in range(DK):
                        mm = nc.tensor.matmul(PS[:, 2 + 2 * (f % 2) + c, 0:CAP // 2], w1[:, z, k, f * P:(f + 1) * P],
                                              dT[:, z, k, c * (CAP // 2):(c + 1) * (CAP // 2)],
                                              start=(k == 0), stop=(k == DK - 1))
                mm.then_inc(moe("h"), 1)
            if not last:
                expert_turn_pe(pe, e + 1, 1 - z, 16 * (i + z) + 16)
            pe.wait_ge(moe("relu"), FT * e + FT)
            for t in range(CT):
                pe.wait_ge(moe("y_out"), CT * e + t + 1)
                for f in range(FT):
                    mm = nc.tensor.matmul(PS[:, 6 + (z * CT + t) % 2, 0:D], hT[:, f, t * P:(t + 1) * P], w2[:, z, f, :],
                                          start=(f == 0), stop=(f == FT - 1))
                mm.then_inc(moe("y"), 1)

        def query1_pe(pe, i, first):
            pe.wait_ge(nrm[2]("xT"), GB * i + GB)
            for p in range(NP):
                if p >= 2:
                    pe.wait_ge(q1sem("tT"), 2 * NP * i + 2 * (p - 1))
                if p == 1 and not first:
                    pe.wait_ge(att[1]("resid"), GB * i)
                for k in range(DK):
                    mm = nc.tensor.matmul(PS[:, 7 - p % 2, :], G[:, k, p, :], xT[:, k, :], start=(k == 0), stop=(k == DK - 1))
                mm.then_inc(q1sem("t"), 1)
            pe.wait_ge(q1sem("tT"), 2 * NP * i + 2 * NP)

        def layer1_pe(pe, i, last):
            def beside(k):
                if not last and 10 <= k < 14:
                    turn_pe(pe, 2, i + 1, k - 10, 7, 1)

            attend_pe(pe, 1, i, beside)
            if not last:
                query1_pe(pe, i + 1, False)
            for j in range(GB):
                turn_pe(pe, 3, i, j, 2 + j, GB)
            logits_pe(pe, 3, i, wg1, ff("logits"))
            for f in range(DK):
                for k in range(DK):
                    mm = nc.tensor.matmul(PS[:, f, :], wf[:, 0, k, f * P:(f + 1) * P], xT2[:, k, :],
                                          start=(k == 0), stop=(k == DK - 1))
                mm.then_inc(ff("up"), 1)
            for j in range(GB):
                for k in range(DK):
                    nc.tensor.matmul(PS[:, 2 + j, D:2 * D], xT2[:, k, j * S:(j + 1) * S], wf[:, 2, k, :],
                                     start=(k == 0), stop=(k == DK - 1))
            pe.wait_ge(ff("relu"), DK * i + DK)
            for j in range(GB):
                for k in range(DK):
                    mm = nc.tensor.matmul(PS[:, 2 + j, 0:D], uT[:, k, j * S:(j + 1) * S], wf[:, 1, k, :],
                                          start=(k == 0), stop=(k == DK - 1))
                mm.then_inc(ff("y"), 1)
            pe.wait_ge(ff("added"), 2 * GB * i + 2 * GB)

        @block.tensor
        def _(pe):
            pe.sem_inc(moe("y"), 2 * CT)
            pe.wait_ge(cs("ident"), 4)
            pe.wait_ge(kvs("rope"), 2)
            for b in range(B):
                if b >= 4:
                    pe.wait_ge(kvs("copied"), b - 3)
                nc.tensor.transpose(PS[:, b % 4, 0:P], kv_dup[:, b, :], ident[:]).then_inc(kvs("turned"), 1)
            for j in range(GB):
                turn_pe(pe, 0, 0, j, 4 + j, GB)
            pe.wait_ge(nrm[0]("xT"), GB)
            fold0_pe(pe, 0)
            pe.wait_ge(cs("ones"), 2)
            layer0_pe(pe, 0, True, False)
            pe.wait_ge(ld("router"), 32)
            with pe.Fori(1, NG - 1) as i:
                layer0_pe(pe, i, False, False)
            layer0_pe(pe, NG - 1, False, True)
            for p in range(NP):
                fold1_pe(pe, p)
                if p == 1:
                    for j in range(GB):
                        turn_pe(pe, 1, NG - 1, j, 6 + j % 2, 2)
                    logits_pe(pe, 1, NG - 1, wg0, rt("logits"))
                if p == 4:
                    place_pe(pe, NG - 1)
                fold1g_pe(pe, p)
            pe.wait_ge(fold[1]("g_out"), NP)
            expert_turn_pe(pe, 0, 0, 16)
            with pe.Fori(0, E // 2 - 1) as i:
                for z in range(2):
                    expert_pe(pe, i, z, False)
            for z in range(2):
                expert_pe(pe, E // 2 - 1, z, z == 1)
            for j in range(GB):
                turn_pe(pe, 2, 0, j, 2 + j, GB)
            query1_pe(pe, 0, True)
            pe.wait_ge(ld("ffn"), 48)
            pe.wait_ge(ff("w_down"), 1)
            with pe.Fori(0, NG - 1) as i:
                layer1_pe(pe, i, False)
            layer1_pe(pe, NG - 1, True)

        def batch(b):
            return x[:, bass.ds(b, 1), :].rearrange("p b d -> p (b d)")

        def stats_dve(dve, n, i):
            s, (stats_, mv_, _, _, _, _) = nrm[n], NBUF[n]
            gate_dve()
            for j in range(GB):
                nc.vector.bn_stats(stats_[:, j, :], batch(GB * i + j)).then_inc(s("stats"), 1)
            dve.wait_ge(s("stats"), GB * i + GB)
            gate_dve()
            for j in range(GB):
                nc.vector.bn_aggr(mv_[:, j, :], stats_[:, j, :]).then_inc(s("mean"), 1)

        def normed_dve(dve, n, i):
            s, (_, mv_, _, rstd_, dst, _) = nrm[n], NBUF[n]
            dve.wait_ge(s("rstd"), i + 1)
            for j in range(GB):
                nc.vector.tensor_scalar(dst[:, j, :], batch(GB * i + j), mv_[:, j, 0:1], rstd_[:, j:j + 1],
                                        ALU.subtract, ALU.mult).then_inc(s("normed"), 1)

        def attend_dve(dve, layer, i, beside):
            s = att[layer]
            for k in range(NU + 5):
                n = k
                if n < NU:
                    dve.wait_ge(s("scores"), NU * i + n + 1)
                    nc.vector.tensor_reduce(negm[:, n % 2, :], PS[:, n % 2, :].rearrange("p (h m) -> p h m", h=4),
                                            AX.X, ALU.max, negate=True).then_inc(s("negmax"), 1)
                    dve.wait_ge(s("negmax"), NU * i + n + 1)
                    if n >= 2:
                        dve.wait_ge(s("scoresT"), NU * i + n - 1)
                    nc.vector.tensor_tensor(diag[:, n % 2], ident[:].unsqueeze(1).to_broadcast([P, 4, P]),
                                            negm[:, n % 2, :].unsqueeze(2).to_broadcast([P, 4, P]),
                                            ALU.mult).then_inc(s("diag"), 1)
                n = k - 3
                if 0 <= n < NU:
                    bank = PS[:, 4 + n % 2, :].rearrange("p (a g m) -> p a g m", a=2, g=2)
                    dve.wait_ge(s("near1"), NU * i + n + 1)
                    flat = "p g m -> p (g m)"
                    nc.vector.scalar_tensor_tensor(out=rinv[:, n % 2].rearrange(flat), in0=sums[:, n % 2].rearrange(flat), scalar=-2.0,
                                                   in1=rinv[:, n % 2].rearrange(flat), op0=ALU.add, op1=ALU.mult).then_inc(s("rinv"), 1)
                    dve.wait_ge(s("rinv"), NU * i + n + 1)
                    if n >= 2:
                        dve.wait_ge(s("unit"), NU * i + n - 1)
                    for a in range(2):
                        own = slice(64 * a, 64 * a + 64)
                        nc.vector.scalar_tensor_tensor(out=cT[own, n % 2].rearrange(flat), in0=bank[own, a].rearrange(flat), scalar=-1.0,
                                                       in1=rinv[own, n % 2].rearrange(flat), op0=ALU.mult, op1=ALU.mult).then_inc(s("ctx"), 1)
                n = k - 5
                if 0 <= n < NU and n % 4 == 3:
                    j = n // 4
                    dve.wait_ge(s("unit"), NU * i + n + 1)
                    nc.vector.tensor_tensor(batch(GB * i + j), PS[:, 6, 0:D], batch(GB * i + j), ALU.add).then_inc(s("resid"), 1)
                beside(k)
            dve.wait_ge(s("resid"), GB * i + GB)

        def wide(a):
            return a.unsqueeze(2).to_broadcast([P, GB, E])

        def choose_dve(dve, i, part_):
            V = nc.vector
            count = [0, 1, 21][part_]

            def step(ins):
                nonlocal count
                count += 1
                ins.then_inc(rt("step"), 1)
                dve.wait_ge(rt("step"), ROUTE_STEPS * i + count)

            if part_ == 0:
                logits = PS[:, 7, 0:GB * E].rearrange("p (j e) -> p j e", j=GB)
                dve.wait_ge(rt("logits"), i + 1)
                step(V.tensor_reduce(rsm[:, 0, :], logits, AX.X, ALU.max))
                V.tensor_tensor(ebuf[:, 0], logits, wide(rsm[:, 0, :]), ALU.subtract).then_inc(rt("shifted"), 1)
            if part_ == 1:
                dve.wait_ge(rt("exp"), i + 1)
                step(V.tensor_reduce(rsm[:, 1, :], ebuf[:, 1], AX.X, ALU.add))
                step(V.reciprocal(rsm[:, 2, :], rsm[:, 1, :]))
                step(V.tensor_tensor(ebuf[:, 2], ebuf[:, 1], wide(rsm[:, 2, :]), ALU.mult))
                probs = ebuf[:, 2]
                for k in range(2):
                    step(V.tensor_reduce(gates[:, k, :], probs, AX.X, ALU.max))
                    step(V.tensor_tensor(ebuf[:, 3], probs, wide(gates[:, k, :]), ALU.is_equal))
                    step(V.tensor_tensor(ebuf[:, 4], ebuf[:, 3], tie[:].unsqueeze(1).to_broadcast([P, GB, E]), ALU.mult))
                    step(V.tensor_reduce(rsm[:, 3, :], ebuf[:, 4], AX.X, ALU.max))
                    step(V.tensor_tensor(oh[:, k], ebuf[:, 4], wide(rsm[:, 3, :]), ALU.is_equal))
                    if k == 0:
                        step(V.scalar_tensor_tensor(out=ebuf[:, 5].rearrange("p j e -> p (j e)"),
                                                    in0=oh[:, 0].rearrange("p j e -> p (j e)"), scalar=-2.0,
                                                    in1=ebuf[:, 2].rearrange("p j e -> p (j e)"), op0=ALU.mult, op1=ALU.add))
                        probs = ebuf[:, 5]
                step(V.tensor_tensor(ebuf[:, 7], oh[:, 0], oh[:, 1], ALU.add))
                step(V.tensor_copy(macc[:, 0, :], macc[:, GB, :]))
                for j in range(GB):
                    step(V.tensor_tensor(macc[:, j + 1, :], macc[:, j, :], ebuf[:, 7, j, :], ALU.add))
                assert count == MASK_STEP, count
            if part_ == 2:
                dve.wait_ge(rt("pos"), i + 1)
                pos = PS[:, 7, 0:GB * E].rearrange("p (j e) -> p j e", j=GB)
                step(V.tensor_scalar(ebuf[:, 8], pos, float(CAP), None, ALU.is_lt))
                step(V.tensor_tensor(ebuf[:, 9], pos, base[:].unsqueeze(1).to_broadcast([P, GB, E]), ALU.add))
                for k in range(2):
                    step(V.tensor_tensor(sel[:, k], oh[:, k], ebuf[:, 8], ALU.mult))
                step(V.tensor_reduce(keep[:], sel[:], AX.X, ALU.add))
                for k in range(2):
                    step(V.tensor_tensor(sel[:, k], oh[:, k], ebuf[:, 9], ALU.mult))
                step(V.tensor_reduce(slot[:], sel[:], AX.X, ALU.add))
                r = rsm[:, 4:6, :]
                step(V.tensor_scalar(r, keep[:], -DROPPED, DROPPED, ALU.mult, ALU.add))
                step(V.tensor_tensor(sidx[:].rearrange("p j k -> p k j"), r, slot[:], ALU.add))
                step(V.tensor_tensor(gidx[:, bass.ds(GB * i, GB), :].rearrange("p j k -> p k j"), slot[:], keep[:], ALU.mult))
                step(V.tensor_tensor(rsm[:, 6:8, :], gates[:], keep[:], ALU.mult))
                step(V.tensor_scalar(gw[:, bass.ds(GB * i, GB), :].rearrange("p j k -> p k j"), rsm[:, 6:8, :], tg[:, 2:3],
                                     None, ALU.mult))
                assert count == ROUTE_STEPS, count

        def rope_dve(dve, i, p):
            V, z = nc.vector, p % 2
            dve.wait_ge(qsem("q"), NP * i + p + 1)
            if p >= 2:
                dve.wait_ge(qsem("add"), 3 * NP * i + 3 * (p - 1))
            q = PS[:, 3 * z:3 * z + 3, :].rearrange("p t (j s) -> p t j s", j=GB)
            c_ = qc[:, z].rearrange("p t (j s) -> p t j s", j=GB)
            s_ = qs[:, z].rearrange("p t (j s) -> p t j s", j=GB)
            V.tensor_tensor(c_, q, cosq[:].unsqueeze(2).to_broadcast([P, 3, GB, S]), ALU.mult).then_inc(qsem("cos"), 1)
            V.tensor_tensor(s_[:, 0:2], q[:, 0:2], sinq[:, 0:2].unsqueeze(2).to_broadcast([P, 2, GB, S]), ALU.mult).then_inc(qsem("cos"), 1)
            for a in range(2):
                src, dst = slice(64 * a, 64 * a + 64), slice(64 - 64 * a, P - 64 * a)
                V.tensor_tensor(s_[dst, 2], q[src, 2], sinq[src, 2, :].unsqueeze(1).to_broadcast([64, GB, S]),
                                ALU.mult).then_inc(qsem("cos"), 1)

        def ffn_norm_dve(dve, i, part_):
            if part_ == 0:
                stats_dve(dve, 1, i)
            else:
                dve.wait_ge(rt("sent"), i + 1)
                normed_dve(dve, 1, i)

        def layer0_dve(dve, i, first, last):
            for p in range(NP):
                rope_dve(dve, i, p)
                if not first:
                    if p < 2:
                        ffn_norm_dve(dve, i - 1, p)
                    if p == 6:
                        choose_dve(dve, i - 1, 0)
                    if p == 7:
                        choose_dve(dve, i - 1, 1)

            def beside(k):
                if not first and k == 2:
                    choose_dve(dve, i - 1, 2)
                if first and k == 3:
                    dve.wait_ge(ld("x"), 16)
                if not last and k == 3:
                    stats_dve(dve, 0, i + 1)
                if not last and k == 6:
                    normed_dve(dve, 0, i + 1)

            attend_dve(dve, 0, i, beside)

        def combine_dve(dve, i, j):
            dve.wait_ge(cb(f"gathered{j}"), 32 * i + 32)
            for k in range(2):
                b = GB * i + j
                if k == 1:
                    dve.wait_ge(cb("added"), 2 * b + 2)
                nc.vector.scalar_tensor_tensor(out=batch(b), in0=grow[:, j, k, :], scalar=gw[:, bass.ds(b, 1), k], in1=batch(b),
                                               op0=ALU.mult, op1=ALU.add).then_inc(cb("added"), 1)

        def layer1_dve(dve, i, last):
            V = nc.vector

            def beside(k):
                if not last and 2 <= k < 6:
                    combine_dve(dve, i + 1, k - 2)
                if not last and k == 6:
                    dve.wait_ge(cb("added"), 2 * GB * i + 4 * GB + 1)
                    stats_dve(dve, 2, i + 1)
                if not last and k == 8:
                    normed_dve(dve, 2, i + 1)

            attend_dve(dve, 1, i, beside)
            stats_dve(dve, 3, i)
            normed_dve(dve, 3, i)
            dve.wait_ge(ff("logits"), i + 1)
            gate_dve()
            for j in range(GB):
                V.max(top8[:, j, :], PS[:, 7, j * E:(j + 1) * E]).then_inc(ff("rw"), 1)
            dve.wait_ge(ff("rw"), 8 * i + 4)
            V.tensor_tensor(rsm[:, 8, :], top8[:, :, 1], top8[:, :, 0], ALU.subtract).then_inc(ff("step"), 1)
            dve.wait_ge(ff("exp"), i + 1)
            V.tensor_scalar(rsm[:, 10, :], rsm[:, 9, :], 1.0, None, ALU.add).then_inc(ff("step"), 1)
            dve.wait_ge(ff("step"), 3 * i + 2)
            V.reciprocal(rsm[:, 11, :], rsm[:, 10, :]).then_inc(ff("step"), 1)
            dve.wait_ge(ff("step"), 3 * i + 3)
            V.tensor_tensor(rsm[:, 12, :], rsm[:, 9, :], rsm[:, 11, :], ALU.mult).then_inc(ff("rw"), 1)
            dve.wait_ge(ff("rw"), 8 * i + 5)
            V.tensor_tensor(rsm[:, 13, :], rsm[:, 12, :], rsm[:, 11, :], ALU.add).then_inc(ff("rw"), 1)
            dve.wait_ge(ff("rw"), 8 * i + 6)
            V.tensor_scalar(rsm[:, 14, :], rsm[:, 13, :], tg[:, 3:4], None, ALU.mult).then_inc(ff("rw"), 2)
            dve.wait_ge(ff("rw"), 8 * i + 8)
            for j in range(GB):
                b = GB * i + j
                dve.wait_ge(ff("y"), b + 1)
                V.tensor_tensor(batch(b), PS[:, 2 + j, 0:D], batch(b), ALU.add).then_inc(ff("added"), 1)
                dve.wait_ge(ff("added"), 2 * b + 1)
                V.scalar_tensor_tensor(out=batch(b), in0=PS[:, 2 + j, D:2 * D], scalar=rsm[:, 14, j:j + 1], in1=batch(b),
                                       op0=ALU.mult, op1=ALU.add).then_inc(ff("added"), 1)

        @block.vector
        def _(dve):
            V = nc.vector
            dve.wait_ge(ld("kv"), 32)
            V.tensor_tensor(kv_cos, kv_raw, kv_tab[:, 0, :].unsqueeze(1).to_broadcast([P, B, DC]), ALU.mult).then_inc(kvs("cos"), 1)
            for a in range(2):
                o, s_ = slice(32 * a, 32 * a + 32), slice(32 - 32 * a, 64 - 32 * a)
                V.tensor_tensor(kv_sin[:, :, o], kv_raw[:, :, s_], kv_tab[:, 1, o].unsqueeze(1).to_broadcast([P, B, 32]),
                                ALU.mult).then_inc(kvs("sin"), 1)
            dve.wait_ge(kvs("cos"), 1)
            dve.wait_ge(kvs("sin"), 2)
            V.tensor_tensor(kv_dup.rearrange("p b (a c) -> p b a c", a=2), kv_cos.unsqueeze(2).to_broadcast([P, B, 2, DC]),
                            kv_sin.unsqueeze(2).to_broadcast([P, B, 2, DC]), ALU.add).then_inc(kvs("rope"), 1)
            V.tensor_tensor(kv_r[:], kv_cos, kv_sin, ALU.add).then_inc(kvs("rope"), 1)
            dve.wait_ge(ld("x0"), 16)
            stats_dve(dve, 0, 0)
            normed_dve(dve, 0, 0)
            V.memset(kvg[:], 0.0).then_inc(kvs("ones"), 1)
            V.memset(kvgr[:].bitcast(F32), 0.0).then_inc(kvs("ones"), 1)
            V.memset(kvag[:], 1.0).then_inc(kvs("ones"), 1)
            V.memset(macc[:], 0.0).then_inc(rt("carry"), 1)
            dve.sem_inc(moe("y_out"), 2)
            dve.sem_inc(cb("added"), 1)
            dve.wait_ge(cs("ones"), 1)
            V.tensor_copy(ones_r[:], ones[:]).then_inc(cs("ones"), 1)
            dve.wait_ge(ld("tab"), 32)
            layer0_dve(dve, 0, True, False)
            dve.wait_ge(cs("misc"), 6)
            dve.wait_ge(ld("zero"), 16 * (E * CAP // (GB * P)))
            with dve.Fori(1, NG - 1) as i:
                layer0_dve(dve, i, False, False)
            layer0_dve(dve, NG - 1, False, True)
            for part_ in range(2):
                ffn_norm_dve(dve, NG - 1, part_)
            for part_ in range(3):
                choose_dve(dve, NG - 1, part_)
            dve.wait_ge(ld("ffn"), 48)
            V.tensor_scalar(wf[:, 1], wf[:, 1], tg[:, 3:4], None, ALU.mult).then_inc(ff("w_down"), 1)
            with dve.Fori(0, E // 2) as i:
                for z in range(2):
                    e = 2 * i + z
                    dve.wait_ge(moe("eo_free"), e + 1)
                    for t in range(CT):
                        dve.wait_ge(moe("y"), CT * e + 2 * CT + t + 1)
                        V.tensor_copy(eo[:, z, t, :], PS[:, 6 + (z * CT + t) % 2, 0:D]).then_inc(moe("y_out"), 1)
            for j in range(GB):
                combine_dve(dve, 0, j)
            dve.wait_ge(cb("added"), 2 * GB + 1)
            stats_dve(dve, 2, 0)
            normed_dve(dve, 2, 0)
            with dve.Fori(0, NG - 1) as i:
                layer1_dve(dve, i, False)
            layer1_dve(dve, NG - 1, True)


def rope_tables(length, dim):
    inv = (np.float32(1.0) / np.float32(10000.0) ** (np.arange(0, dim, 2, dtype=np.float32) / np.float32(dim))).astype(np.float32)
    f = np.arange(length, dtype=np.float32)[:, None] * inv[None, :]
    return np.repeat(np.sin(f), 2, axis=-1), np.repeat(np.cos(f), 2, axis=-1)


def query_tables():
    sin, cos = rope_tables(S, DQ)
    r = np.arange(P)
    q = np.stack([np.where(r < LO, r, r - LO), np.where(r < LO, r, r - LO) + LO,
                  np.where(r < 64, P - LO + r, P + r - 64)], axis=1)
    partner = np.where(q >= LO, q - LO, q + LO)
    sign = np.where(q >= LO, -1.0, 1.0).astype(np.float32)
    return (np.ascontiguousarray(cos.T[q], np.float32),
            np.ascontiguousarray(sin.T[partner] * sign[:, :, None], np.float32))


def context_table():
    sin, cos = rope_tables(S, DC)
    sign = np.where(np.arange(DC) < DC // 2, -1.0, 1.0).astype(np.float32)
    return np.ascontiguousarray(np.stack([cos, sin * sign], axis=1), np.float32)


def pack_pairs(wq, cq, ckv, wo, wqr, wkr):
    by_pair = lambda a: a.reshape(NP, 2, KH, -1).transpose(2, 0, 1, 3).reshape(KH, NP, -1)
    qrT = wqr.transpose(2, 0, 1).reshape(64, NP, 2, 2, LO)
    qr = np.zeros((P, NP, 3, P), wqr.dtype)
    qr[0:64, :, 0:2, 0:LO] = qrT[:, :, 0]
    qr[64:P, :, 0:2, LO:P] = qrT[:, :, 1, :, 0:P - LO]
    qr[64:P, :, 2] = qrT[:, :, 1, :, P - LO:LO].reshape(64, NP, P)
    krT = wkr.transpose(2, 0, 1).reshape(64, NP, 2, DC)
    kr = np.zeros((P, NP, 2, DC), wkr.dtype)
    kr[0:64, :, 0] = krT[:, :, 0]
    kr[64:P, :, 1] = krT[:, :, 1]
    return np.concatenate([by_pair(wq), by_pair(cq), by_pair(ckv), by_pair(wo.T),
                           qr.reshape(P, NP, -1), kr.reshape(P, NP, -1)], axis=2)


def kernel(**inputs):
    import concourse.bacc as bacc
    from concourse.bass_utils import run_bass_kernel_spmd

    nc = bacc.Bacc("TRN2", target_bir_lowering=False, num_devices=1)
    arrays = {}

    def give(name, a):
        a = np.ascontiguousarray(a)
        arrays["in_" + name] = a
        return nc.dram_tensor("in_" + name, a.shape, mybir.dt.from_np(a.dtype), kind="ExternalInput").ap()

    def raw(name):
        return np.asarray(inputs[name])

    cosq, sinq = query_tables()
    io = {
        "x": give("x", raw("x")).rearrange("b s d -> s b d"),
        "ctx": give("ctx", raw("ctx_512")).rearrange("b l c -> l b c"),
        "g_xattn": give("g_xattn", raw("g_xattn").reshape(1, 2)).to_broadcast([P, 2]),
        "g_ffn": give("g_ffn", raw("g_ffn").reshape(1, 2)).to_broadcast([P, 2]),
        "cosq": give("cosq", cosq),
        "sinq": give("sinq", sinq),
        "kv_tab": give("kv_tab", context_table()),
        "wg0": give("wg0", raw("L0_ffn_Wg")).rearrange("(k p) e -> p k e", p=P),
        "w1": give("w1", raw("L0_ffn_w1")),
        "w2": give("w2", raw("L0_ffn_w2")),
        "wg1": give("wg1", raw("L1_ffn_W_gate").T).rearrange("(k p) e -> p k e", p=P),
        "w_up": give("w_up", raw("L1_ffn_W_up").T).rearrange("(k p) e -> p k e", p=P),
        "w_dn": give("w_dn", raw("L1_ffn_W_down").T).rearrange("(k p) e -> p k e", p=P),
        "w_ex": give("w_ex", raw("L1_ffn_W_expert")).rearrange("(k p) e -> p k e", p=P),
    }
    for n in LAYERS:
        io[n] = give(f"pairs{n}", pack_pairs(*(raw(f"L{n}_xattn_{w}") for w in ("Wq", "w_kc_q", "w_kc_kv", "Wo", "W_qr", "W_kr"))))
    out = nc.dram_tensor("out", (B, S, D), F32, kind="ExternalOutput").ap()
    io["out"] = out.rearrange("b s d -> s b d")
    build(nc, io)
    done = run_bass_kernel_spmd(nc, [arrays], core_ids=[0])
    return done.results[0]["out"]
```

```python
from contextlib import ExitStack

import numpy as np

import concourse.bass as bass
from concourse import mybir

F32 = mybir.dt.float32
F32R = mybir.dt.float32r
I32 = mybir.dt.int32
ALU = mybir.AluOpType
ACT = mybir.ActivationFunctionType
AX = mybir.AxisListType

P = 128
B, S, D = 16, 128, 256
H, KH, DC, DQ = 16, 128, 64, 192
LO = DQ // 2
NP = H // 2
DK = D // P
GB = 4
NG = B // GB
TG = GB * S
NU = GB * H // 4
E, FF = 8, 1024
CAP = int(np.ceil(1.25 * B * S * 2 / E))
CT = CAP // P
SPLIT = CAP - P
FT = FF // P
DROPPED = 1.0e5
EPS = 1e-5

LAYERS = (0, 1)
LATE = 3
PACK = (("wq", 2 * D), ("cq", 2 * DQ), ("kv", 2 * DC), ("wo", 2 * D), ("qr", 3 * P), ("kr", P))
PACKED = sum(n for _, n in PACK)
FIRST = PACK[0][1] + PACK[1][1]


def build(nc, io):
    with ExitStack() as ctx:
        def sb(name, shape, dt=F32):
            return ctx.enter_context(nc.sbuf_tensor(name, shape, dt))

        def sem(name):
            return ctx.enter_context(nc.semaphore(name))

        class Sems:

            def __init__(self, stage, signals):
                self.of = {s: sem(f"{stage}_{s}") for s in signals.split()}

            def __call__(self, s):
                return self.of[s]

        PS = ctx.enter_context(nc.psum_tensor("PS", [P, 8, 512], F32))
        disp = nc.dram_tensor("disp_rows", (E * CAP, D), F32, kind="Internal").ap()
        eout = nc.dram_tensor("expert_rows", (E * CAP, D), F32, kind="Internal").ap()

        x = sb("x_res", [P, B, D])
        kv_r = sb("kv_roped", [P, B, DC])
        kvT = sb("kvT", [P, B, P])
        U = sb("U_out", [P, NP, D])
        tS = sb("score_rows", [P, H, TG], F32R)
        xn = sb("x_norm", [P, GB, D])
        ffn = sb("ffn_rows", [P, 2 * TG * DK])
        xn2 = ffn[:, 0:GB * D].rearrange("p (j d) -> p j d", j=GB)
        xT2 = ffn[:, GB * D:GB * D + DK * TG].rearrange("p (k t) -> p k t", k=DK)
        xT = sb("xT", [P, DK, TG])
        tTr = sb("tT_round", [P, NP, TG], F32R)
        kvgr = sb("kv_group_round", [P, GB, 2, P], F32R)
        kvh = sb("kv_group_high", [P, GB, P], F32R)
        kvl = sb("kv_group_low", [P, GB, P], F32R)
        kvag = sb("kv_group_ones", [P, GB, 3 * DC])
        diag = sb("diag", [P, 2, 4, P], F32R)
        work = sb("attention_rows", [P, 2 * CT * D])
        PT = work[:, 0:8 * P].rearrange("p (z h m) -> p z h m", z=2, h=4)
        cT = work[:, 8 * P:12 * P].rearrange("p (z g m) -> p z g m", z=2, g=2)
        sums = work[:, 12 * P:16 * P].rearrange("p (z g m) -> p z g m", z=2, g=2)
        rinv = work[:, 16 * P:20 * P].rearrange("p (z g m) -> p z g m", z=2, g=2)
        ident = sb("ident", [P, P])
        before = sb("before", [P, P])
        ones = sb("ones", [P, P])
        ones_r = sb("ones_round", [P, P], F32R)
        epsv = sb("eps", [P, GB])
        scrap_p = sb("scrap_pool", [P, 1])
        scrap = sb("scrap", [P, 1])
        mhalf = sb("minus_half", [P, GB])
        cosq = sb("cosq", [P, 3, S])
        sinq = sb("sinq", [P, 3, S])
        kv_tab = sb("kv_tab", [P, 2, DC])
        gains = sb("gains", [P, 4])
        tg = sb("tanh_gains", [P, 4])
        wg0 = sb("wg0", [P, DK, E])
        stats = sb("stats", [P, GB, 6])
        mv = sb("mean_var", [P, GB, 2])
        veps = sb("var_eps", [P, GB])
        rstd = sb("rstd", [P, GB])
        stats2 = sb("stats_ffn", [P, GB, 6])
        mv2 = sb("mean_var_ffn", [P, GB, 2])
        veps2 = sb("var_eps_ffn", [P, GB])
        rstd2 = sb("rstd_ffn", [P, GB])
        negm = sb("neg_max", [P, 2, 4])
        tie = sb("tie_order", [P, E])
        base = sb("slot_base", [P, E])
        ebuf = sb("route_tmp", [P, 10, GB, E])
        oh = sb("chosen", [P, 2, GB, E])
        sel = sb("chosen_value", [P, 2, GB, E])
        macc = sb("chosen_before", [P, GB + 1, E])
        rsm = sb("route_small", [P, 16, GB])
        keep = sb("keep", [P, 2, GB])
        slot = sb("slot", [P, 2, GB])
        gates = sb("gates", [P, 2, GB])
        sidx = sb("scatter_idx", [P, GB, 2], I32)
        gidx = sb("gather_idx", [P, B, 2], I32)
        gw = sb("gate_weight", [P, B, 2])
        top8 = sb("top8", [P, GB, E])

        arena = sb("arena", [P, 72 * 256])

        def area(kib, n):
            return arena[:, kib * 256:kib * 256 + n]

        A = area(0, DK * NP * 3 * P).rearrange("p (k n t m) -> p k n t m", k=DK, n=NP, t=3)
        MK = area(24, NP * 3 * P).rearrange("p (n t m) -> p n t m", n=NP, t=3)
        qc = area(36, 2 * 3 * TG).rearrange("p (z t n) -> p z t n", z=2, t=3)
        qs = area(48, 2 * 3 * TG).rearrange("p (z t n) -> p z t n", z=2, t=3)
        qr = area(60, 2 * 3 * TG).rearrange("p (z t n) -> p z t n", z=2, t=3)
        kv_dup = area(16, B * P).rearrange("p (b m) -> p b m", b=B)
        kv_raw = area(54, B * DC).rearrange("p (b c) -> p b c", b=B)
        kv_sin = area(60, B * DC).rearrange("p (b c) -> p b c", b=B)
        kv_cos = area(66, B * DC).rearrange("p (b c) -> p b c", b=B)
        mkst = area(52, 2 * 3 * P).rearrange("p (z t m) -> p z t m", z=2, t=3)
        at = area(55, 2 * 3 * D).rearrange("p (z t d) -> p z t d", z=2, t=3)
        G = area(62, DK * NP * P).rearrange("p (k n m) -> p k n m", k=DK, n=NP)
        w1 = area(0, 2 * DK * FF).rearrange("p (z k f) -> p z k f", z=2, k=DK)
        w2 = area(16, 2 * FT * D).rearrange("p (z f d) -> p z f d", z=2, f=FT)
        hT = area(32, FT * CAP).rearrange("p (f c) -> p f c", f=FT)
        dx = work[:, 0:CT * D].rearrange("p (t d) -> p t d", t=CT)
        dT = area(52, 2 * DK * P).rearrange("p (z k c) -> p z k c", z=2, k=DK)
        dTs = tTr[:].rearrange("p n t -> p (n t)").rearrange("p (z m k c) -> p z m k c", z=2, m=2, k=DK)
        w1s = tS[:].rearrange("p h t -> p (h t)").rearrange("p (z m k f) -> p z m k f", z=2, m=2, k=DK)
        eo = work[:, CT * D:2 * CT * D].rearrange("p (t d) -> p t d", t=CT)
        grow = area(32, GB * 2 * D).rearrange("p (j k d) -> p j k d", j=GB, k=2)
        uT = area(8, DK * TG).rearrange("p (k t) -> p k t", k=DK)
        wf = area(40, 2 * DK * D).rearrange("p (w k d) -> p w k d", w=2, k=DK)
        wex = area(44, DK * (D + E)).rearrange("p (k e) -> p k e", k=DK)

        staging = [[ffn[:], x[:, B - PACKED // D:B, :].rearrange("p b d -> p (b d)")],
                   [area(36, PACKED), area(44, PACKED)], [area(0, PACKED), area(16, PACKED)]]

        def stage_of(layer, p):
            return 2 if layer == 1 and p >= NP - LATE else layer

        def part(layer, p, name):
            at_ = 0
            for n, size in PACK:
                if n == name:
                    return staging[stage_of(layer, p)][p % 2][:, at_:at_ + size]
                at_ += size

        def staged(layer, p):
            def heads(n):
                return part(layer, p, n).rearrange("p (h m) -> p h m", h=2)
            return (heads("wq"), heads("cq"), heads("kv"), heads("wo"),
                    part(layer, p, "qr").rearrange("p (t m) -> p t m", t=3), part(layer, p, "kr"))

        ld = Sems("load", "first x0 x x_rest kv tab router gain zero ffn")
        cs = Sems("const", "ident ones misc tanh zeros")
        kvs = Sems("kv", "cos sin rope ones turned copied")
        fold = [Sems(f"fold{n}", "staged0 staged1 product score_w out g_out") for n in LAYERS]
        NORM = "stats mean rstd normed turned xT veps"
        nrm = [Sems(f"norm_{n}", NORM) for n in ("att0", "ffn0", "att1", "ffn1")]
        qsem = Sems("query0", "q cos add t high low")
        q1sem = Sems("query1", "t high low")
        att = [Sems(f"att{n}", "scores negmax diag scoresT probs pv sums ln guess near1 rinv ctx unit resid kvg kvlow") for n in LAYERS]
        rt = Sems("route", "logits shifted exp step pos scattered sent carry")
        DVE_DIAG = ((0, 1), (0, 1))
        MASK_STEP, ROUTE_STEPS = 21, 34
        ROUTE_AT = ((2, 6), (7, 11), (12, 16), (17, MASK_STEP), None, (MASK_STEP + 1, 24), (25, 27), (28, 31), (32, ROUTE_STEPS))
        moe = Sems("moe", "weights0 weights1 rows0 rows1 turned dT low w_high w_split h relu y y_out stored0 stored1 eo_free")
        cb = Sems("combine", "index gathered0 gathered1 gathered2 gathered3 added")
        ff = Sems("ffn1", "logits step exp rw up relu y added stored w_down")
        NBUF = [(stats, mv, veps, rstd, xn, xT), (stats2, mv2, veps2, rstd2, xn2, xT2)] * 2

        block = ctx.enter_context(nc.Block())

        @block.sync
        def _(sp):
            def stage(layer, p):
                if p >= 2:
                    sp.wait_ge(fold[layer]("product"), p - 1)
                dst, src = staging[stage_of(layer, p)][p % 2], io[layer][:, p, :]
                if layer == 0 and p == 0:
                    dst, src = dst[:, FIRST:PACKED], src[:, FIRST:PACKED]
                sp.dma_start(dst, src).then_inc(fold[layer](f"staged{p % 2}"), 16)

            sp.dma_start(staging[0][0][:, 0:FIRST], io[0][:, 0, 0:FIRST]).then_inc(ld("first"), 16)
            sp.dma_start(x[:, 0:GB, :], io["x"][:, 0:GB, :]).then_inc(ld("x0"), 16)
            stage(0, 0)
            sp.dma_start(gains[:, 0:2], io["g_xattn"]).then_inc(ld("gain"), 16)
            sp.dma_start(gains[:, 2:4], io["g_ffn"]).then_inc(ld("gain"), 16)
            sp.dma_start(kv_raw, io["ctx"]).then_inc(ld("kv"), 16)
            sp.dma_start(kv_tab[:], io["kv_tab"]).then_inc(ld("kv"), 16)
            for dst, src in ((cosq[:], io["cosq"]), (sinq[:], io["sinq"])):
                sp.dma_start(dst, src).then_inc(ld("tab"), 16)
            for p in range(1, NP):
                stage(0, p)
            sp.dma_start(x[:, GB:2 * GB, :], io["x"][:, GB:2 * GB, :]).then_inc(ld("x"), 16)
            sp.dma_start(wg0[:], io["wg0"]).then_inc(ld("router"), 16)
            sp.wait_ge(fold[0]("product"), NP)
            sp.dma_start(x[:, 2 * GB:B, :], io["x"][:, 2 * GB:B, :]).then_inc(ld("x_rest"), 16)
            sp.wait_ge(cs("zeros"), 1)
            for n in range(E * CAP // (GB * P)):
                sp.dma_start(disp[n * GB * P:(n + 1) * GB * P, :].rearrange("(p j) d -> p j d", p=P),
                             xn2).then_inc(ld("zero"), 16)
            sp.wait_ge(qsem("t"), NG * NP)
            for p in range(NP - LATE):
                stage(1, p)

            def expert_weights(e, z):
                for dst, name in ((w1, "w1"), (w2, "w2")):
                    sp.dma_start(dst[:, z], io[name][bass.ds(e, 1), :, :].rearrange("e (k p) f -> p (e k) f", p=P)).then_inc(moe(f"weights{z}"), 16)

            def expert_rows(e, z):
                sp.wait_ge(moe("turned"), CT * e + CT)
                src = disp.rearrange("(e t p) d -> e p t d", e=E, p=P)[bass.ds(e, 1)]
                sp.dma_start(dx, src.rearrange("e p t d -> p (e t) d")).then_inc(moe(f"rows{z}"), 16)

            expert_weights(0, 0)
            sp.wait_ge(rt("scattered"), 16 * 2 * B)
            for z in range(2):
                expert_rows(z, z)
            expert_weights(1, 1)
            with sp.Fori(0, E // 2 - 1) as i:
                for z in range(2):
                    e = 2 * i + z
                    expert_rows(e + 2, z)
                    sp.wait_ge(moe("y"), 2 * CT + CT * e + CT)
                    expert_weights(e + 2, z)
            sp.wait_ge(moe("y"), 2 * CT + CT * (E - 1))
            for p in range(NP - LATE, NP):
                stage(1, p)
            sp.wait_ge(moe("y"), 2 * CT + CT * E)
            for dst, name in ((wf[:, 0], "w_up"), (wf[:, 1], "w_dn"), (wex[:, :, 0:D], "w_ex"), (wex[:, :, D:D + E], "wg1")):
                sp.dma_start(dst, io[name]).then_inc(ld("ffn"), 16)
            pieces = [(GB * i, GB) for i in range(NG - 1)] + [(b, 1) for b in range(B - GB, B)]
            for b, n in pieces:
                g, j = b // GB, b % GB
                sp.wait_ge(ff("added"), 2 * GB * g + GB + j + n)
                sp.dma_start(io["out"][:, b:b + n, :], x[:, b:b + n, :]).then_inc(ff("stored"), 16)
            sp.wait_ge(ff("stored"), 16 * len(pieces))

        def t_bank(p):
            return 7 if p == NP - 2 else 6

        def q1_bank(p):
            return 6 if p == NP - 1 else (7, 0, 1)[p % 3]

        def y_bank(j):
            return (0, 1, 6, 7)[j]

        def gate_dve():
            nc.vector.memset(scrap[:], 0.0)

        def gate_pool():
            nc.gpsimd.tensor_tensor(scrap_p[:], mhalf[:, 0:1], mhalf[:, 0:1], ALU.add)

        def rstd_pool(pool, n, i):
            s, (_, mv_, veps_, rstd_, _, _) = nrm[n], NBUF[n]
            pool.wait_ge(s("mean"), GB * i + GB)
            nc.gpsimd.tensor_tensor(veps_[:], mv_[:, :, 1], epsv[:], ALU.add).then_inc(s("veps"), 1)
            pool.wait_ge(s("veps"), i + 1)
            nc.gpsimd.tensor_tensor(rstd_[:], veps_[:], mhalf[:], ALU.pow).then_inc(s("rstd"), 1)

        def near1_pool(pool, i, n):
            s = att[1]
            pool.wait_ge(s("guess"), NU * i + n + 1)
            nc.gpsimd.tensor_tensor(sums[:, n % 2], sums[:, n % 2], rinv[:, n % 2], ALU.mult).then_inc(s("near1"), 1)

        def attend_pool(pool, layer, i, beside):
            s = att[layer]
            for k in range(NU + 3):
                if layer == 1 and k >= 3:
                    near1_pool(pool, i, k - 3)
                n = k
                if n < NU and n not in DVE_DIAG[layer]:
                    pool.wait_ge(s("negmax"), NU * i + n + 1)
                    if n >= 2:
                        pool.wait_ge(s("scoresT"), NU * i + n - 1)
                    nc.gpsimd.tensor_tensor(diag[:, n % 2], ident[:].unsqueeze(1).to_broadcast([P, 4, P]),
                                            negm[:, n % 2, :].unsqueeze(2).to_broadcast([P, 4, P]), ALU.mult).then_inc(s("diag"), 1)
                if n < NU:
                    beside(n)

        def scatter_pool(pool, i, j, k):
            nc.gpsimd.indirect_dma_start(
                out=disp, out_offset=bass.IndirectOffsetOnAxis(ap=sidx[:, j, k:k + 1], axis=0),
                in_=xn2[:, j, :], in_offset=None, bounds_check=E * CAP - 1,
                oob_is_err=False).then_inc(rt("scattered"), 16)

        def scattered_pool(pool, i):
            pool.wait_ge(rt("scattered"), 16 * 2 * GB * i + 16 * 2 * GB)
            pool.sem_inc(rt("sent"), 1)

        def indices_pool(pool, i):
            pool.wait_ge(cb("added"), 2 * GB * i + 1)
            for j in range(GB):
                for k in range(2):
                    nc.gpsimd.tensor_copy(sidx[:, j, k:k + 1], gidx[:, bass.ds(GB * i + j, 1), k]).then_inc(cb("index"), 1)
            pool.wait_ge(cb("index"), 2 * GB * i + 2 * GB)

        def gathers_pool(pool):
            gate_pool()
            for j in range(GB):
                for k in range(2):
                    nc.gpsimd.indirect_dma_start(
                        out=grow[:, j, k, :], out_offset=None, in_=eout,
                        in_offset=bass.IndirectOffsetOnAxis(ap=sidx[:, j, k:k + 1], axis=0),
                        bounds_check=E * CAP - 1, oob_is_err=False).then_inc(cb(f"gathered{j}"), 16)

        def group_low_pool(pool, layer, i):
            pool.wait_ge(att[layer]("kvg"), 4 * i + 4)
            nc.gpsimd.tensor_tensor(kvl[:], kvT[:, bass.ds(GB * i, GB), :], kvh[:].bitcast(F32), ALU.subtract).then_inc(att[layer]("kvlow"), 1)

        def layer0_pool(pool, i, first, last):
            for p in range(NP):
                pool.wait_ge(qsem("cos"), 4 * NP * i + 4 * p + 4)
                if p >= 2:
                    pool.wait_ge(qsem("t"), NP * i + p - 1)
                z = p % 2
                for t in range(3):
                    nc.gpsimd.tensor_tensor(qr[:, z, t, :], qc[:, z, t, :], qs[:, z, (1, 0, 2)[t], :],
                                            ALU.add).then_inc(qsem("add"), 1)
                if p == 0 and not first:
                    rstd_pool(pool, 1, i - 1)
                if p == 2:
                    group_low_pool(pool, 0, i)
            if first:
                pool.wait_ge(fold[0]("product"), NP)
                nc.gpsimd.memset(xn2, 0.0).then_inc(cs("zeros"), 1)

            def beside(k):
                if not last and k == 4:
                    rstd_pool(pool, 0, i + 1)
                if not first and k == 8:
                    pool.wait_ge(rt("step"), ROUTE_STEPS * (i - 1) + ROUTE_STEPS)
                    gate_pool()
                if not first and 8 <= k < 16:
                    scatter_pool(pool, i - 1, (k - 8) // 2, (k - 8) % 2)
                if not first and k == NU - 1:
                    scattered_pool(pool, i - 1)

            attend_pool(pool, 0, i, beside)

        def layer1_pool(pool, i, last):
            group_low_pool(pool, 1, i)
            if not last:
                indices_pool(pool, i + 1)
                gathers_pool(pool)

            def beside(k):
                if not last and k == 9:
                    rstd_pool(pool, 2, i + 1)

            attend_pool(pool, 1, i, beside)
            rstd_pool(pool, 3, i)

        @block.gpsimd
        def _(pool):
            nc.gpsimd.memset(ident[:], 0.0).then_inc(cs("ident"), 1)
            nc.gpsimd.memset(before[:], 1.0).then_inc(cs("ident"), 1)
            pool.wait_ge(cs("ident"), 2)
            nc.gpsimd.affine_select(out=ident[:], in_=ident[:], compare_op=ALU.not_equal, fill=1.0, base=0,
                                    pattern=[[-1, P]], channel_multiplier=1).then_inc(cs("ident"), 1)
            nc.gpsimd.affine_select(out=before[:], in_=before[:], compare_op=ALU.is_gt, fill=0.0, base=0,
                                    pattern=[[1, P]], channel_multiplier=-1).then_inc(cs("ident"), 1)
            nc.gpsimd.memset(ones[:], 1.0).then_inc(cs("ones"), 1)
            nc.gpsimd.memset(mhalf[:], -0.5).then_inc(cs("misc"), 1)
            nc.gpsimd.memset(epsv[:], EPS).then_inc(cs("misc"), 1)
            nc.gpsimd.iota(ebuf[:, 0, 0, :].bitcast(I32), pattern=[[-1, E]], base=E, channel_multiplier=0).then_inc(cs("misc"), 1)
            nc.gpsimd.iota(ebuf[:, 1, 0, :].bitcast(I32), pattern=[[CAP, E]], base=0, channel_multiplier=0).then_inc(cs("misc"), 1)
            pool.wait_ge(cs("misc"), 4)
            nc.gpsimd.tensor_copy(tie[:], ebuf[:, 0, 0, :].bitcast(I32)).then_inc(cs("misc"), 1)
            nc.gpsimd.tensor_copy(base[:], ebuf[:, 1, 0, :].bitcast(I32)).then_inc(cs("misc"), 1)
            pool.sem_inc(rt("sent"), 1)
            pool.sem_inc(moe("eo_free"), 1)
            rstd_pool(pool, 0, 0)
            layer0_pool(pool, 0, True, False)
            with pool.Fori(1, NG - 1) as i:
                layer0_pool(pool, i, False, False)
            layer0_pool(pool, NG - 1, False, True)
            rstd_pool(pool, 1, NG - 1)
            pool.wait_ge(rt("step"), ROUTE_STEPS * NG)
            for j in range(GB):
                for k in range(2):
                    scatter_pool(pool, NG - 1, j, k)
            scattered_pool(pool, NG - 1)
            indices_pool(pool, 0)
            with pool.Fori(0, E // 2) as i:
                for z in range(2):
                    pool.wait_ge(moe("y_out"), 2 * CT * i + CT * (z + 1) + 2)
                    nc.gpsimd.dma_start(eout.rearrange("(e t p) d -> e p t d", e=E, p=P)[bass.ds(2 * i + z, 1)].rearrange("e p t d -> p (e t) d"),
                                        eo).then_inc(moe(f"stored{z}"), 16)
                    pool.wait_ge(moe(f"stored{z}"), 16 * i + 16)
                    pool.sem_inc(moe("eo_free"), 1)
            gathers_pool(pool)
            rstd_pool(pool, 2, 0)
            with pool.Fori(0, NG - 1) as i:
                layer1_pool(pool, i, False)
            layer1_pool(pool, NG - 1, True)

        def turned_act(act, n, i, j, bank):
            act.wait_ge(nrm[n]("turned"), GB * i + j + 1)
            nc.scalar.activation(NBUF[n][5][:, :, j * S:(j + 1) * S],
                                 PS[:, bank, 0:D].rearrange("p (k m) -> p k m", k=DK), ACT.Copy).then_inc(nrm[n]("xT"), 1)

        def group_kv(act, layer, i):
            s = att[layer]
            nc.scalar.activation(kvag[:, :, DC:2 * DC], kv_r[:, bass.ds(GB * i, GB), :], ACT.Copy).then_inc(s("kvg"), 1)
            nc.scalar.activation(kvh[:], kvT[:, bass.ds(GB * i, GB), :], ACT.Copy).then_inc(s("kvg"), 1)
            for half in range(2):
                h = slice(64 * half, 64 * half + 64)
                src = kvT[h, bass.ds(GB * i, GB), :]
                nc.scalar.activation(kvgr[h, :, half, :], src, ACT.Copy).then_inc(s("kvg"), 1)

        def t_act(act, s, layer, i, p, bank):
            act.wait_ge(s("t"), NP * i + p + 1)
            nc.scalar.activation(tTr[:, p, :], PS[:, bank, :], ACT.Copy).then_inc(s("high"), 1)
            act.wait_ge(s("high"), 3 * NP * i + 3 * p + 1)
            for a in range(2):
                nc.scalar.activation(tS[0:64, 2 * p + a, :], tTr[64 * a:64 * a + 64, p, :].bitcast(F32),
                                     ACT.Copy).then_inc(s("high"), 1)

        def attend_act(act, layer, i, beside):
            s = att[layer]
            for k in range(NU + 4):
                n = k - 1
                if 0 <= n < NU:
                    act.wait_ge(s("scoresT"), NU * i + n + 1)
                    if n >= 2:
                        act.wait_ge(s("pv"), NU * i + n - 1)
                    nc.scalar.activation(PT[:, n % 2], PS[:, 2 + n % 2, :].rearrange("p (h m) -> p h m", h=4),
                                         ACT.Exp).then_inc(s("probs"), 1)
                n = k - 2
                if 0 <= n < NU:
                    act.wait_ge(s("pv"), NU * i + n + 1)
                    if n >= 2:
                        act.wait_ge(s("ctx"), 2 * NU * i + 2 * n - 2)
                    bank = PS[:, 4 + n % 2, :].rearrange("p (a g m) -> p a g m", a=2, g=2)
                    for a in range(2):
                        own, other = slice(64 * a, 64 * a + 64), slice(64 - 64 * a, P - 64 * a)
                        nc.scalar.activation(sums[own, n % 2], bank[other, a], ACT.Copy).then_inc(s("sums"), 1)
                    act.wait_ge(s("sums"), 2 * NU * i + 2 * n + 2)
                    nc.scalar.activation(rinv[:, n % 2], sums[:, n % 2], ACT.Ln).then_inc(s("ln"), 1)
                    act.wait_ge(s("ln"), NU * i + n + 1)
                    nc.scalar.activation(rinv[:, n % 2], rinv[:, n % 2], ACT.Exp, scale=-1.0).then_inc(s("guess"), 1)
                beside(k)

        def fold0_act(act, p):
            z = 3 * (p % 2)
            act.wait_ge(fold[0]("product"), p + 1)
            for k in range(DK):
                src = PS[:, z + k, :]
                h0 = src[:, 0:DQ].rearrange("p (a q) -> p a q", a=2)
                h1 = src[:, DQ:2 * DQ].rearrange("p (a q) -> p a q", a=2)
                dst = A[:, k, p]
                nc.scalar.activation(dst[:, 0:2, 0:LO], h0, ACT.Copy)
                nc.scalar.activation(dst[:, 0:2, LO:P], h1[:, :, 0:P - LO], ACT.Copy)
                nc.scalar.activation(dst[:, 2, :].rearrange("p (a m) -> p a m", a=2), h1[:, :, P - LO:LO], ACT.Copy)
            nc.scalar.activation(MK[:, p].rearrange("p t m -> p (t m)"), PS[:, z + 2, 0:3 * P], ACT.Copy)
            nc.scalar.activation(U[:, p, :], PS[:, 7, 0:D], ACT.Copy, scale=tg[:, 0:1]).then_inc(fold[0]("out"), 1)

        def fold1_act(act, p):
            z = p % 2
            act.wait_ge(fold[1]("product"), p + 1)
            nc.scalar.activation(at[:, z, 0:2, :].rearrange("p t d -> p (t d)"), PS[:, 3 * z, :], ACT.Copy)
            nc.scalar.activation(at[:, z, 2, :], PS[:, 3 * z + 1, 0:D], ACT.Copy)
            nc.scalar.activation(mkst[:, z].rearrange("p t m -> p (t m)"), PS[:, 3 * z + 2, 0:3 * P], ACT.Copy)
            nc.scalar.activation(U[:, p, :], PS[:, 3 * z + 1, D:2 * D], ACT.Copy, scale=tg[:, 1:2]).then_inc(fold[1]("out"), 1)

        def fold1g_act(act, p):
            act.wait_ge(fold[1]("score_w"), p + 1)
            nc.scalar.activation(G[:, :, p, :], PS[:, 3 * (p % 2), 0:2 * P].rearrange("p (k m) -> p k m", k=DK),
                                 ACT.Copy).then_inc(fold[1]("g_out"), 1)

        def layer0_act(act, i, first, last):
            for p in range(NP):
                if first and p == 0:
                    for b in range(B):
                        act.wait_ge(kvs("turned"), b + 1)
                        nc.scalar.activation(kvT[:, b, :], PS[:, 3 + b % 4, 0:P], ACT.Copy).then_inc(kvs("copied"), 1)
                    act.wait_ge(kvs("ones"), 2)
                    act.wait_ge(kvs("copied"), B)
                if first and p + 1 < NP:
                    fold0_act(act, p + 1)
                if not first and p == NP - 1:
                    route_exp_act(act, i - 1)
                if p >= 2:
                    t_act(act, qsem, 0, i, p - 2, t_bank(p - 2))
                if p == 1:
                    group_kv(act, 0, i)
                if not first and 2 <= p < 6:
                    turned_act(act, 1, i - 1, p - 2, 7)

            def beside(k):
                if k < 2:
                    t_act(act, qsem, 0, i, NP - 2 + k, t_bank(NP - 2 + k))
                if not last and 10 <= k < 14:
                    turned_act(act, 0, i + 1, k - 10, 7)

            attend_act(act, 0, i, beside)

        def route_exp_act(act, i):
            act.wait_ge(rt("shifted"), i + 1)
            nc.scalar.activation(ebuf[:, 1], ebuf[:, 0], ACT.Exp).then_inc(rt("exp"), 1)

        def expert_turned_act(act, e, z, t):
            act.wait_ge(moe("turned"), CT * e + CT + t + 1)
            dst = dT[:, z] if t == CT - 1 else dTs[:, z, 0, :, t * P:(t + 1) * P]
            nc.scalar.activation(dst, PS[:, t % 2, 0:D].rearrange("p (k m) -> p k m", k=DK), ACT.Copy).then_inc(moe("dT"), 1)

        def expert_act(act, e, z, last):
            for f in range(FT):
                act.wait_ge(moe("h"), FT * e + f + 1)
                nc.scalar.activation(hT[:, f, 0:SPLIT], PS[:, 2 + 2 * (f % 2), :], ACT.Relu)
                nc.scalar.activation(hT[:, f, SPLIT:CAP], PS[:, 3 + 2 * (f % 2), 0:P], ACT.Relu).then_inc(moe("relu"), 1)
                if not last and f >= FT - CT:
                    expert_turned_act(act, e + 1, 1 - z, f - (FT - CT))

        def layer1_act(act, i, last):
            def beside(k):
                if not last and 13 <= k < 17:
                    turned_act(act, 2, i + 1, k - 13, 7)
                if not last and NU + 1 <= k < NU + 3:
                    t_act(act, q1sem, 1, i + 1, k - NU - 1, q1_bank(k - NU - 1))

            attend_act(act, 1, i, beside)
            if not last:
                group_kv(act, 1, i + 1)
            for p in range(2, NP):
                if not last:
                    t_act(act, q1sem, 1, i + 1, p, q1_bank(p))
                if p >= 4:
                    turned_act(act, 3, i, p - 4, p - 2)
            for f in range(DK):
                act.wait_ge(ff("up"), DK * i + f + 1)
                nc.scalar.activation(uT[:, f, :], PS[:, f, :], ACT.Relu).then_inc(ff("relu"), 1)
            act.wait_ge(ff("step"), 3 * i + 1)
            nc.scalar.activation(rsm[:, 9, :], rsm[:, 8, :], ACT.Exp).then_inc(ff("exp"), 1)

        @block.scalar
        def _(act):
            act.wait_ge(ld("gain"), 32)
            nc.scalar.activation(tg[:], gains[:], ACT.Tanh).then_inc(cs("tanh"), 1)
            act.wait_ge(cs("tanh"), 1)
            nc.scalar.preload_act_table_set("natural_log_exp_and_others")
            fold0_act(act, 0)
            for j in range(GB):
                turned_act(act, 0, 0, j, 3 + j)
            layer0_act(act, 0, True, False)
            with act.Fori(1, NG - 1) as i:
                layer0_act(act, i, False, False)
            layer0_act(act, NG - 1, False, True)
            fold1_act(act, 0)
            for p in range(NP - LATE):
                if p + 1 < NP - LATE:
                    fold1_act(act, p + 1)
                if p == 0:
                    for j in range(GB):
                        turned_act(act, 1, NG - 1, j, 6 + j % 2)
                    route_exp_act(act, NG - 1)
                fold1g_act(act, p)
            for t in range(CT):
                expert_turned_act(act, 0, 0, t)
            with act.Fori(0, E // 2 - 1) as i:
                for z in range(2):
                    expert_act(act, 2 * i + z, z, False)
            for z in range(2):
                expert_act(act, E - 2 + z, z, z == 1)
            fold1_act(act, NP - LATE)
            for p in range(NP - LATE, NP):
                if p + 1 < NP:
                    fold1_act(act, p + 1)
                fold1g_act(act, p)
            for j in range(GB):
                turned_act(act, 2, 0, j, 6 + j % 2)
            group_kv(act, 1, 0)
            for p in range(NP):
                t_act(act, q1sem, 1, 0, p, q1_bank(p))
            with act.Fori(0, NG - 1) as i:
                layer1_act(act, i, False)
            layer1_act(act, NG - 1, True)

        def turn_pe(pe, n, i, j, bank, reused):
            s, src = nrm[n], NBUF[n][4]
            pe.wait_ge(s("normed"), GB * i + j + 1)
            if j >= reused:
                pe.wait_ge(s("xT"), GB * i + j + 1 - reused)
            for k in range(DK):
                mm = nc.tensor.transpose(PS[:, bank, k * P:(k + 1) * P], src[:, j, k * P:(k + 1) * P], ident[:])
            mm.then_inc(s("turned"), 1)

        def attend_pe(pe, layer, i, start, beside):
            s = att[layer]
            pe.wait_ge(s("kvg"), 4 * i + 4)
            pe.wait_ge(s("kvlow"), i + 1)
            for k in range(NU + 4):
                n = k
                if n < NU:
                    j, q = n // 4, n % 4
                    tok = slice(j * S, (j + 1) * S)
                    start(n)
                    if n >= 2:
                        pe.wait_ge(s("negmax"), NU * i + n - 1)
                    for pp in range(2):
                        mm = nc.tensor.matmul(PS[:, n % 2, pp * 2 * P:(pp + 1) * 2 * P], tTr[:, 2 * q + pp, tok],
                                              kvgr[:, j].rearrange("p a m -> p (a m)"), start=True, stop=True)
                    mm.then_inc(s("scores"), 1)
                    if n >= 2:
                        pe.wait_ge(s("probs"), NU * i + n - 1)
                    for m, kv in enumerate((kvh, kvl)):
                        nc.tensor.matmul(PS[:, 2 + n % 2, :], kv[:, j, :], tS[:, 4 * q:4 * q + 4, tok],
                                         start=(m == 0), stop=False, skip_group_check=True)
                n = k - 1
                if 0 <= n < NU:
                    pe.wait_ge(s("diag"), NU * i + n + 1)
                    nc.tensor.matmul(PS[:, 2 + n % 2, :], ones_r[:], diag[:, n % 2].rearrange("p h m -> p (h m)"),
                                     start=False, stop=True, skip_group_check=True).then_inc(s("scoresT"), 1)
                n = k - 2
                if 0 <= n < NU:
                    pe.wait_ge(s("probs"), NU * i + n + 1)
                    if n >= 2:
                        pe.wait_ge(s("ctx"), 2 * NU * i + 2 * n - 2)
                    probs = PT[:, n % 2].rearrange("p (g a) m -> p g a m", a=2)
                    for a in range(2):
                        mm = nc.tensor.matmul(PS[:, 4 + n % 2, a * 2 * P:(a + 1) * 2 * P], kvag[:, n // 4, DC - DC * a:3 * DC - DC * a],
                                              probs[:, :, a, :], start=True, stop=True)
                    mm.then_inc(s("pv"), 1)
                n = k - 4
                if 0 <= n < NU:
                    j, q = n // 4, n % 4
                    pe.wait_ge(s("ctx"), 2 * NU * i + 2 * n + 2)
                    if q == 0 and j >= 1:
                        pe.wait_ge(s("resid"), GB * i + j)
                    for g in range(2):
                        mm = nc.tensor.matmul(PS[:, 6, 0:D], cT[:, n % 2, g, :], U[:, 2 * q + g, :],
                                              start=(q == 0 and g == 0), stop=(q == 3 and g == 1))
                    mm.then_inc(s("unit"), 1)
                beside(k)

        def fold_mk_u(layer, p, mk_bank, u_out):
            _, _, wkv, wo, wqr, wkr = staged(layer, p)
            for t in range(3):
                nc.tensor.matmul(PS[:, mk_bank, t * P:(t + 1) * P], wqr[:, t, :], wkr, start=True, stop=True)
            for h in range(2):
                mm = nc.tensor.matmul(u_out[64 * h:64 * h + 64, :], wkv[:, h, :], wo[:, h, :], start=True, stop=True)
            mm.then_inc(fold[layer]("product"), 1)

        def fold0_pe(pe, p):
            wq, cq = staged(0, p)[0:2]
            if p == 0:
                pe.wait_ge(ld("first"), 16)
            else:
                pe.wait_ge(fold[0](f"staged{p % 2}"), 16 * (p // 2 + 1))
                pe.wait_ge(fold[0]("out"), p)
            for k in range(DK):
                for h in range(2):
                    nc.tensor.matmul(PS[:, 3 * (p % 2) + k, h * DQ:(h + 1) * DQ], wq[:, h, k * P:(k + 1) * P], cq[:, h, :],
                                     start=True, stop=True)
            pe.wait_ge(fold[0](f"staged{p % 2}"), 16 * (p // 2 + 1))
            fold_mk_u(0, p, 3 * (p % 2) + 2, PS[:, 7, 0:D])

        def fold1_pe(pe, p):
            z = p % 2
            wq, cq = staged(1, p)[0:2]
            pe.wait_ge(fold[1](f"staged{z}"), 16 * (p // 2 + 1))
            if p >= 2:
                pe.wait_ge(fold[1]("g_out"), p - 1)
            c0, c1 = cq[:, 0, :], cq[:, 1, :]
            for t in range(2):
                bank = PS[:, 3 * z, t * D:(t + 1) * D]
                nc.tensor.matmul(bank[0:LO, :], c0[:, t * LO:(t + 1) * LO], wq[:, 0, :], start=True, stop=True)
                nc.tensor.matmul(bank[LO:P, :], c1[:, t * LO:t * LO + P - LO], wq[:, 1, :], start=True, stop=True)
            for t in range(2):
                nc.tensor.matmul(PS[64 * t:64 * t + 64, 3 * z + 1, 0:D], c1[:, t * LO + P - LO:(t + 1) * LO], wq[:, 1, :],
                                 start=True, stop=True)
            fold_mk_u(1, p, 3 * z + 2, PS[:, 3 * z + 1, D:2 * D])

        def fold1g_pe(pe, p):
            z = p % 2
            pe.wait_ge(fold[1]("out"), p + 1)
            for k in range(DK):
                for t in range(3):
                    mm = nc.tensor.matmul(PS[:, 3 * z, k * P:(k + 1) * P], at[:, z, t, k * P:(k + 1) * P], mkst[:, z, t, :],
                                          start=(t == 0), stop=(t == 2))
            mm.then_inc(fold[1]("score_w"), 1)

        def logits_pe(pe, n, i, w, done):
            pe.wait_ge(nrm[n]("xT"), GB * i + GB)
            src = NBUF[n][5]
            for j in range(GB):
                for k in range(DK):
                    mm = nc.tensor.matmul(PS[:, 7, j * E:(j + 1) * E], src[:, k, j * S:(j + 1) * S], w[:, k, :],
                                          start=(k == 0), stop=(k == DK - 1))
            mm.then_inc(done, 1)

        def place_pe(pe, i):
            pe.wait_ge(rt("step"), ROUTE_STEPS * i + MASK_STEP)
            nc.tensor.matmul(PS[:, 7, 0:GB * E], before[:], ebuf[:, 7].rearrange("p j e -> p (j e)"), start=True, stop=False)
            nc.tensor.matmul(PS[:, 7, 0:GB * E], ones[:], macc[:, 0:GB, :].rearrange("p j e -> p (j e)"),
                             start=False, stop=True).then_inc(rt("pos"), 1)

        def q_pe(pe, i, p, tiles=range(3)):
            for t in tiles:
                for k in range(DK):
                    mm = nc.tensor.matmul(PS[:, 3 * (p % 2) + t, :], A[:, k, p, t, :], xT[:, k, :],
                                          start=(k == 0), stop=(k == DK - 1))
            if tiles[-1] == 2:
                mm.then_inc(qsem("q"), 1)

        def t_pe(pe, i, p, first):
            pe.wait_ge(qsem("add"), 3 * NP * i + 3 * p + 3)
            if p == NP - 2:
                if not first:
                    pe.wait_ge(rt("shifted"), i)
            elif p >= 1:
                before = p - 1 if p == NP - 1 else p
                pe.wait_ge(qsem("high"), 3 * NP * i + 3 * before)
                pe.wait_ge(qsem("low"), 2 * NP * i + 2 * before)
            for t in range(3):
                mm = nc.tensor.matmul(PS[:, t_bank(p), :], MK[:, p, t, :], qr[:, p % 2, t, :], start=(t == 0), stop=(t == 2))
            mm.then_inc(qsem("t"), 1)

        def layer0_pe(pe, i, first, last):
            for p in range(NP):
                if p >= 2:
                    pe.wait_ge(qsem("cos"), 4 * NP * i + 4 * (p - 1))
                elif p == 1 and not first:
                    pe.wait_ge(att[0]("ctx"), 2 * NU * i)
                if first:
                    pe.wait_ge(fold[0]("out"), p + 1)
                if p >= 1 or first:
                    q_pe(pe, i, p)
                if first and p == 0:
                    pe.wait_ge(kvs("rope"), 2)
                    for b in range(B):
                        if b >= 4:
                            pe.wait_ge(kvs("copied"), b - 3)
                        nc.tensor.transpose(PS[:, 3 + b % 4, 0:P], kv_dup[:, b, :], ident[:]).then_inc(kvs("turned"), 1)
                    pe.wait_ge(kvs("copied"), B)
                if first and p + 1 < NP:
                    if p >= 1:
                        pe.wait_ge(qsem("cos"), 4 * p)
                    fold0_pe(pe, p + 1)
                if not first and 2 <= p < 6:
                    turn_pe(pe, 1, i - 1, p - 2, 7, 1)
                if not first and p == 6:
                    logits_pe(pe, 1, i - 1, wg0, rt("logits"))
                if p >= 2:
                    t_pe(pe, i, p - 2, first)

            def start(n):
                if n < 4:
                    pe.wait_ge(qsem("high"), 3 * NP * i + 6 * (n + 1))
                    pe.wait_ge(qsem("low"), 2 * NP * i + 4 * (n + 1))
                if n < 2:
                    pe.wait_ge(qsem("cos"), 4 * NP * i + 4 * (NP - 1 + n))

            def beside(k):
                if k < 2:
                    t_pe(pe, i, NP - 2 + k, first)
                if not first and k == 5:
                    place_pe(pe, i - 1)
                if not last and 10 <= k < 14:
                    turn_pe(pe, 0, i + 1, k - 10, 7, 1)
                if not last and k == NU + 1:
                    pe.wait_ge(nrm[0]("xT"), GB * (i + 2))
                    pe.wait_ge(att[0]("negmax"), NU * (i + 1))
                    q_pe(pe, i + 1, 0, (0,))
                if not last and k == NU + 2:
                    q_pe(pe, i + 1, 0, (1, 2))

            attend_pe(pe, 0, i, start, beside)

        def expert_turn_pe(pe, e, z, t, rows):
            if t == 0:
                pe.wait_ge(moe(f"rows{z}"), rows)
            if t >= 2:
                pe.wait_ge(moe("dT"), CT * e + t - 1)
                pe.wait_ge(moe("low"), (CT - 1) * e + t - 1)
            for k in range(DK):
                mm = nc.tensor.transpose(PS[:, t % 2, k * P:(k + 1) * P], dx[:, t, k * P:(k + 1) * P], ident[:])
            mm.then_inc(moe("turned"), 1)

        def expert_pe(pe, i, z, last):
            e = 2 * i + z
            pe.wait_ge(moe("dT"), CT * e + CT)
            pe.wait_ge(moe("low"), (CT - 1) * e + CT - 1)
            pe.wait_ge(moe("w_split"), e + 1)
            pe.wait_ge(moe(f"weights{z}"), 32 * i + 32)
            for f in range(FT):
                if f >= 2:
                    pe.wait_ge(moe("relu"), FT * e + f - 1)
                col = slice(f * P, (f + 1) * P)
                for k in range(DK):
                    for m, c in ((0, 0), (0, 1), (1, 0)):
                        nc.tensor.matmul(PS[:, 2 + 2 * (f % 2), :], w1s[:, z, m, k, col], dTs[:, z, c, k, :],
                                         start=(k == 0 and m == c), stop=(k == DK - 1 and m == 1))
                for k in range(DK):
                    mm = nc.tensor.matmul(PS[:, 3 + 2 * (f % 2), 0:P], w1[:, z, k, col], dT[:, z, k, :],
                                          start=(k == 0), stop=(k == DK - 1))
                mm.then_inc(moe("h"), 1)
                if not last and f >= FT - CT:
                    expert_turn_pe(pe, e + 1, 1 - z, f - (FT - CT), 16 * (i + z) + 16)
            pe.wait_ge(moe("relu"), FT * e + FT)
            for t in range(CT):
                pe.wait_ge(moe("y_out"), CT * e + t + 1)
                for f in range(FT):
                    mm = nc.tensor.matmul(PS[:, 6 + (z * CT + t) % 2, 0:D], hT[:, f, t * P:(t + 1) * P], w2[:, z, f, :],
                                          start=(f == 0), stop=(f == FT - 1))
                mm.then_inc(moe("y"), 1)

        def query1_pe(pe, i, p):
            if p >= 3:
                pe.wait_ge(q1sem("high"), 3 * NP * i + 3 * (p - 2))
                pe.wait_ge(q1sem("low"), 2 * NP * i + 2 * (p - 2))
            for k in range(DK):
                mm = nc.tensor.matmul(PS[:, q1_bank(p), :], G[:, k, p, :], xT[:, k, :], start=(k == 0), stop=(k == DK - 1))
            mm.then_inc(q1sem("t"), 1)

        def expert1_pe(pe, i, j):
            pe.wait_ge(nrm[3]("xT"), GB * i + j + 1)
            for k in range(DK):
                mm = nc.tensor.matmul(PS[:, 2 + j, 0:D + E], xT2[:, k, j * S:(j + 1) * S], wex[:, k, :],
                                      start=(k == 0), stop=(k == DK - 1))
            mm.then_inc(ff("logits"), 1)

        def layer1_pe(pe, i, first, last):
            def start(n):
                if n >= 4:
                    return
                if first:
                    pe.wait_ge(q1sem("high"), 3 * max(2 * n + 2, NP - 3 + n))
                    pe.wait_ge(q1sem("low"), 2 * max(2 * n + 2, NP - 3 + n))
                    return
                pe.wait_ge(ff("added"), 2 * GB * (i - 1) + GB + n + 1)

            def beside(k):
                if not last and 13 <= k < 17:
                    turn_pe(pe, 2, i + 1, k - 13, 7, 1)
                if not last and k == NU + 1:
                    pe.wait_ge(nrm[2]("xT"), GB * (i + 2))
                    pe.wait_ge(att[1]("negmax"), NU * (i + 1))
                    query1_pe(pe, i + 1, 0)
                if not last and k == NU + 2:
                    query1_pe(pe, i + 1, 1)

            attend_pe(pe, 1, i, start, beside)
            for p in range(2, NP):
                if not last:
                    query1_pe(pe, i + 1, p)
                if p >= 4:
                    turn_pe(pe, 3, i, p - 4, p - 2, GB)
            if first:
                pe.wait_ge(ld("ffn"), 64)
                pe.wait_ge(ff("w_down"), 1)
            expert1_pe(pe, i, 0)
            expert1_pe(pe, i, 1)
            if not last:
                pe.wait_ge(q1sem("high"), 3 * NP * (i + 2))
                pe.wait_ge(q1sem("low"), 2 * NP * (i + 2))
            pe.wait_ge(nrm[3]("xT"), GB * i + GB)
            for f in range(DK):
                for k in range(DK):
                    mm = nc.tensor.matmul(PS[:, f, :], wf[:, 0, k, f * P:(f + 1) * P], xT2[:, k, :],
                                          start=(k == 0), stop=(k == DK - 1))
                mm.then_inc(ff("up"), 1)
            expert1_pe(pe, i, 2)
            expert1_pe(pe, i, 3)
            pe.wait_ge(ff("relu"), DK * i + DK)
            for j in range(GB):
                for k in range(DK):
                    mm = nc.tensor.matmul(PS[:, y_bank(j), 0:D], uT[:, k, j * S:(j + 1) * S], wf[:, 1, k, :],
                                          start=(k == 0), stop=(k == DK - 1))
                mm.then_inc(ff("y"), 1)

        @block.tensor
        def _(pe):
            pe.sem_inc(moe("y"), 2 * CT)
            pe.sem_inc(moe("turned"), CT)
            pe.wait_ge(cs("ident"), 4)
            fold0_pe(pe, 0)
            for j in range(GB):
                turn_pe(pe, 0, 0, j, 3 + j, GB)
            pe.wait_ge(nrm[0]("xT"), GB)
            pe.wait_ge(cs("ones"), 2)
            layer0_pe(pe, 0, True, False)
            pe.wait_ge(ld("router"), 16)
            with pe.Fori(1, NG - 1) as i:
                layer0_pe(pe, i, False, False)
            layer0_pe(pe, NG - 1, False, True)
            fold1_pe(pe, 0)
            for p in range(NP - LATE):
                if p + 1 < NP - LATE:
                    fold1_pe(pe, p + 1)
                if p == 0:
                    for j in range(GB):
                        turn_pe(pe, 1, NG - 1, j, 6 + j % 2, 2)
                    logits_pe(pe, 1, NG - 1, wg0, rt("logits"))
                if p == 1:
                    place_pe(pe, NG - 1)
                fold1g_pe(pe, p)
            pe.wait_ge(fold[1]("g_out"), NP - LATE)
            for t in range(CT):
                expert_turn_pe(pe, 0, 0, t, 16)
            with pe.Fori(0, E // 2 - 1) as i:
                for z in range(2):
                    expert_pe(pe, i, z, False)
            for z in range(2):
                expert_pe(pe, E // 2 - 1, z, z == 1)
            fold1_pe(pe, NP - LATE)
            for p in range(NP - LATE, NP):
                if p + 1 < NP:
                    fold1_pe(pe, p + 1)
                fold1g_pe(pe, p)
            for j in range(GB):
                turn_pe(pe, 2, 0, j, 6 + j % 2, 2)
            pe.wait_ge(fold[1]("g_out"), NP)
            pe.wait_ge(nrm[2]("xT"), GB)
            for p in range(NP):
                query1_pe(pe, 0, p)
            layer1_pe(pe, 0, True, False)
            with pe.Fori(1, NG - 1) as i:
                layer1_pe(pe, i, False, False)
            layer1_pe(pe, NG - 1, False, True)

        def batch(b):
            return x[:, bass.ds(b, 1), :].rearrange("p b d -> p (b d)")

        def stats_dve(dve, n, i, js=range(GB)):
            s, (stats_, mv_, _, _, _, _) = nrm[n], NBUF[n]
            if n == 2:
                dve.wait_ge(cb("added"), 2 * (GB * i + js[-1]) + 3)
            gate_dve()
            for j in js:
                nc.vector.bn_stats(stats_[:, j, :], batch(GB * i + j)).then_inc(s("stats"), 1)
            if js[-1] == GB - 1:
                dve.wait_ge(s("stats"), GB * i + GB)
                gate_dve()
                for j in range(GB):
                    nc.vector.bn_aggr(mv_[:, j, :], stats_[:, j, :]).then_inc(s("mean"), 1)

        def normed_dve(dve, n, i, js=range(GB)):
            s, (_, mv_, _, rstd_, dst, _) = nrm[n], NBUF[n]
            dve.wait_ge(s("rstd"), i + 1)
            for j in js:
                nc.vector.tensor_scalar(dst[:, j, :], batch(GB * i + j), mv_[:, j, 0:1], rstd_[:, j:j + 1],
                                        ALU.subtract, ALU.mult).then_inc(s("normed"), 1)

        def attend_dve(dve, layer, i, beside):
            s = att[layer]
            for k in range(NU + 5):
                n = k - 5
                if 0 <= n < NU and n % 4 == 3:
                    j = n // 4
                    dve.wait_ge(s("unit"), NU * i + n + 1)
                    nc.vector.tensor_tensor(batch(GB * i + j), PS[:, 6, 0:D], batch(GB * i + j), ALU.add).then_inc(s("resid"), 1)
                n = k
                if n < NU:
                    dve.wait_ge(s("scores"), NU * i + n + 1)
                    if n >= 2:
                        dve.wait_ge(s("diag"), NU * i + n - 1)
                    nc.vector.tensor_reduce(negm[:, n % 2, :], PS[:, n % 2, :].rearrange("p (h m) -> p h m", h=4),
                                            AX.X, ALU.max, negate=True).then_inc(s("negmax"), 1)
                    if n in DVE_DIAG[layer]:
                        dve.wait_ge(s("negmax"), NU * i + n + 1)
                        nc.vector.tensor_tensor(diag[:, n % 2], ident[:].unsqueeze(1).to_broadcast([P, 4, P]),
                                                negm[:, n % 2, :].unsqueeze(2).to_broadcast([P, 4, P]), ALU.mult).then_inc(s("diag"), 1)
                n = k - 3
                if 0 <= n < NU:
                    bank = PS[:, 4 + n % 2, :].rearrange("p (a g m) -> p a g m", a=2, g=2)
                    flat = "p g m -> p (g m)"
                    if layer == 0:
                        dve.wait_ge(s("guess"), NU * i + n + 1)
                        nc.vector.tensor_tensor(sums[:, n % 2], sums[:, n % 2], rinv[:, n % 2], ALU.mult).then_inc(s("near1"), 1)
                    dve.wait_ge(s("near1"), NU * i + n + 1)
                    nc.vector.scalar_tensor_tensor(out=rinv[:, n % 2].rearrange(flat), in0=sums[:, n % 2].rearrange(flat), scalar=-2.0,
                                                   in1=rinv[:, n % 2].rearrange(flat), op0=ALU.add, op1=ALU.mult).then_inc(s("rinv"), 1)
                    dve.wait_ge(s("rinv"), NU * i + n + 1)
                    if n >= 2:
                        dve.wait_ge(s("unit"), NU * i + n - 1)
                    for a in range(2):
                        own = slice(64 * a, 64 * a + 64)
                        nc.vector.scalar_tensor_tensor(out=cT[own, n % 2].rearrange(flat), in0=bank[own, a].rearrange(flat), scalar=-1.0,
                                                       in1=rinv[own, n % 2].rearrange(flat), op0=ALU.mult, op1=ALU.mult).then_inc(s("ctx"), 1)
                beside(k)
            dve.wait_ge(s("resid"), GB * i + GB)

        def wide(a):
            return a.unsqueeze(2).to_broadcast([P, GB, E])

        def choose_dve(dve, i, lo, hi):
            V = nc.vector
            count = 0

            def step(instruction):
                nonlocal count
                count += 1
                if lo <= count <= hi:
                    instruction().then_inc(rt("step"), 1)
                    dve.wait_ge(rt("step"), ROUTE_STEPS * i + count)

            logits = PS[:, 7, 0:GB * E].rearrange("p (j e) -> p j e", j=GB)
            if lo == 1:
                dve.wait_ge(rt("logits"), i + 1)
            step(lambda: V.tensor_reduce(rsm[:, 0, :], logits, AX.X, ALU.max))
            if lo == 1:
                V.tensor_tensor(ebuf[:, 0], logits, wide(rsm[:, 0, :]), ALU.subtract).then_inc(rt("shifted"), 1)
            if lo == 2:
                dve.wait_ge(rt("exp"), i + 1)
            step(lambda: V.tensor_reduce(rsm[:, 1, :], ebuf[:, 1], AX.X, ALU.add))
            step(lambda: V.reciprocal(rsm[:, 2, :], rsm[:, 1, :]))
            step(lambda: V.tensor_tensor(ebuf[:, 2], ebuf[:, 1], wide(rsm[:, 2, :]), ALU.mult))
            probs = ebuf[:, 2]
            for k in range(2):
                step(lambda: V.tensor_reduce(gates[:, k, :], probs, AX.X, ALU.max))
                step(lambda: V.tensor_tensor(ebuf[:, 3], probs, wide(gates[:, k, :]), ALU.is_equal))
                step(lambda: V.tensor_tensor(ebuf[:, 4], ebuf[:, 3], tie[:].unsqueeze(1).to_broadcast([P, GB, E]), ALU.mult))
                step(lambda: V.tensor_reduce(rsm[:, 3, :], ebuf[:, 4], AX.X, ALU.max))
                step(lambda: V.tensor_tensor(oh[:, k], ebuf[:, 4], wide(rsm[:, 3, :]), ALU.is_equal))
                if k == 0:
                    step(lambda: V.scalar_tensor_tensor(out=ebuf[:, 5].rearrange("p j e -> p (j e)"),
                                                in0=oh[:, 0].rearrange("p j e -> p (j e)"), scalar=-2.0,
                                                in1=ebuf[:, 2].rearrange("p j e -> p (j e)"), op0=ALU.mult, op1=ALU.add))
                    probs = ebuf[:, 5]
            step(lambda: V.tensor_tensor(ebuf[:, 7], oh[:, 0], oh[:, 1], ALU.add))
            step(lambda: V.tensor_copy(macc[:, 0, :], macc[:, GB, :]))
            for j in range(GB):
                step(lambda: V.tensor_tensor(macc[:, j + 1, :], macc[:, j, :], ebuf[:, 7, j, :], ALU.add))
            assert count == MASK_STEP, count
            if lo == MASK_STEP + 1:
                dve.wait_ge(rt("pos"), i + 1)
            pos = PS[:, 7, 0:GB * E].rearrange("p (j e) -> p j e", j=GB)
            step(lambda: V.tensor_scalar(ebuf[:, 8], pos, float(CAP), None, ALU.is_lt))
            step(lambda: V.tensor_tensor(ebuf[:, 9], pos, base[:].unsqueeze(1).to_broadcast([P, GB, E]), ALU.add))
            for k in range(2):
                step(lambda: V.tensor_tensor(sel[:, k], oh[:, k], ebuf[:, 8], ALU.mult))
            step(lambda: V.tensor_reduce(keep[:], sel[:], AX.X, ALU.add))
            for k in range(2):
                step(lambda: V.tensor_tensor(sel[:, k], oh[:, k], ebuf[:, 9], ALU.mult))
            step(lambda: V.tensor_reduce(slot[:], sel[:], AX.X, ALU.add))
            r = rsm[:, 4:6, :]
            step(lambda: V.tensor_scalar(r, keep[:], -DROPPED, DROPPED, ALU.mult, ALU.add))
            step(lambda: V.tensor_tensor(sidx[:].rearrange("p j k -> p k j"), r, slot[:], ALU.add))
            step(lambda: V.tensor_tensor(gidx[:, bass.ds(GB * i, GB), :].rearrange("p j k -> p k j"), slot[:], keep[:], ALU.mult))
            step(lambda: V.tensor_tensor(rsm[:, 6:8, :], gates[:], keep[:], ALU.mult))
            step(lambda: V.tensor_scalar(gw[:, bass.ds(GB * i, GB), :].rearrange("p j k -> p k j"), rsm[:, 6:8, :], tg[:, 2:3],
                                 None, ALU.mult))
            assert count == ROUTE_STEPS, count

        def rope_dve(dve, i, p):
            V, z = nc.vector, p % 2
            dve.wait_ge(qsem("q"), NP * i + p + 1)
            if p >= 2:
                dve.wait_ge(qsem("add"), 3 * NP * i + 3 * (p - 1))
            q = PS[:, 3 * z:3 * z + 3, :].rearrange("p t (j s) -> p t j s", j=GB)
            c_ = qc[:, z].rearrange("p t (j s) -> p t j s", j=GB)
            s_ = qs[:, z].rearrange("p t (j s) -> p t j s", j=GB)
            V.tensor_tensor(c_, q, cosq[:].unsqueeze(2).to_broadcast([P, 3, GB, S]), ALU.mult).then_inc(qsem("cos"), 1)
            V.tensor_tensor(s_[:, 0:2], q[:, 0:2], sinq[:, 0:2].unsqueeze(2).to_broadcast([P, 2, GB, S]), ALU.mult).then_inc(qsem("cos"), 1)
            for a in range(2):
                src, dst = slice(64 * a, 64 * a + 64), slice(64 - 64 * a, P - 64 * a)
                V.tensor_tensor(s_[dst, 2], q[src, 2], sinq[src, 2, :].unsqueeze(1).to_broadcast([64, GB, S]),
                                ALU.mult).then_inc(qsem("cos"), 1)

        def low_dve(dve, s, layer, i, p, bank):
            dve.wait_ge(s("high"), 3 * NP * i + 3 * p + 1)
            for a in range(2):
                own = slice(64 * a, 64 * a + 64)
                nc.vector.tensor_tensor(tS[64:P, 2 * p + a, :], PS[own, bank, :], tTr[own, p, :].bitcast(F32),
                                        ALU.subtract).then_inc(s("low"), 1)

        def ffn_norm_dve(dve, i, part_):
            if part_ == 0:
                stats_dve(dve, 1, i)
            else:
                dve.wait_ge(rt("sent"), i + 1)
                normed_dve(dve, 1, i)

        def layer0_dve(dve, i, first, last):
            for p in range(NP):
                rope_dve(dve, i, p)
                if p >= 2:
                    low_dve(dve, qsem, 0, i, p - 2, t_bank(p - 2))
                if not first:
                    if p < 2:
                        ffn_norm_dve(dve, i - 1, p)
                    if p == 6:
                        choose_dve(dve, i - 1, 1, 1)

            def beside(k):
                if 1 <= k < 3:
                    low_dve(dve, qsem, 0, i, NP - 3 + k, t_bank(NP - 3 + k))
                if not first and k < len(ROUTE_AT) and ROUTE_AT[k]:
                    choose_dve(dve, i - 1, *ROUTE_AT[k])
                if first and k == 3:
                    dve.wait_ge(ld("x"), 16)
                if not last and 3 <= k < 5:
                    stats_dve(dve, 0, i + 1, (2 * k - 6, 2 * k - 5))
                if not last and 8 <= k < 12:
                    normed_dve(dve, 0, i + 1, (k - 8,))

            attend_dve(dve, 0, i, beside)

        def weights_split_dve(dve, e, i, z):
            dve.wait_ge(moe(f"weights{z}"), 32 * i + 32)
            nc.vector.tensor_copy(w1s[:, z, 0], w1[:, z]).then_inc(moe("w_high"), 1)
            dve.wait_ge(moe("w_high"), e + 1)
            nc.vector.tensor_tensor(w1s[:, z, 1], w1[:, z], w1s[:, z, 0].bitcast(F32), ALU.subtract).then_inc(moe("w_split"), 1)

        def rows_rest_dve(dve, e, z):
            for t in range(CT - 1):
                dve.wait_ge(moe("dT"), CT * e + t + 1)
                high, low = (dTs[:, z, m, :, t * P:(t + 1) * P] for m in range(2))
                nc.vector.tensor_tensor(low, PS[:, t % 2, 0:D].rearrange("p (k m) -> p k m", k=DK), high.bitcast(F32),
                                        ALU.subtract).then_inc(moe("low"), 1)

        def expert_out_dve(dve, e, z):
            dve.wait_ge(moe("eo_free"), e + 1)
            for t in range(CT):
                dve.wait_ge(moe("y"), CT * e + 2 * CT + t + 1)
                nc.vector.tensor_copy(eo[:, t, :], PS[:, 6 + (z * CT + t) % 2, 0:D]).then_inc(moe("y_out"), 1)

        def combine_dve(dve, i, j, choices=(0, 1)):
            dve.wait_ge(cb(f"gathered{j}"), 32 * i + 32)
            for k in choices:
                b = GB * i + j
                if k == 1:
                    dve.wait_ge(cb("added"), 2 * b + 2)
                nc.vector.scalar_tensor_tensor(out=batch(b), in0=grow[:, j, k, :], scalar=gw[:, bass.ds(b, 1), k], in1=batch(b),
                                               op0=ALU.mult, op1=ALU.add).then_inc(cb("added"), 1)

        def layer1_dve(dve, i, last):
            V = nc.vector

            def beside(k):
                if not last and 2 <= k < 10:
                    combine_dve(dve, i + 1, (k - 2) // 2, ((k - 2) % 2,))
                if not last and 3 <= k < 11 and k % 2:
                    stats_dve(dve, 2, i + 1, ((k - 3) // 2,))
                if not last and 12 <= k < 16:
                    normed_dve(dve, 2, i + 1, (k - 12,))

                if not last and NU + 2 <= k < NU + 4:
                    low_dve(dve, q1sem, 1, i + 1, k - NU - 2, q1_bank(k - NU - 2))

            attend_dve(dve, 1, i, beside)
            stats_dve(dve, 3, i)
            if not last:
                for p in range(2, 3):
                    low_dve(dve, q1sem, 1, i + 1, p, q1_bank(p))
            normed_dve(dve, 3, i)
            if not last:
                for p in range(3, NP):
                    low_dve(dve, q1sem, 1, i + 1, p, q1_bank(p))
            dve.wait_ge(ff("logits"), GB * i + GB)
            gate_dve()
            for j in range(GB):
                V.max(top8[:, j, :], PS[:, 2 + j, D:D + E]).then_inc(ff("rw"), 1)
            dve.wait_ge(ff("rw"), 8 * i + 4)
            V.tensor_tensor(rsm[:, 8, :], top8[:, :, 1], top8[:, :, 0], ALU.subtract).then_inc(ff("step"), 1)
            dve.wait_ge(ff("exp"), i + 1)
            V.tensor_scalar(rsm[:, 10, :], rsm[:, 9, :], 1.0, None, ALU.add).then_inc(ff("step"), 1)
            dve.wait_ge(ff("step"), 3 * i + 2)
            V.reciprocal(rsm[:, 11, :], rsm[:, 10, :]).then_inc(ff("step"), 1)
            dve.wait_ge(ff("step"), 3 * i + 3)
            V.tensor_tensor(rsm[:, 12, :], rsm[:, 9, :], rsm[:, 11, :], ALU.mult).then_inc(ff("rw"), 1)
            dve.wait_ge(ff("rw"), 8 * i + 5)
            V.tensor_tensor(rsm[:, 13, :], rsm[:, 12, :], rsm[:, 11, :], ALU.add).then_inc(ff("rw"), 1)
            dve.wait_ge(ff("rw"), 8 * i + 6)
            V.tensor_scalar(rsm[:, 14, :], rsm[:, 13, :], tg[:, 3:4], None, ALU.mult).then_inc(ff("rw"), 2)
            dve.wait_ge(ff("rw"), 8 * i + 8)
            for j in range(GB):
                V.scalar_tensor_tensor(out=batch(GB * i + j), in0=PS[:, 2 + j, 0:D], scalar=rsm[:, 14, j:j + 1], in1=batch(GB * i + j),
                                       op0=ALU.mult, op1=ALU.add).then_inc(ff("added"), 1)
            for j in range(GB):
                dve.wait_ge(ff("y"), GB * i + j + 1)
                dve.wait_ge(ff("added"), 2 * GB * i + j + 1)
                V.tensor_tensor(batch(GB * i + j), PS[:, y_bank(j), 0:D], batch(GB * i + j), ALU.add).then_inc(ff("added"), 1)

        @block.vector
        def _(dve):
            V = nc.vector
            V.memset(kvgr[:].bitcast(F32), 0.0).then_inc(kvs("ones"), 1)
            V.memset(kvag[:], 1.0).then_inc(kvs("ones"), 1)
            V.memset(macc[:], 0.0).then_inc(rt("carry"), 1)
            dve.sem_inc(moe("y_out"), 2)
            dve.sem_inc(cb("added"), 1)
            dve.wait_ge(cs("ones"), 1)
            V.tensor_copy(ones_r[:], ones[:]).then_inc(cs("ones"), 1)
            dve.wait_ge(ld("x0"), 16)
            stats_dve(dve, 0, 0)
            normed_dve(dve, 0, 0)
            dve.wait_ge(ld("kv"), 32)
            V.tensor_tensor(kv_cos, kv_raw, kv_tab[:, 0, :].unsqueeze(1).to_broadcast([P, B, DC]), ALU.mult).then_inc(kvs("cos"), 1)
            for a in range(2):
                o, s_ = slice(32 * a, 32 * a + 32), slice(32 - 32 * a, 64 - 32 * a)
                V.tensor_tensor(kv_sin[:, :, o], kv_raw[:, :, s_], kv_tab[:, 1, o].unsqueeze(1).to_broadcast([P, B, 32]),
                                ALU.mult).then_inc(kvs("sin"), 1)
            dve.wait_ge(kvs("cos"), 1)
            dve.wait_ge(kvs("sin"), 2)
            V.tensor_tensor(kv_dup.rearrange("p b (a c) -> p b a c", a=2), kv_cos.unsqueeze(2).to_broadcast([P, B, 2, DC]),
                            kv_sin.unsqueeze(2).to_broadcast([P, B, 2, DC]), ALU.add).then_inc(kvs("rope"), 1)
            V.tensor_tensor(kv_r[:], kv_cos, kv_sin, ALU.add).then_inc(kvs("rope"), 1)
            dve.wait_ge(ld("tab"), 32)
            layer0_dve(dve, 0, True, False)
            dve.wait_ge(ld("x_rest"), 16)
            dve.wait_ge(cs("misc"), 6)
            dve.wait_ge(ld("zero"), 16 * (E * CAP // (GB * P)))
            with dve.Fori(1, NG - 1) as i:
                layer0_dve(dve, i, False, False)
            layer0_dve(dve, NG - 1, False, True)
            for part_ in range(2):
                ffn_norm_dve(dve, NG - 1, part_)
            for lo, hi in ((1, 1), (2, MASK_STEP), (MASK_STEP + 1, ROUTE_STEPS)):
                choose_dve(dve, NG - 1, lo, hi)
            weights_split_dve(dve, 0, 0, 0)
            rows_rest_dve(dve, 0, 0)
            with dve.Fori(0, E // 2 - 1) as i:
                for z in range(2):
                    rows_rest_dve(dve, 2 * i + z + 1, 1 - z)
                    weights_split_dve(dve, 2 * i + z + 1, i + z, 1 - z)
                    expert_out_dve(dve, 2 * i + z, z)
            rows_rest_dve(dve, E - 1, 1)
            weights_split_dve(dve, E - 1, E // 2 - 1, 1)
            for z in range(2):
                expert_out_dve(dve, E - 2 + z, z)
            for j in range(GB):
                combine_dve(dve, 0, j)
                stats_dve(dve, 2, 0, (j,))
            normed_dve(dve, 2, 0)
            for p in range(NP):
                low_dve(dve, q1sem, 1, 0, p, q1_bank(p))
            dve.wait_ge(ld("ffn"), 64)
            V.tensor_scalar(wf[:, 1], wf[:, 1], tg[:, 3:4], None, ALU.mult).then_inc(ff("w_down"), 1)
            with dve.Fori(0, NG - 1) as i:
                layer1_dve(dve, i, False)
            layer1_dve(dve, NG - 1, True)


def rope_tables(length, dim):
    inv = (np.float32(1.0) / np.float32(10000.0) ** (np.arange(0, dim, 2, dtype=np.float32) / np.float32(dim))).astype(np.float32)
    f = np.arange(length, dtype=np.float32)[:, None] * inv[None, :]
    return np.repeat(np.sin(f), 2, axis=-1), np.repeat(np.cos(f), 2, axis=-1)


def query_tables():
    sin, cos = rope_tables(S, DQ)
    r = np.arange(P)
    q = np.stack([np.where(r < LO, r, r - LO), np.where(r < LO, r, r - LO) + LO,
                  np.where(r < 64, P - LO + r, P + r - 64)], axis=1)
    partner = np.where(q >= LO, q - LO, q + LO)
    sign = np.where(q >= LO, -1.0, 1.0).astype(np.float32)
    return (np.ascontiguousarray(cos.T[q], np.float32),
            np.ascontiguousarray(sin.T[partner] * sign[:, :, None], np.float32))


def context_table():
    sin, cos = rope_tables(S, DC)
    sign = np.where(np.arange(DC) < DC // 2, -1.0, 1.0).astype(np.float32)
    return np.ascontiguousarray(np.stack([cos, sin * sign], axis=1), np.float32)


def pack_pairs(wq, cq, ckv, wo, wqr, wkr):
    by_pair = lambda a: a.reshape(NP, 2, KH, -1).transpose(2, 0, 1, 3).reshape(KH, NP, -1)
    qrT = wqr.transpose(2, 0, 1).reshape(64, NP, 2, 2, LO)
    qr = np.zeros((P, NP, 3, P), wqr.dtype)
    qr[0:64, :, 0:2, 0:LO] = qrT[:, :, 0]
    qr[64:P, :, 0:2, LO:P] = qrT[:, :, 1, :, 0:P - LO]
    qr[64:P, :, 2] = qrT[:, :, 1, :, P - LO:LO].reshape(64, NP, P)
    krT = wkr.transpose(2, 0, 1).reshape(64, NP, 2, DC)
    kr = np.zeros((P, NP, 2, DC), wkr.dtype)
    kr[0:64, :, 0] = krT[:, :, 0]
    kr[64:P, :, 1] = krT[:, :, 1]
    return np.concatenate([by_pair(wq), by_pair(cq), by_pair(ckv), by_pair(wo.T),
                           qr.reshape(P, NP, -1), kr.reshape(P, NP, -1)], axis=2)


def kernel(**inputs):
    import concourse.bacc as bacc
    from concourse.bass_utils import run_bass_kernel_spmd

    nc = bacc.Bacc("TRN2", target_bir_lowering=False, num_devices=1)
    arrays = {}

    def give(name, a):
        a = np.ascontiguousarray(a)
        arrays["in_" + name] = a
        return nc.dram_tensor("in_" + name, a.shape, mybir.dt.from_np(a.dtype), kind="ExternalInput").ap()

    def raw(name):
        return np.asarray(inputs[name])

    cosq, sinq = query_tables()
    io = {
        "x": give("x", raw("x")).rearrange("b s d -> s b d"),
        "ctx": give("ctx", raw("ctx_512")).rearrange("b l c -> l b c"),
        "g_xattn": give("g_xattn", raw("g_xattn").reshape(1, 2)).to_broadcast([P, 2]),
        "g_ffn": give("g_ffn", raw("g_ffn").reshape(1, 2)).to_broadcast([P, 2]),
        "cosq": give("cosq", cosq),
        "sinq": give("sinq", sinq),
        "kv_tab": give("kv_tab", context_table()),
        "wg0": give("wg0", raw("L0_ffn_Wg")).rearrange("(k p) e -> p k e", p=P),
        "w1": give("w1", raw("L0_ffn_w1")),
        "w2": give("w2", raw("L0_ffn_w2")),
        "wg1": give("wg1", raw("L1_ffn_W_gate").T).rearrange("(k p) e -> p k e", p=P),
        "w_up": give("w_up", raw("L1_ffn_W_up").T).rearrange("(k p) e -> p k e", p=P),
        "w_dn": give("w_dn", raw("L1_ffn_W_down").T).rearrange("(k p) e -> p k e", p=P),
        "w_ex": give("w_ex", raw("L1_ffn_W_expert")).rearrange("(k p) e -> p k e", p=P),
    }
    for n in LAYERS:
        io[n] = give(f"pairs{n}", pack_pairs(*(raw(f"L{n}_xattn_{w}") for w in ("Wq", "w_kc_q", "w_kc_kv", "Wo", "W_qr", "W_kr"))))
    out = nc.dram_tensor("out", (B, S, D), F32, kind="ExternalOutput").ap()
    io["out"] = out.rearrange("b s d -> s b d")
    build(nc, io)
    done = run_bass_kernel_spmd(nc, [arrays], core_ids=[0])
    return done.results[0]["out"]
```
